# Optimizing a Trainium2 kernel written in Bass

```python
import numpy as np
import jax
import jax.numpy as jnp

def _softmax(x, axis=-1):
    return jax.nn.softmax(x, axis=axis)

def _gelu(x):
    return jax.nn.gelu(x, approximate=True)

def _silu(x):
    return jax.nn.silu(x)

def _sigmoid(x):
    return jax.nn.sigmoid(x)

def _layernorm(x, axis=-1, eps=1e-05):
    m = jnp.mean(x, axis=axis, keepdims=True)
    v = jnp.var(x, axis=axis, keepdims=True)
    return (x - m) / jnp.sqrt(v + eps)

def _scatter_add(tgt, idx, src, axis=0):
    return tgt.at[idx].add(src)

def _segment_sum(src, seg, n):
    return jax.ops.segment_sum(src, seg, n)
kernel_name = 'mk_gps_d1_gnn_r8_44b1e4'

def setup_inputs(seed: int=0):
    np.random.seed(seed)
    _w = jnp.asarray

    def _rec_inputs():
        import jax
        import jax.numpy as jnp
        _gk = jax.random.key(seed)
        x = -0.0006008 + 1.001 * jax.random.normal(jax.random.fold_in(_gk, 1), (1250, 512), jnp.float32)
        src = jax.random.randint(jax.random.fold_in(_gk, 2), (40000,), 0, 1250, jnp.int32)
        dst = jax.random.randint(jax.random.fold_in(_gk, 3), (40000,), 0, 1250, jnp.int32)
        _o = jnp.argsort(dst, stable=True)
        src = src[_o]
        dst = dst[_o]
        edge_attr_20 = jax.random.uniform(jax.random.fold_in(_gk, 12), (40000, 20), jnp.float32, 0.0, 0.999999)
        edge_attr_3 = -0.0005747 + 0.998114 * jax.random.normal(jax.random.fold_in(_gk, 13), (40000, 3), jnp.float32)
        edge_weight = jax.random.uniform(jax.random.fold_in(_gk, 14), (40000,), jnp.float32, 0.0, 0.999973)
        return (x, src, dst, edge_attr_20, edge_attr_3, edge_weight)
    x, src, dst, edge_attr_20, edge_attr_3, edge_weight = _rec_inputs()

    def _L0_gnn_setup():
        import jax, jax.numpy as jnp
        import numpy as np
        N_ATOMS = 625
        N_EDGES = 6250
        C = 128
        F = 128
        N_RBF = 20
        LOG2 = float(np.log(2.0))
        Y0 = float(1.0 / np.sqrt(4.0 * np.pi))
        Y1_SCALE = float(np.sqrt(3.0 / (4.0 * np.pi)))

        def shifted_softplus(x):
            return jax.nn.softplus(x) - LOG2

        def _forward(x, idx_i, idx_j, f_ij, rcut_ij, r_ij, W_in2f_s, W_in2f_v, Wf1, bf1, Wf2, bf2, W1_s, W1_v, W2_s, W2_v):
            n = x.shape[0]
            e = r_ij.shape[0]
            xs = x[:, :C] @ (W_in2f_s / np.sqrt(C))
            xv = jnp.einsum('nci,cf->nfi', x[:, C:].reshape(n, C, 3), W_in2f_v) / np.sqrt(C)
            sj = xs[idx_j]
            vj = xv[idx_j]
            u = r_ij / jnp.linalg.norm(r_ij, axis=-1, keepdims=True)
            Yv = Y1_SCALE * u
            o0a = sj * Y0
            o0b = jnp.einsum('efi,ei->ef', vj, Yv) / np.sqrt(3.0)
            s2 = jnp.stack([o0a, o0b], axis=-1).reshape(e, 2 * F)
            ova = sj[:, :, None] * Yv[:, None, :]
            ovb = vj * Y0
            v2 = jnp.stack([ova, ovb], axis=2)
            w1 = jnp.cross(vj, Yv[:, None, :]) / np.sqrt(2.0)
            ax, ay, az = (vj[..., 0], vj[..., 1], vj[..., 2])
            bx, by, bz = (Yv[:, None, 0], Yv[:, None, 1], Yv[:, None, 2])
            t = jnp.stack([(ax * by + ay * bx) / np.sqrt(2.0), (ay * bz + az * by) / np.sqrt(2.0), (2.0 * az * bz - ax * bx - ay * by) / np.sqrt(6.0), (az * bx + ax * bz) / np.sqrt(2.0), (ax * bx - ay * by) / np.sqrt(2.0)], axis=-1)
            h = shifted_softplus(f_ij @ Wf1 + bf1)
            W = (h @ Wf2 + bf2) * rcut_ij[:, None]
            m_s = s2 * W[:, :2 * F]
            m_v = (v2.reshape(e, 2 * F, 3) * W[:, 2 * F:4 * F, None]).reshape(e, 6 * F)
            m_w = (w1 * W[:, 4 * F:5 * F, None]).reshape(e, 3 * F)
            m_t = (t * W[:, 5 * F:6 * F, None]).reshape(e, 5 * F)
            x_ij = jnp.concatenate([m_s, m_v, m_w, m_t], axis=1)
            agg = jax.ops.segment_sum(x_ij, idx_i, num_segments=n)
            S = agg[:, :2 * F] @ (W1_s / np.sqrt(2 * F))
            V = jnp.einsum('nmi,mc->nci', agg[:, 2 * F:8 * F].reshape(n, 2 * F, 3), W1_v) / np.sqrt(2 * F)
            S = shifted_softplus(S)
            S = S @ (W2_s / np.sqrt(C))
            V = jnp.einsum('nci,cd->ndi', V, W2_v) / np.sqrt(C)
            return jnp.concatenate([S, V.reshape(n, 3 * C)], axis=1)
        key = jax.random.key(seed)
        ks = jax.random.split(key, 16)
        f32 = jnp.float32
        x = jax.random.normal(ks[0], (N_ATOMS, 4 * C), f32)
        idx_i = jnp.sort(jax.random.randint(ks[1], (N_EDGES,), 0, N_ATOMS))
        idx_j = jax.random.randint(ks[2], (N_EDGES,), 0, N_ATOMS)
        f_ij = jax.random.uniform(ks[3], (N_EDGES, N_RBF), f32)
        rcut_ij = jax.random.uniform(ks[4], (N_EDGES,), f32)
        r_ij = jax.random.normal(ks[5], (N_EDGES, 3), f32)
        W_in2f_s = jax.random.normal(ks[6], (C, F), f32)
        W_in2f_v = jax.random.normal(ks[7], (C, F), f32)
        Wf1 = jax.random.normal(ks[8], (N_RBF, F), f32) / np.sqrt(N_RBF)
        bf1 = 0.1 * jax.random.normal(ks[9], (F,), f32)
        Wf2 = jax.random.normal(ks[10], (F, 6 * F), f32) / np.sqrt(F)
        bf2 = 0.1 * jax.random.normal(ks[11], (6 * F,), f32)
        W1_s = jax.random.normal(ks[12], (2 * F, C), f32)
        W1_v = jax.random.normal(ks[13], (2 * F, C), f32)
        W2_s = jax.random.normal(ks[14], (C, C), f32)
        W2_v = jax.random.normal(ks[15], (C, C), f32)
        return dict(x=x, idx_i=idx_i, idx_j=idx_j, f_ij=f_ij, rcut_ij=rcut_ij, r_ij=r_ij, W_in2f_s=W_in2f_s, W_in2f_v=W_in2f_v, Wf1=Wf1, bf1=bf1, Wf2=Wf2, bf2=bf2, W1_s=W1_s, W1_v=W1_v, W2_s=W2_s, W2_v=W2_v)
    _L0_gnn_all = _L0_gnn_setup()
    _L0_gnn_in = {k: v for k, v in _L0_gnn_all.items() if k in ('W_in2f_s', 'W_in2f_v', 'Wf1', 'bf1', 'Wf2', 'bf2', 'W1_s', 'W1_v', 'W2_s', 'W2_v')}
    del _L0_gnn_all

    def _L0_mix_setup():
        import jax, jax.numpy as jnp
        import numpy as np
        HEADS = 8
        DIM_HEAD = 64
        key = jax.random.key(seed)
        ks = jax.random.split(key, 6)
        dim = 512
        inner = HEADS * DIM_HEAD
        x = jax.random.normal(ks[0], (4, 512, dim), dtype=jnp.float32)
        s = 1.0 / np.sqrt(dim)
        Wq = jax.random.normal(ks[1], (dim, inner), dtype=jnp.float32) * s
        Wk = jax.random.normal(ks[2], (dim, inner), dtype=jnp.float32) * s
        Wv = jax.random.normal(ks[3], (dim, inner), dtype=jnp.float32) * s
        Wo = jax.random.normal(ks[4], (inner, dim), dtype=jnp.float32) * (1.0 / np.sqrt(inner))
        bo = jax.random.normal(ks[5], (dim,), dtype=jnp.float32) * 0.01
        return {'x': x, 'Wq': Wq, 'Wk': Wk, 'Wv': Wv, 'Wo': Wo, 'bo': bo}
    _L0_mix_all = _L0_mix_setup()
    _L0_mix_in = {k: v for k, v in _L0_mix_all.items() if k in ('Wq', 'Wk', 'Wv', 'Wo', 'bo')}
    del _L0_mix_all

    def _L0_ffn_setup():
        import jax, jax.numpy as jnp
        import numpy as np
        B, C, IN_LEN, OUT_LEN, E, TOP_K, N_I = (1, 1024, 512, 512, 8, 2, 16)
        key = jax.random.key(seed)
        ks = jax.random.split(key, 8)
        w = lambda k, shape, sc=0.02: jax.random.normal(k, shape, dtype=jnp.float32) * sc
        return {'x': jax.random.normal(ks[0], (B, C, IN_LEN), dtype=jnp.float32), 'Ins_tk': jax.random.normal(ks[1], (B, N_I, OUT_LEN), dtype=jnp.float32), 'gate_w': w(ks[2], (IN_LEN, E)), 'expert_w': w(ks[3], (E, IN_LEN, OUT_LEN)), 'expert_b': jnp.zeros((E, OUT_LEN), dtype=jnp.float32), 'gamma_w': w(ks[4], (E, OUT_LEN)), 'beta_w': w(ks[5], (E, OUT_LEN, OUT_LEN)), 'rmod_w': w(ks[6], (OUT_LEN, E))}
    _L0_ffn_all = _L0_ffn_setup()
    _L0_ffn_in = {k: v for k, v in _L0_ffn_all.items() if k in ('Ins_tk', 'gate_w', 'expert_w', 'expert_b', 'gamma_w', 'beta_w', 'rmod_w')}
    del _L0_ffn_all
    return {'x': x, 'src': src, 'dst': dst, 'edge_attr_20': edge_attr_20, 'edge_attr_3': edge_attr_3, 'edge_weight': edge_weight, 'L0_gnn_W_in2f_s': _L0_gnn_in['W_in2f_s'], 'L0_gnn_W_in2f_v': _L0_gnn_in['W_in2f_v'], 'L0_gnn_Wf1': _L0_gnn_in['Wf1'], 'L0_gnn_bf1': _L0_gnn_in['bf1'], 'L0_gnn_Wf2': _L0_gnn_in['Wf2'], 'L0_gnn_bf2': _L0_gnn_in['bf2'], 'L0_gnn_W1_s': _L0_gnn_in['W1_s'], 'L0_gnn_W1_v': _L0_gnn_in['W1_v'], 'L0_gnn_W2_s': _L0_gnn_in['W2_s'], 'L0_gnn_W2_v': _L0_gnn_in['W2_v'], 'L0_mix_Wq': _L0_mix_in['Wq'], 'L0_mix_Wk': _L0_mix_in['Wk'], 'L0_mix_Wv': _L0_mix_in['Wv'], 'L0_mix_Wo': _L0_mix_in['Wo'], 'L0_mix_bo': _L0_mix_in['bo'], 'L0_ffn_Ins_tk': _L0_ffn_in['Ins_tk'], 'L0_ffn_gate_w': _L0_ffn_in['gate_w'], 'L0_ffn_expert_w': _L0_ffn_in['expert_w'], 'L0_ffn_expert_b': _L0_ffn_in['expert_b'], 'L0_ffn_gamma_w': _L0_ffn_in['gamma_w'], 'L0_ffn_beta_w': _L0_ffn_in['beta_w'], 'L0_ffn_rmod_w': _L0_ffn_in['rmod_w']}

def reference(x, src, dst, edge_attr_20, edge_attr_3, edge_weight, L0_gnn_W_in2f_s, L0_gnn_W_in2f_v, L0_gnn_Wf1, L0_gnn_bf1, L0_gnn_Wf2, L0_gnn_bf2, L0_gnn_W1_s, L0_gnn_W1_v, L0_gnn_W2_s, L0_gnn_W2_v, L0_mix_Wq, L0_mix_Wk, L0_mix_Wv, L0_mix_Wo, L0_mix_bo, L0_ffn_Ins_tk, L0_ffn_gate_w, L0_ffn_expert_w, L0_ffn_expert_b, L0_ffn_gamma_w, L0_ffn_beta_w, L0_ffn_rmod_w):
    import jax
    import jax.numpy as jnp

    def _L0_gnn_ref(x, idx_i, idx_j, f_ij, rcut_ij, r_ij, W_in2f_s, W_in2f_v, Wf1, bf1, Wf2, bf2, W1_s, W1_v, W2_s, W2_v):
        import jax, jax.numpy as jnp
        import numpy as np
        N_ATOMS = 625
        N_EDGES = 6250
        C = 128
        F = 128
        N_RBF = 20
        LOG2 = float(np.log(2.0))
        Y0 = float(1.0 / np.sqrt(4.0 * np.pi))
        Y1_SCALE = float(np.sqrt(3.0 / (4.0 * np.pi)))

        def shifted_softplus(x):
            return jax.nn.softplus(x) - LOG2

        def _forward(x, idx_i, idx_j, f_ij, rcut_ij, r_ij, W_in2f_s, W_in2f_v, Wf1, bf1, Wf2, bf2, W1_s, W1_v, W2_s, W2_v):
            n = x.shape[0]
            e = r_ij.shape[0]
            xs = x[:, :C] @ (W_in2f_s / np.sqrt(C))
            xv = jnp.einsum('nci,cf->nfi', x[:, C:].reshape(n, C, 3), W_in2f_v) / np.sqrt(C)
            sj = xs[idx_j]
            vj = xv[idx_j]
            u = r_ij / jnp.linalg.norm(r_ij, axis=-1, keepdims=True)
            Yv = Y1_SCALE * u
            o0a = sj * Y0
            o0b = jnp.einsum('efi,ei->ef', vj, Yv) / np.sqrt(3.0)
            s2 = jnp.stack([o0a, o0b], axis=-1).reshape(e, 2 * F)
            ova = sj[:, :, None] * Yv[:, None, :]
            ovb = vj * Y0
            v2 = jnp.stack([ova, ovb], axis=2)
            w1 = jnp.cross(vj, Yv[:, None, :]) / np.sqrt(2.0)
            ax, ay, az = (vj[..., 0], vj[..., 1], vj[..., 2])
            bx, by, bz = (Yv[:, None, 0], Yv[:, None, 1], Yv[:, None, 2])
            t = jnp.stack([(ax * by + ay * bx) / np.sqrt(2.0), (ay * bz + az * by) / np.sqrt(2.0), (2.0 * az * bz - ax * bx - ay * by) / np.sqrt(6.0), (az * bx + ax * bz) / np.sqrt(2.0), (ax * bx - ay * by) / np.sqrt(2.0)], axis=-1)
            h = shifted_softplus(f_ij @ Wf1 + bf1)
            W = (h @ Wf2 + bf2) * rcut_ij[:, None]
            m_s = s2 * W[:, :2 * F]
            m_v = (v2.reshape(e, 2 * F, 3) * W[:, 2 * F:4 * F, None]).reshape(e, 6 * F)
            m_w = (w1 * W[:, 4 * F:5 * F, None]).reshape(e, 3 * F)
            m_t = (t * W[:, 5 * F:6 * F, None]).reshape(e, 5 * F)
            x_ij = jnp.concatenate([m_s, m_v, m_w, m_t], axis=1)
            agg = jax.ops.segment_sum(x_ij, idx_i, num_segments=n)
            S = agg[:, :2 * F] @ (W1_s / np.sqrt(2 * F))
            V = jnp.einsum('nmi,mc->nci', agg[:, 2 * F:8 * F].reshape(n, 2 * F, 3), W1_v) / np.sqrt(2 * F)
            S = shifted_softplus(S)
            S = S @ (W2_s / np.sqrt(C))
            V = jnp.einsum('nci,cd->ndi', V, W2_v) / np.sqrt(C)
            return jnp.concatenate([S, V.reshape(n, 3 * C)], axis=1)
        return _forward(x, idx_i, idx_j, f_ij, rcut_ij, r_ij, W_in2f_s, W_in2f_v, Wf1, bf1, Wf2, bf2, W1_s, W1_v, W2_s, W2_v)

    def _L0_mix_ref(x, Wq, Wk, Wv, Wo, bo):
        import jax, jax.numpy as jnp
        import numpy as np
        HEADS = 8
        DIM_HEAD = 64
        b, n, _ = x.shape
        h, d = (HEADS, DIM_HEAD)
        q = (x @ Wq).reshape(b, n, h, d).transpose(0, 2, 1, 3)
        k = (x @ Wk).reshape(b, n, h, d).transpose(0, 2, 1, 3)
        v = (x @ Wv).reshape(b, n, h, d).transpose(0, 2, 1, 3)
        q = jax.nn.softmax(q, axis=-1)
        k = jax.nn.softmax(k, axis=-1)
        context = jnp.einsum('bhnd,bhne->bhde', k, v)
        out = jnp.einsum('bhnd,bhde->bhne', q, context)
        out = out.transpose(0, 2, 1, 3).reshape(b, n, h * d)
        return out @ Wo + bo

    def _L0_ffn_ref(x, Ins_tk, gate_w, expert_w, expert_b, gamma_w, beta_w, rmod_w):
        import jax, jax.numpy as jnp
        import numpy as np
        B, C, IN_LEN, OUT_LEN, E, TOP_K, N_I = (1, 1024, 512, 512, 8, 2, 16)
        Bx, Cx, L = x.shape
        xf = x.reshape(-1, L)
        ins = Ins_tk[0]
        router_gamma = jnp.mean(ins @ rmod_w, axis=0)
        logits = xf @ gate_w + router_gamma
        probs = jax.nn.softmax(logits.astype(jnp.float32), axis=-1)
        rw, sel = jax.lax.top_k(probs, TOP_K)
        combine = jnp.sum(jax.nn.one_hot(sel, E, dtype=rw.dtype) * rw[..., None], axis=1)
        gam = jnp.mean(ins @ gamma_w.T, axis=0)
        bet = jnp.einsum('nh,ehd->ed', ins, beta_w) / N_I
        eo = jnp.einsum('nl,eld->end', xf, expert_w) + expert_b[:, None, :]
        mod = gam[:, None, None] * eo + bet[:, None, :]
        out = jnp.einsum('ne,end->nd', combine, mod)
        return out.reshape(Bx, Cx, OUT_LEN)
    xn = _layernorm(x, axis=-1)
    x = x + _L0_gnn_ref(xn, src, dst, edge_attr_20, edge_weight, edge_attr_3, L0_gnn_W_in2f_s, L0_gnn_W_in2f_v, L0_gnn_Wf1, L0_gnn_bf1, L0_gnn_Wf2, L0_gnn_bf2, L0_gnn_W1_s, L0_gnn_W1_v, L0_gnn_W2_s, L0_gnn_W2_v) + _L0_mix_ref(xn[None], L0_mix_Wq, L0_mix_Wk, L0_mix_Wv, L0_mix_Wo, L0_mix_bo)[0]
    x = x + _L0_ffn_ref(_layernorm(x, axis=-1)[None], L0_ffn_Ins_tk, L0_ffn_gate_w, L0_ffn_expert_w, L0_ffn_expert_b, L0_ffn_gamma_w, L0_ffn_beta_w, L0_ffn_rmod_w)[0]
    return x

_drawn_inputs = setup_inputs


def setup_inputs(seed=0):
    import zlib

    import numpy as np

    out = dict(_drawn_inputs(seed))
    spreads = {'L0_ffn_expert_b': (0.0, 0.8)}
    factors = {'L0_mix_bo': 6.336,
     'L0_ffn_expert_w': 3.934,
     'L0_ffn_gamma_w': 5.064,
     'L0_ffn_rmod_w': 4.401}
    for name, (base, spread) in spreads.items():
        noise = np.random.default_rng([zlib.crc32(name.encode()), seed]).standard_normal(out[name].shape)
        drawn = base * np.exp(spread * noise) if base else spread * noise
        out[name] = jnp.asarray(drawn.astype(out[name].dtype))
    for name, factor in factors.items():
        out[name] = (out[name] * factor).astype(out[name].dtype)
    return out
```

```python
from contextlib import ExitStack

import numpy as np

import concourse.bass as bass
from concourse import mybir

F32 = mybir.dt.float32
BF16 = mybir.dt.bfloat16
I32 = mybir.dt.int32
ALU = mybir.AluOpType
ACT = mybir.ActivationFunctionType
AX_X = mybir.AxisListType.X
ds = bass.ds

P = 128
GROUP = 256
TPG = GROUP // P
UNROLL = 4
EPS = 1e-5


def upto(i, per, j):
    return i * per + (j + 1)


def gps_layer(nc, x, src, dst, edge_attr_20, edge_attr_3, edge_weight, W_in2f_s, W_in2f_v, Wf1, bf1, Wf2, bf2,
              W1_s, W1_v, W2_s, W2_v, Wq, Wk, Wv, Wo, bo, Ins_tk, gate_w, expert_w, expert_b, gamma_w, beta_w,
              rmod_w, out):
    N, D = x.shape
    E, R = edge_attr_20.shape
    C = W_in2f_s.shape[0]
    KD = D // P
    NB = 10
    NT = N // NB
    HEADS, DH = 8, 64
    X8, OUT = expert_w.shape[0], expert_w.shape[2]
    NI = Ins_tk.shape[1]
    GROUPS = -(-(E + NB * (GROUP - 1)) // GROUP)
    GROUPS = -(-GROUPS // UNROLL) * UNROLL
    NCOL = GROUPS * TPG
    FULL = E // P
    REM = E - FULL * P
    RC1 = FULL + 1
    SPARE = NCOL - FULL
    REC = 4 * C + 8
    COLS = 2 * UNROLL
    FITER = NCOL // COLS
    MITER = GROUPS // UNROLL
    MSG = 8 * C
    Y0 = float(1.0 / np.sqrt(4.0 * np.pi))
    assert NB * NT == N and NT <= P and C == P and NCOL % COLS == 0 and REM % 32 == 0 and OUT == D

    rec_dram = nc.dram_tensor("edge_records", [NCOL * P, REC], F32, kind="Internal").ap()
    tab_dram = nc.dram_tensor("node_table", [N, 4 * C], F32, kind="Internal").ap()

    ctx = ExitStack()
    with ctx:
        def sb(name, shape, dt=F32):
            return ctx.enter_context(nc.sbuf_tensor(name, shape, dt))

        def sem(name):
            return ctx.enter_context(nc.semaphore(name))

        def sems(name, n):
            return [sem(f"{name}{k}") for k in range(n)]

        PS = ctx.enter_context(nc.psum_tensor("PS", [P, 8, 512], F32))

        X = sb("X", [P, NB, D])
        ident = sb("ident", [P, P])
        iota_f = sb("iota_f", [P, P])
        ones = sb("ones", [P, 320])
        ltri = sb("ltri", [P, P])
        w1s = sb("w1s", [P, 2, C])
        w1v = sb("w1v", [P, 2, C])
        w2s = sb("w2s", [P, C])
        w2v = sb("w2v", [P, C])
        gate = sb("gate", [P, KD, X8])
        small = sb("small", [P, 640])
        gam8 = small[:, 0:8]
        rgam = small[:, 8:16]
        mean = small[:, 16:26]
        var_eps = small[:, 26:36]
        rstd = small[:, 36:46]
        stats = small[:, 48:108].rearrange("p (t s) -> p t s", s=6)
        aggr = small[:, 108:128].rearrange("p (t s) -> p t s", s=2)
        mxq, mxk = small[:, 128:136], small[:, 136:144]
        smq, smk = small[:, 144:152], small[:, 152:160]
        cnt = small[:, 160:170]
        tot = small[:, 170:180]
        pref = small[:, 180:190]
        ngf = small[:, 190:200]
        endg = small[:, 200:210]
        base = small[:, 210:220]
        off = small[:, 220:230]
        cumt = small[:, 230:240]
        cpad = small[:, 240:250]
        rq, rk = small[:, 250:258], small[:, 258:266]
        mi = small[:, 266:270]
        tmp8 = small[:, 270:278]
        gcol = small[:, 278:279]
        bb_g = small[:, 280:300]
        prob = small[:, 300:308]
        comb = small[:, 308:316]
        cg = small[:, 316:324]
        rank = small[:, 324:332]
        st1 = small[:, 332:340]
        comb_t = small[:, 340:468]
        tie = small[:, 468:532].rearrange("p (a b) -> p a b", b=X8)
        cmp_a = small[:, 532:596].rearrange("p (a b) -> p a b", b=X8)
        ints = sb("ints", [P, 16], I32)
        goff = sb("goff", [P, GROUPS], I32)
        cmp_b = sb("cmp_b", [P, X8, X8])
        half = sb("half", [P, 1])
        bb = sb("bb", [P, D])

        we_words = X8 * KD * OUT
        R2 = sb("R2", [P, we_words])
        at = [0]

        def r2(words):
            a = at[0]
            at[0] += words
            assert at[0] <= we_words
            return R2[:, a:a + words]

        Fe = r2(NCOL * R).rearrange("p (c r) -> p c r", r=R)
        meta = r2(NCOL * 8).rearrange("p (c m) -> p c m", m=8)
        rcut = r2(NCOL)
        posi = r2(NCOL).bitcast(I32)
        srci = r2(RC1).bitcast(I32)
        srcf = r2(RC1)
        bkt = r2(RC1)
        rnk = r2(RC1)
        tA, tB = r2(RC1), r2(RC1)
        kd = r2(SPARE)
        pd = r2(SPARE)
        we = R2[:, :].rearrange("p (e k n) -> p e k n", e=X8, k=KD)

        r1_words = 27400
        R1 = sb("R1", [P, r1_words])

        class Carve:

            def __init__(self, start=0):
                self.at = start

            def __call__(self, words):
                a = self.at
                self.at += words
                assert self.at <= r1_words, self.at
                return R1[:, a:a + words]

        c1 = Carve()
        wqkv = c1(3 * KD * D).rearrange("p (w k n) -> p w k n", w=3, k=KD)
        KN = c1(NB * D).rearrange("p (t n) -> p t n", t=NB)
        VN = c1(NB * D).rearrange("p (t n) -> p t n", t=NB)
        QT = c1(KD * NB * NT).rearrange("p (t k n) -> p t k n", t=NB, k=KD)
        wo = c1(KD * D).rearrange("p (k n) -> p k n", k=KD)
        XN = c1(2 * D).rearrange("p (s n) -> p s n", s=2)
        XT = c1(2 * KD * NT).rearrange("p (s k n) -> p s k n", s=2, k=KD)
        TAB = c1(2 * D).rearrange("p (s n) -> p s n", s=2)
        QW = c1(D)
        wsv = c1(2 * C).rearrange("p (w n) -> p w n", w=2)
        MO = wqkv[:, 0, :, :]
        ctxT = wqkv[:, 1, 0, :].rearrange("p (k n) -> p k n", k=KD)
        bo_b = wqkv[:, 2, 0, :]
        bslot = [VN[:, 0:4, :], VN[:, 4:8, :]]
        ins_sb = QW[0:NI, :]
        z_mi = VN[:, 8:9, 0:KD * X8 * X8].rearrange("p o (k e f) -> p (o k) e f", k=KD, e=X8)
        gamT = wsv[:, 0, 0:KD * X8].rearrange("p (k e) -> p k e", k=KD)
        rmod = wsv[:, 0, 32:32 + KD * X8].rearrange("p (k e) -> p k e", k=KD)
        gam_row = XN[0:X8, 0, :]
        mi_bc = KN[:, 0, :].rearrange("p (k n) -> p k n", k=KD)
        be_row = XN[0:X8, 1, :]

        c2 = Carve(3 * KD * D)
        ST = c2(COLS * REC).rearrange("p (s r) -> p s r", r=REC)
        fT = c2(2 * 512).rearrange("p (h n) -> p h n", h=2)
        tz = c2(2 * 512).rearrange("p (h n) -> p h n", h=2)
        hT = c2(2 * 512).rearrange("p (h n) -> p h n", h=2)
        Fst = c2(2 * UNROLL * R).rearrange("p (h c r) -> p h c r", h=2, r=R)
        rcst = c2(2 * UNROLL).rearrange("p (h c) -> p h c", h=2)
        idxst = c2(COLS).bitcast(I32)
        assert c2.at <= 3 * KD * D + 2 * NB * D

        c3 = Carve()
        acc = c3(NB * MSG)
        RB = c3(UNROLL * TPG * REC).rearrange("p (s t r) -> p s t r", s=UNROLL, t=TPG)
        GB = c3(UNROLL * TPG * 4 * C).rearrange("p (s t n) -> p s t n", s=UNROLL, t=TPG)
        MB = c3(2 * TPG * 9 * C).rearrange("p (s t k n) -> p s t k n", s=2, t=TPG, k=9)
        OH = c3(2 * TPG * P).rearrange("p (s t n) -> p s t n", s=2, t=TPG)
        DT = c3(TPG * 3 * C).rearrange("p (t k n) -> p t k n", t=TPG, k=3)

        c4 = Carve(NB * MSG)
        AT = c4(8 * P).rearrange("p (k n) -> p k n", k=8)
        S1 = c4(4 * P).rearrange("p (k n) -> p k n", k=4)
        sz = c4(P)
        XF = c4(2 * D).rearrange("p (s n) -> p s n", s=2)
        XFT = c4(2 * KD * P).rearrange("p (s k n) -> p s k n", s=2, k=KD)

        wf1 = sb("wf1", [R + 1, P])
        wf2 = sb("wf2", [P, 4, C])
        b2s = sb("b2s", [3, 4, C], BF16)
        ones3 = sb("ones3", [3, P], BF16)
        rraw = KN[:, 0:2, :].rearrange("p t n -> p (t n)")[:, 0:RC1 * 3].rearrange("p (c i) -> p c i", i=3)
        ssq = KN[:, 2, 0:RC1]
        inv = KN[:, 3, 0:RC1]
        rtmp = KN[:, 4:6, :].rearrange("p t n -> p (t n)")[:, 0:RC1 * 3].rearrange("p (c i) -> p c i", i=3)
        dsti = KN[:, 6, 0:RC1].bitcast(I32)
        wf2raw = KN[:, 7, :]
        b2raw = KN[0:3, 8, :]
        b2rem = KN[0:3, 9, :]
        b2p = [VN[0:3, k, 0:256].bitcast(BF16) for k in range(3)]

        consts = sem("constants_ready")
        pool_step = sem("pool_step")
        dve_step = sem("dve_step")
        act_step = sem("act_step")
        x_in = sems("x_in", 2)
        wsv_in, wqkv_in, wo_in = sem("wsv_in"), sems("wqkv_in", 3), sem("wo_in")
        bo_in, ffn_small_in, w12_in = sem("bo_in"), sem("ffn_small_in"), sem("w12_in")
        edge_in, f_in, rcut_in, wf_in, b2_in = sem("edge_in"), sem("f_in"), sem("rcut_in"), sem("wf_in"), sem("b2_in")
        edge_zero = sem("edge_buffers_filled")
        b2_parts = sem("b2_parts_made")
        b2_placed = sem("b2_placed")
        var_ready, std_ready, nrm_sq, nrm_root = sem("var_ready"), sem("std_ready"), sem("norm_sq"), sem("norm_root")
        xn_ready = sem("xn_ready")
        xT_psum, xT_ready = sem("xT_psum"), sem("xT_ready")
        tab_psum, tab_ready, tab_out = sem("table_psum"), sem("table_ready"), sems("table_out", 2)
        q_psum, k_psum, v_psum = sem("q_psum"), sem("k_psum"), sem("v_psum")
        q_shift, k_shift, q_exp, k_exp = sem("q_shifted"), sem("k_shifted"), sem("q_exp"), sem("k_exp")
        q_norm, k_norm, v_ready = sem("q_normal"), sem("k_normal"), sem("v_ready")
        qT_psum, qT_ready = sem("qT_psum"), sem("qT_ready")
        counts_ready, counts_psum = sem("counts_ready"), sem("counts_psum")
        pos_ready = sem("positions_ready")
        ctx_psum, ctx_zero, ctx_ready = sem("context_psum"), sem("context_zeroed"), sem("context_ready")
        mo_psum, mo_ready = sem("context_wo_psum"), sem("context_wo_ready")
        y_psum, mix_added = sem("mix_psum"), sem("mix_added")
        mi_psum, mi_ready, z_ready = sem("ins_mean_psum"), sem("ins_mean_ready"), sem("ins_mean_spread")
        gamT_psum, gamT_ready = sem("gammaT_psum"), sem("gammaT_ready")
        gam_psum = sem("gamma_psum")
        beta_in, beta_used = sems("beta_in", 2), sem("beta_used")
        router_ready = sem("router_ready")
        staged = sem("edge_columns_staged")
        f_used = sem("f_transposed")
        fT_ready, z_psum, z_abs, l_ready, h_ready = (sem("fT_ready"), sem("z_psum"), sem("z_abs"), sem("log_ready"),
                                                     sem("h_ready"))
        w_psum, w_even, w_odd = sem("filter_psum"), sem("filter_even_ready"), sem("filter_odd_ready")
        e_ready = sem("exp_ready")
        scattered = sems("scattered", COLS)
        scatter_turn, gather_turn = sem("scatter_turn"), sem("gather_turn")
        rec_in = sems("record_in", UNROLL)
        gathered = [sems(f"gathered{s}_", TPG) for s in range(UNROLL)]
        acc_zero = sem("sums_zeroed")
        dot1, dot2, dot3 = sem("dot_x"), sem("dot_xy"), sem("dot_xyz")
        onehot, ac_ready, b_ready, d_ready, c_ready = (sem("onehot_ready"), sem("message_ac"), sem("message_b"),
                                                       sem("message_d"), sem("message_c"))
        summed, flushed = sem("group_summed"), sem("group_flushed")
        we_in = sem("expert_w_in")
        aT_psum, aT_ready = sem("sumsT_psum"), sem("sumsT_ready")
        sv_psum, s_abs, s_ln, s_ready, v1_ready = (sem("mixed_psum"), sem("s_abs"), sem("s_log"), sem("s_ready"),
                                                   sem("v_mixed_ready"))
        g_psum, x1_ready = sem("gnn_psum"), sem("x1_ready")
        var2_ready, std2_ready = sem("var2_ready"), sem("std2_ready")
        xf_ready, xfT_psum, xfT_ready = sem("xf_ready"), sem("xfT_psum"), sem("xfT_ready")
        logit_psum, shift_ready, prob_exp = sem("logit_psum"), sem("logits_shifted"), sem("logits_exp")
        comb_ready, combT_psum, combT_ready, bias_psum = (sem("combine_ready"), sem("combineT_psum"),
                                                          sem("combineT_ready"), sem("expert_bias_psum"))
        eo_psum, eo_used = sem("expert_psum"), sem("expert_used")
        o_ready, o_out = sem("output_ready"), sem("output_stored")

        block = ctx.enter_context(nc.Block())


        @block.sync
        def _(sp):
            xv = x.rearrange("(t p) d -> p t d", p=NT)
            sp.dma_start(X[0:NT, 0:2, :], xv[:, 0:2, :]).then_inc(x_in[0], 16)
            sp.dma_start(X[0:NT, 2:NB, :], xv[:, 2:NB, :]).then_inc(x_in[1], 16)
            sp.dma_start(wsv[:, 0, :], W_in2f_s).then_inc(wsv_in, 16)
            sp.dma_start(wsv[:, 1, :], W_in2f_v).then_inc(wsv_in, 16)
            for w, (wt, s) in enumerate(zip((Wq, Wk, Wv), wqkv_in)):
                sp.dma_start(wqkv[:, w, 0, :], wt[0:C, :]).then_inc(s, 16)
                sp.dma_start(wqkv[:, w, 1:KD, :], wt[C:D, :].rearrange("(c i) n -> c i n", i=3)).then_inc(s, 16)
            sp.dma_start(wo, Wo.rearrange("(k p) n -> p k n", p=P)).then_inc(wo_in, 16)
            sp.dma_start(w1s[:, :, :], W1_s.rearrange("(f a) c -> f a c", a=2)).then_inc(w12_in, 16)
            sp.dma_start(w1v[:, :, :], W1_v.rearrange("(f a) c -> f a c", a=2)).then_inc(w12_in, 16)
            sp.dma_start(w2s[:, :], W2_s).then_inc(w12_in, 16)
            sp.dma_start(w2v[:, :], W2_v).then_inc(w12_in, 16)
            sp.dma_start(gate[:, :, :], gate_w.rearrange("(k p) e -> p k e", p=P)).then_inc(w12_in, 16)
            for t in range(NB):
                sp.wait_ge(tab_ready, t + 1)
                sp.dma_start(tab_dram[t * NT:(t + 1) * NT, :], TAB[0:NT, t % 2, :]).then_inc(tab_out[t % 2], 16)
            sp.wait_ge(ctx_psum, 1)
            sp.wait_ge(tab_psum, NB)
            sp.wait_ge(qT_psum, NB)
            sp.wait_ge(xT_psum, NB)
            sp.dma_start(bo_b[0:NT, :], bo.rearrange("(o n) -> o n", o=1).to_broadcast([NT, D])).then_inc(bo_in, 16)
            sp.dma_start(ins_sb, Ins_tk[0]).then_inc(ffn_small_in, 16)
            sp.dma_start(gam_row, gamma_w).then_inc(ffn_small_in, 16)
            sp.dma_start(be_row, expert_b).then_inc(ffn_small_in, 16)
            sp.dma_start(rmod, rmod_w.rearrange("(k p) e -> p k e", p=P)).then_inc(ffn_small_in, 16)
            for e in range(X8):
                if e >= 2:
                    sp.wait_ge(beta_used, e - 1)
                sp.dma_start(bslot[e % 2], beta_w[e].rearrange("(k p) n -> p k n", p=P)).then_inc(beta_in[e % 2], 16)

            for j in range(COLS):
                sp.wait_ge(scattered[j], 16 * FITER)
            sp.wait_ge(router_ready, 1)
            sp.wait_ge(mix_added, NB)
            rv = rec_dram.rearrange("(g p t) r -> g p (t r)", p=P, t=TPG)

            def load(i, first):
                for s in range(UNROLL):
                    if not first:
                        sp.wait_ge(b_ready, upto(i - 1, UNROLL * TPG, s * TPG + 1))
                        sp.wait_ge(d_ready, upto(i - 1, UNROLL * TPG, s * TPG + 1))
                        sp.wait_ge(c_ready, upto(i - 1, UNROLL * TPG, s * TPG + 1))
                        sp.wait_ge(onehot, upto(i - 1, UNROLL * TPG, s * TPG + 1))
                    g = i * UNROLL + s
                    r = rv[g] if first else rv[ds(g, 1)].rearrange("o p r -> p (o r)")
                    sp.dma_start(RB[:, s, :, :].rearrange("p t r -> p (t r)"), r).then_inc(rec_in[s], 16)

            load(0, True)
            with sp.Fori(1, MITER) as i:
                load(i, False)
            for t in range(NB):
                sp.wait_ge(o_ready, t + 1)
                sp.dma_start(out[t * NT:(t + 1) * NT, :], X[0:NT, t, :]).then_inc(o_out, 16)
            sp.wait_ge(o_out, 16 * NB)
            for s in range(2):
                sp.wait_ge(tab_out[s], 16 * (NB // 2))

        @block.gpsimd
        def _(pool):
            steps = [0]

            def step(ins):
                steps[0] += 1
                ins.then_inc(pool_step, 1)
                pool.wait_ge(pool_step, steps[0])

            g = nc.gpsimd
            step(g.memset(ones[:, :], 1.0))
            step(g.memset(ident[:, :], 0.0))
            step(g.affine_select(out=ident[:, :], in_=ident[:, :], compare_op=ALU.not_equal, fill=1.0, base=0,
                                 pattern=[[-1, P]], channel_multiplier=1))
            step(g.affine_select(out=ltri[:, :], in_=ones[:, 0:P], compare_op=ALU.is_gt, fill=0.0, base=0,
                                 pattern=[[1, P]], channel_multiplier=-1))
            g.iota(iota_f[:, :], pattern=[[1, P]], base=0, channel_multiplier=0,
                   allow_small_or_imprecise_dtypes=True).then_inc(consts, 1)
            g.memset(meta[:, :, :], 0.0)
            g.memset(srci[:, :], 0)
            g.memset(dsti[:, :], 0)
            g.memset(rraw[:, :, :], 1.0)
            g.memset(rcut[:, :], 0.0)
            g.memset(Fe[:, FULL:NCOL, :], 0.0).then_inc(edge_zero, 1)
            g.memset(ones3[:, :], 1.0)
            g.affine_select(out=tie, in_=ones[:, 0:X8 * X8].rearrange("p (a b) -> p a b", b=X8), compare_op=ALU.is_gt,
                            fill=0.0, base=0, pattern=[[1, X8], [-1, X8]], channel_multiplier=0)
            g.iota(kd[:, :], pattern=[[P, SPARE]], base=-REM, channel_multiplier=1,
                   allow_small_or_imprecise_dtypes=True)
            g.iota(goff[:, :], pattern=[[1, GROUPS]], base=0, channel_multiplier=0).then_inc(consts, 1)
            pool.wait_ge(edge_zero, 1)
            for dest, values in ((srci, src), (dsti, dst)):
                v = values.rearrange("(n o) -> n o", o=1)
                g.dma_start(dest[:, 0:FULL], values[0:P * FULL].rearrange("(p c) -> p c", p=P)).then_inc(edge_in, 16)
                g.dma_start(dest[0:REM, FULL:RC1], v[P * FULL:E, :]).then_inc(edge_in, 16)
            g.dma_start(rraw[:, 0:FULL, :], edge_attr_3[0:P * FULL, :].rearrange("(p c) i -> p c i", p=P))\
                .then_inc(edge_in, 16)
            g.dma_start(rraw[0:REM, FULL, :], edge_attr_3[P * FULL:E, :]).then_inc(edge_in, 16)
            g.dma_start(rcut[:, 0:FULL], edge_weight[0:P * FULL].rearrange("(p c) -> p c", p=P)).then_inc(rcut_in, 16)
            g.dma_start(rcut[0:REM, FULL:RC1], edge_weight.rearrange("(n o) -> n o", o=1)[P * FULL:E, :])\
                .then_inc(rcut_in, 16)
            g.dma_start(wf2raw, Wf2[:, 0:4 * C]).then_inc(wf_in, 16)
            g.dma_start(b2raw, bf2.rearrange("(o n) -> o n", o=1)[:, 0:4 * C].to_broadcast([3, 4 * C]))\
                .then_inc(b2_in, 16)
            g.dma_start(wf1[0:R, :], Wf1).then_inc(wf_in, 16)
            g.dma_start(wf1[R:R + 1, :], bf1.rearrange("(o n) -> o n", o=1)).then_inc(wf_in, 16)
            g.dma_start(Fe[:, 0:FULL, :], edge_attr_20[0:P * FULL, :].rearrange("(p c) r -> p c r", p=P))\
                .then_inc(f_in, 16)
            g.dma_start(Fe[0:REM, FULL, :], edge_attr_20[P * FULL:E, :]).then_inc(f_in, 16)
            pool.wait_ge(b2_parts, 1)
            for k in range(3):
                g.dma_start(b2s[k:k + 1, :, :].rearrange("p k n -> p (k n)"), b2p[k][k:k + 1, :])\
                    .then_inc(b2_placed, 16)

            def scatter(i):
                for j in range(COLS):
                    pool.wait_ge(w_odd if j % 2 else w_even, upto(i, COLS // 2, j // 2))
                    pool.wait_ge(staged, upto(i, 2, j // UNROLL))
                    pool.sem_inc(scatter_turn, 1)
                    g.indirect_dma_start(out=rec_dram, out_offset=bass.IndirectOffsetOnAxis(ap=idxst[:, j:j + 1], axis=0),
                                         in_=ST[:, j, :], in_offset=None).then_inc(scattered[j], 16)

            scatter(0)
            with pool.Fori(1, FITER) as i:
                scatter(i)
            for j in range(COLS):
                pool.wait_ge(scattered[j], 16 * FITER)
            pool.wait_ge(mix_added, NB)
            pool.wait_ge(router_ready, 1)
            pool.wait_ge(w_psum, FITER * COLS)
            g.memset(acc[:, :], 0.0).then_inc(acc_zero, 1)
            for s in range(2):
                pool.wait_ge(tab_out[s], 16 * (NB // 2))
            g.dma_start(we, expert_w.rearrange("e (k p) n -> p e k n", p=P)).then_inc(we_in, 16)

            def gather(i, first):
                for s in range(UNROLL):
                    pool.wait_ge(rec_in[s], 16 * (i + 1) if first else i * 16 + 16)
                    if not first:
                        pool.wait_ge(b_ready, upto(i - 1, UNROLL * TPG, s * TPG + 1))
                        pool.wait_ge(d_ready, upto(i - 1, UNROLL * TPG, s * TPG + 1))
                    pool.sem_inc(gather_turn, 1)
                    for t in range(TPG):
                        idx = RB[:, s, t, 4 * C + 4:4 * C + 5].bitcast(I32)
                        g.indirect_dma_start(out=GB[:, s, t, :], out_offset=None, in_=tab_dram,
                                             in_offset=bass.IndirectOffsetOnAxis(ap=idx, axis=0))\
                            .then_inc(gathered[s][t], 16)

            gather(0, True)
            with pool.Fori(1, MITER) as i:
                gather(i, False)

        @block.scalar
        def _(act):
            a = nc.scalar
            act.wait_ge(var_ready, 1)
            a.activation(rstd[0:NT, :], var_eps[0:NT, :], ACT.Sqrt).then_inc(std_ready, 1)
            act.wait_ge(nrm_sq, 1)
            a.activation(inv, ssq, ACT.Sqrt).then_inc(nrm_root, 1)
            a.preload_act_table_set("natural_log_exp_and_others")

            def evac_xT(t):
                act.wait_ge(xT_psum, t + 1)
                if t >= 2:
                    act.wait_ge(v_psum, t - 1)
                a.activation(XT[:, t % 2, :, :].rearrange("p k n -> p (k n)"), PS[:, t % 2, 0:KD * NT], ACT.Copy)\
                    .then_inc(xT_ready, 1)

            evac_xT(0)
            for t in range(NB):
                if t + 1 < NB:
                    evac_xT(t + 1)
                act.wait_ge(tab_psum, t + 1)
                if t >= 2:
                    act.wait_ge(tab_out[t % 2], 16 * (t // 2))
                a.activation(TAB[0:NT, t % 2, :], PS[0:NT, 2, :], ACT.Copy, scale=Y0 / float(np.sqrt(C)))\
                    .then_inc(tab_ready, 1)
                act.wait_ge(q_shift, t + 1)
                a.activation(QW[0:NT, :], QW[0:NT, :], ACT.Exp).then_inc(q_exp, 1)
                act.wait_ge(k_shift, t + 1)
                a.activation(KN[0:NT, t, :], KN[0:NT, t, :], ACT.Exp).then_inc(k_exp, 1)
                act.wait_ge(v_psum, t + 1)
                a.activation(VN[0:NT, t, :], PS[0:NT, 5, :], ACT.Copy).then_inc(v_ready, 1)
                act.wait_ge(qT_psum, t + 1)
                a.activation(QT[:, t, :, :].rearrange("p k n -> p (k n)"), PS[:, 6, 0:KD * NT], ACT.Copy)\
                    .then_inc(qT_ready, 1)
            act.wait_ge(ctx_psum, 1)
            act.wait_ge(ctx_zero, 1)
            for hh in range(2):
                r = slice(hh * DH, (hh + 1) * DH)
                a.activation(ctxT[r, :, hh * DH:(hh + 1) * DH],
                             PS[r, 0, :].rearrange("p (k n) -> p k n", k=KD)[:, :, hh * DH:(hh + 1) * DH], ACT.Copy)\
                    .then_inc(ctx_ready, 1)
            for k in range(KD):
                act.wait_ge(mo_psum, k + 1)
                a.activation(MO[:, k, :], PS[:, 1 + k % 2, :], ACT.Copy).then_inc(mo_ready, 1)

            act.wait_ge(mix_added, NB)
            act.wait_ge(router_ready, 1)
            a.activation(fT[0:32, :, :].rearrange("p h n -> p (h n)"),
                         ones[0:32, 0:1].to_broadcast([32, 2 * 512]), ACT.Copy).then_inc(act_step, 1)
            act.wait_ge(act_step, 1)

            def filters(i, first):
                def radial(h):
                    act.wait_ge(f_used, upto(i, 2, h))
                    if not first:
                        act.wait_ge(z_psum, upto(i - 1, 2, h))
                    a.activation(fT[0:R, h, :], PS[0:R, 0, :], ACT.Copy).then_inc(fT_ready, 1)

                def log_part(h):
                    act.wait_ge(z_psum, upto(i, 2, h))
                    if not first:
                        act.wait_ge(h_ready, upto(i - 1, 2, h))
                    a.activation(tz[:, h, :], PS[:, 1 + h, :], ACT.Abs).then_inc(z_abs, 1)
                    act.wait_ge(z_abs, upto(i, 2, h))
                    a.activation(tz[:, h, :], tz[:, h, :], ACT.Exp, scale=-1.0).then_inc(e_ready, 1)
                    act.wait_ge(e_ready, upto(i, 2, h))
                    a.activation(tz[:, h, :], tz[:, h, :], ACT.Ln, bias=half[:, 0:1], scale=0.5).then_inc(l_ready, 1)

                def even(h):
                    for j in range(h * UNROLL, (h + 1) * UNROLL, 2):
                        act.wait_ge(w_psum, upto(i, COLS, j))
                        act.wait_ge(staged, upto(i, 2, h))
                        a.activation(ST[:, j, 0:4 * C], PS[:, 3 + j % 4, :], ACT.Copy,
                                     scale=rcst[:, h, j % UNROLL:j % UNROLL + 1]).then_inc(w_even, 1)

                radial(0)
                log_part(0)
                radial(1)
                even(0)
                log_part(1)
                even(1)

            filters(0, True)
            with act.Fori(1, FITER) as i:
                filters(i, False)

            def c_messages(i, first):
                for s in range(UNROLL):
                    for t in range(TPG):
                        act.wait_ge(ac_ready, upto(i, UNROLL * TPG, s * TPG + t))
                        for k in range(3):
                            last = a.activation(MB[:, s % 2, t, 2 + k, :], MB[:, s % 2, t, 8, :], ACT.Copy,
                                                scale=RB[:, s, t, 4 * C + k:4 * C + k + 1])
                        last.then_inc(c_ready, 1)

            c_messages(0, True)
            with act.Fori(1, MITER) as i:
                c_messages(i, False)

            for t in range(NB):
                act.wait_ge(aT_psum, t + 1)
                if t:
                    act.wait_ge(sv_psum, t)
                for b in range(2):
                    last = a.activation(AT[:, 4 * b:4 * b + 4, 0:NT],
                                        PS[:, b, 0:4 * NT].rearrange("p (k n) -> p k n", n=NT), ACT.Copy)
                last.then_inc(aT_ready, 1)
                act.wait_ge(sv_psum, t + 1)
                if t:
                    act.wait_ge(g_psum, t)
                a.activation(sz[:, 0:NT], PS[:, 2, 0:NT], ACT.Abs).then_inc(s_abs, 1)
                a.activation(S1[:, 1:4, 0:NT], PS[:, 2, NT:4 * NT].rearrange("p (k n) -> p k n", n=NT), ACT.Copy)\
                    .then_inc(v1_ready, 1)
                act.wait_ge(s_abs, 2 * t + 1)
                a.activation(sz[:, 0:NT], sz[:, 0:NT], ACT.Exp, scale=-1.0).then_inc(s_abs, 1)
                act.wait_ge(s_abs, 2 * t + 2)
                a.activation(sz[:, 0:NT], sz[:, 0:NT], ACT.Ln, bias=half[:, 0:1], scale=0.5).then_inc(s_ln, 1)
            act.wait_ge(var2_ready, 1)
            a.activation(rstd[0:NT, :], var_eps[0:NT, :], ACT.Sqrt).then_inc(std2_ready, 1)
            for t in range(NB):
                act.wait_ge(xfT_psum, t + 1)
                if t >= 2:
                    act.wait_ge(eo_psum, (t - 1) * X8)
                a.activation(XFT[:, t % 2, :, 0:NT],
                             PS[:, 0, 0:KD * NT].rearrange("p (k n) -> p k n", k=KD), ACT.Copy).then_inc(xfT_ready, 1)
                act.wait_ge(shift_ready, t + 1)
                a.activation(prob[0:NT, :], prob[0:NT, :], ACT.Exp).then_inc(prob_exp, 1)
                act.wait_ge(combT_psum, t + 1)
                a.activation(comb_t[0:X8, 0:NT], PS[0:X8, 1, 16:16 + NT], ACT.Copy).then_inc(combT_ready, 1)

        @block.vector
        def _(dve):
            v = nc.vector
            steps = [0]

            def step(ins):
                steps[0] += 1
                ins.then_inc(dve_step, 1)
                dve.wait_ge(dve_step, steps[0])

            dve.wait_ge(x_in[0], 16)
            for t in range(NB):
                if t == 2:
                    dve.wait_ge(x_in[1], 16)
                last = v.bn_stats(stats[0:NT, t, :], X[0:NT, t, :])
            step(last)
            for t in range(NB):
                last = v.bn_aggr(aggr[0:NT, t, :], stats[0:NT, t, :])
            step(last)
            v.tensor_scalar(var_eps[0:NT, :], aggr[0:NT, :, 1], EPS, None, ALU.add).then_inc(var_ready, 1)
            step(v.memset(half[:, :], 0.5))
            step(v.tensor_copy(mean[0:NT, :], aggr[0:NT, :, 0]))
            dve.wait_ge(std_ready, 1)
            step(v.reciprocal(rstd[0:NT, :], rstd[0:NT, :]))

            def normal(t):
                if t >= 2:
                    dve.wait_ge(xT_psum, t - 1)
                v.tensor_scalar(XN[0:NT, t % 2, :], X[0:NT, t, :], mean[0:NT, t:t + 1], rstd[0:NT, t:t + 1],
                                ALU.subtract, ALU.mult).then_inc(xn_ready, 1)

            normal(0)
            normal(1)
            dve.wait_ge(consts, 2)
            dve.wait_ge(edge_in, 16 * 6)
            step(v.tensor_tensor(rtmp, rraw, rraw, ALU.mult))
            step(v.tensor_tensor(ssq, rtmp[:, :, 0], rtmp[:, :, 1], ALU.add))
            v.tensor_tensor(ssq, ssq, rtmp[:, :, 2], ALU.add).then_inc(nrm_sq, 1)
            step(v.tensor_copy(meta[:, 0:RC1, 4].bitcast(I32), dsti))
            dve.wait_ge(b2_in, 16)
            dve.wait_ge(wf_in, 48)
            w4 = wf2raw.rearrange("p (g f a) -> p g a f", g=2, a=2)
            r4 = b2raw.rearrange("p (g f a) -> p g a f", g=2, a=2)
            step(v.tensor_copy(wf2[:, :, :].rearrange("p (g a) f -> p g a f", g=2), w4))
            step(v.tensor_copy(b2rem.rearrange("p (g a f) -> p g a f", g=2, a=2), r4))
            step(v.tensor_scalar(wf2[:, 2, :], wf2[:, 2, :], float(np.sqrt(3.0)), None, ALU.mult))
            step(v.tensor_scalar(b2rem[:, 2 * C:3 * C], b2rem[:, 2 * C:3 * C], float(np.sqrt(3.0)), None, ALU.mult))
            for k in range(3):
                last = v.tensor_copy(b2p[k], b2rem)
                if k < 2:
                    step(last)
                    step(v.tensor_tensor(b2rem, b2rem, b2p[k], ALU.subtract))
            last.then_inc(b2_parts, 1)
            dve.wait_ge(nrm_root, 1)
            step(v.reciprocal(inv, inv))
            step(v.tensor_tensor(meta[:, 0:RC1, 0:3], rraw, inv.unsqueeze(2).to_broadcast([P, RC1, 3]), ALU.mult))
            step(v.tensor_copy(srcf, srci))
            step(v.memset(srcf[REM:P, FULL:RC1], 1e6))
            step(v.tensor_scalar(bkt, srcf, float(NT), None, ALU.is_ge))
            for b in range(2, NB + 1):
                step(v.scalar_tensor_tensor(bkt, srcf, float(b * NT), bkt, ALU.is_ge, ALU.add))
            v.scalar_tensor_tensor(meta[:, 0:RC1, 3], bkt, float(-NT), srcf, ALU.mult, ALU.add)
            step(v.memset(rnk, 0.0))

            def shift(bank, dst, mx, psum_ready, t, signal):
                dve.wait_ge(psum_ready, t + 1)
                src3 = PS[0:NT, bank, :].rearrange("p (h d) -> p h d", h=HEADS)
                step(v.reduce_max(mx[0:NT, :], src3, AX_X))
                v.tensor_tensor(dst.rearrange("p (h d) -> p h d", h=HEADS), src3,
                                mx[0:NT, :].unsqueeze(2).to_broadcast([NT, HEADS, DH]), ALU.subtract)\
                    .then_inc(signal, 1)

            def normalise(dst, sm, exp_ready, t, signal):
                dve.wait_ge(exp_ready, t + 1)
                d3 = dst.rearrange("p (h d) -> p h d", h=HEADS)
                step(v.reduce_sum(sm[0:NT, :], d3, AX_X))
                step(v.reciprocal(sm[0:NT, :], sm[0:NT, :]))
                v.tensor_tensor(d3, d3, sm[0:NT, :].unsqueeze(2).to_broadcast([NT, HEADS, DH]), ALU.mult)\
                    .then_inc(signal, 1)

            for t in range(NB):
                if t + 2 < NB:
                    normal(t + 2)
                if t == 0:
                    dve.wait_ge(b2_placed, 48)
                else:
                    dve.wait_ge(qT_psum, t)
                shift(3, QW[0:NT, :], mxq, q_psum, t, q_shift)
                shift(4, KN[0:NT, t, :], mxk, k_psum, t, k_shift)
                normalise(QW[0:NT, :], smq, q_exp, t, q_norm)
                normalise(KN[0:NT, t, :], smk, k_exp, t, k_norm)
                step(v.tensor_scalar(tA, bkt, float(t), None, ALU.is_equal))
                step(v.tensor_tensor_scan(tB, ones[:, 0:RC1], tA, 0.0, ALU.mult, ALU.add))
                v.tensor_copy(cnt[:, t:t + 1], tB[:, RC1 - 1:RC1]).then_inc(counts_ready, 1)
                step(v.tensor_tensor(tA, tA, tB, ALU.mult))
                step(v.tensor_tensor(rnk, rnk, tA, ALU.add))
            dve.wait_ge(counts_psum, 1)
            step(v.tensor_copy(pref, PS[:, 7, 0:NB]))
            step(v.tensor_copy(tot, PS[:, 7, NB:2 * NB]))
            step(v.tensor_scalar(ints[:, 0:NB], tot, float(GROUP - 1), None, ALU.add))
            step(v.tensor_scalar(ints[:, 0:NB], ints[:, 0:NB], GROUP.bit_length() - 1, None, ALU.arith_shift_right))
            step(v.tensor_copy(ngf, ints[:, 0:NB]))
            step(v.tensor_tensor_scan(endg, ones[:, 0:NB], ngf, 0.0, ALU.mult, ALU.add))
            step(v.tensor_tensor_scan(cumt, ones[:, 0:NB], tot, 0.0, ALU.mult, ALU.add))
            step(v.tensor_tensor(base, endg, ngf, ALU.subtract))
            step(v.tensor_scalar(base, base, float(GROUP), None, ALU.mult))
            step(v.scalar_tensor_tensor(off, pref, -1.0, base, ALU.add, ALU.add))
            step(v.tensor_tensor(cpad, base, cumt, ALU.subtract))
            step(v.tensor_tensor(cpad, cpad, tot, ALU.add))
            step(v.tensor_copy(pd, kd))
            for b in range(NB):
                step(v.tensor_scalar(tA, bkt, float(b), off[:, b:b + 1], ALU.is_equal, ALU.mult))
                step(v.tensor_tensor(rnk, rnk, tA, ALU.add))
                step(v.tensor_scalar(tB[:, 0:SPARE], kd, cpad[:, b:b + 1], tot[:, b:b + 1], ALU.is_ge, ALU.mult))
                step(v.tensor_tensor(pd, pd, tB[:, 0:SPARE], ALU.add))
            step(v.tensor_copy(posi[:, 0:RC1], rnk))
            step(v.tensor_copy(posi[:, RC1:NCOL], pd[:, 1:SPARE]))
            step(v.tensor_copy(posi[REM:P, FULL:RC1], pd[REM:P, 0:1]))
            step(v.tensor_copy(tA[:, 0:GROUPS], goff[:, :]))
            step(v.tensor_scalar(tB[:, 0:GROUPS], tA[:, 0:GROUPS], endg[:, 0:1], None, ALU.is_ge))
            for b in range(1, NB - 1):
                step(v.scalar_tensor_tensor(tB[:, 0:GROUPS], tA[:, 0:GROUPS], endg[:, b:b + 1], tB[:, 0:GROUPS],
                                            ALU.is_ge, ALU.add))
            step(v.tensor_scalar(goff[:, :], tB[:, 0:GROUPS], float(MSG), None, ALU.mult))
            dve.wait_ge(w12_in, 16 * 5)
            v.tensor_scalar(w1s[:, :, :], w1s[:, :, :], float(1 / np.sqrt(2 * C)), None, ALU.mult)
            v.tensor_scalar(w1v[:, :, :], w1v[:, :, :], float(1 / np.sqrt(2 * C)), None, ALU.mult)
            v.tensor_scalar(w2s[:, :], w2s[:, :], float(1 / np.sqrt(C)), None, ALU.mult)
            v.tensor_scalar(w2v[:, :], w2v[:, :], float(1 / np.sqrt(C)), None, ALU.mult)
            dve.wait_ge(ctx_psum, 1)
            v.memset(ctxT[:, :, :].rearrange("p k n -> p (k n)"), 0.0).then_inc(ctx_zero, 1)
            dve.wait_ge(bo_in, 16)
            step(v.tensor_tensor(X[0:NT, :, :], X[0:NT, :, :],
                                 bo_b[0:NT, :].unsqueeze(1).to_broadcast([NT, NB, D]), ALU.add))
            for t in range(NB):
                dve.wait_ge(y_psum, t + 1)
                v.tensor_tensor(X[0:NT, t, :], X[0:NT, t, :], PS[0:NT, 3 + t % 2, :], ALU.add).then_inc(mix_added, 1)
            dve.wait_ge(mi_psum, 1)
            step(v.tensor_scalar(mi, PS[:, 5, 0:KD], 1.0 / NI, None, ALU.mult))
            step(v.memset(z_mi, 0.0))
            for e in range(X8):
                v.tensor_copy(z_mi[:, :, e, e], mi)
            v.tensor_copy(mi_bc, mi.unsqueeze(2).to_broadcast([P, KD, P])).then_inc(z_ready, 1)
            dve.wait_ge(gamT_psum, 1)
            v.tensor_copy(gamT, PS[:, 0, 0:KD * X8].rearrange("p (k e) -> p k e", k=KD)).then_inc(gamT_ready, 1)
            dve.wait_ge(gam_psum, 1)
            v.tensor_copy(gam8, PS[:, 6, 0:X8])
            v.tensor_copy(rgam, PS[:, 6, 8:8 + X8])
            step(v.tensor_copy(gcol[0:X8, :], PS[0:X8, 6, 16:17]))
            dve.wait_ge(beta_used, X8)
            v.scalar_tensor_tensor(bb[0:X8, :], be_row, gcol[0:X8, :], PS[0:X8, 7, :], ALU.mult, ALU.add)\
                .then_inc(router_ready, 1)
            dve.wait_ge(router_ready, 1)
            dve.wait_ge(f_in, 32)
            dve.wait_ge(rcut_in, 32)

            def filters(i, first):
                def stage(h):
                    c0 = i * COLS + h * UNROLL
                    cols = slice(c0, c0 + UNROLL) if first else ds(c0, UNROLL)
                    if not first:
                        for j in range(h * UNROLL, (h + 1) * UNROLL):
                            dve.wait_ge(scattered[j], i * 16)
                        dve.wait_ge(f_used, upto(i - 1, 2, h))
                    v.tensor_copy(Fst[:, h, :, :], Fe[:, cols, :])
                    v.tensor_copy(rcst[:, h, :], rcut[:, cols])
                    v.tensor_copy(ST[:, h * UNROLL:(h + 1) * UNROLL, 4 * C:REC], meta[:, cols, :])
                    v.tensor_copy(idxst[:, h * UNROLL:(h + 1) * UNROLL], posi[:, cols]).then_inc(staged, 1)

                def hidden(h):
                    dve.wait_ge(l_ready, upto(i, 2, h))
                    if not first:
                        dve.wait_ge(w_psum, upto(i - 1, COLS, (h + 1) * UNROLL - 1))
                    v.scalar_tensor_tensor(hT[:, h, :], PS[:, 1 + h, :], 0.0, tz[:, h, :], ALU.max, ALU.add)\
                        .then_inc(h_ready, 1)

                def odd(h):
                    for j in range(h * UNROLL + 1, (h + 1) * UNROLL, 2):
                        dve.wait_ge(w_psum, upto(i, COLS, j))
                        dve.wait_ge(staged, upto(i, 2, h))
                        v.tensor_scalar(ST[:, j, 0:4 * C], PS[:, 3 + j % 4, :],
                                        rcst[:, h, j % UNROLL:j % UNROLL + 1], None, ALU.mult).then_inc(w_odd, 1)

                stage(0)
                hidden(0)
                stage(1)
                odd(0)
                hidden(1)
                odd(1)

            filters(0, True)
            with dve.Fori(1, FITER) as i:
                filters(i, False)

            def messages(i, first):
                per = UNROLL * TPG
                for s in range(UNROLL):
                    prev_free = not first or s >= 2
                    for t in range(TPG):
                        n = s * TPG + t
                        if t == 0:
                            dve.wait_ge(rec_in[s], i * 16 + 16)
                            if s >= 2:
                                dve.wait_ge(summed, upto(i, UNROLL, s - 2))
                            elif not first:
                                dve.wait_ge(summed, upto(i - 1, UNROLL, s + 2))
                        v.tensor_scalar(OH[:, s % 2, t, 0:NT], iota_f[:, 0:NT], RB[:, s, t, 4 * C + 3:4 * C + 4], None,
                                        ALU.is_equal).then_inc(onehot, 1)
                    for t in range(TPG):
                        n = s * TPG + t
                        dve.wait_ge(gathered[s][t], i * 16 + 16)
                        if s > 0:
                            dve.wait_ge(b_ready, upto(i, per, n - TPG))
                        elif not first:
                            dve.wait_ge(b_ready, upto(i - 1, per, per - TPG + t))
                        v.tensor_scalar(DT[:, t, 0, :], GB[:, s, t, C:2 * C], RB[:, s, t, 4 * C:4 * C + 1], None,
                                        ALU.mult).then_inc(dot1, 1)
                    for t in range(TPG):
                        w4 = RB[:, s, t, 0:4 * C].rearrange("p (k n) -> p k n", k=4)
                        v.tensor_tensor(MB[:, s % 2, t, 0:9:8, :], w4[:, 0:3:2, :],
                                        GB[:, s, t, 0:C].unsqueeze(1).to_broadcast([P, 2, C]), ALU.mult)\
                            .then_inc(ac_ready, 1)
                    for k, (have, done) in enumerate(((dot1, dot2), (dot2, dot3))):
                        for t in range(TPG):
                            n = s * TPG + t
                            dve.wait_ge(have, upto(i, per, n))
                            v.scalar_tensor_tensor(DT[:, t, k + 1, :], GB[:, s, t, (k + 2) * C:(k + 3) * C],
                                                   RB[:, s, t, 4 * C + k + 1:4 * C + k + 2], DT[:, t, k, :],
                                                   ALU.mult, ALU.add).then_inc(done, 1)
                    for t in range(TPG):
                        w4 = RB[:, s, t, 0:4 * C].rearrange("p (k n) -> p k n", k=4)
                        v.tensor_tensor(MB[:, s % 2, t, 5:8, :],
                                        GB[:, s, t, C:4 * C].rearrange("p (k n) -> p k n", k=3),
                                        w4[:, 3:4, :].to_broadcast([P, 3, C]), ALU.mult).then_inc(d_ready, 1)
                    for t in range(TPG):
                        dve.wait_ge(dot3, upto(i, per, s * TPG + t))
                        v.tensor_tensor(MB[:, s % 2, t, 1, :], DT[:, t, 2, :], RB[:, s, t, C:2 * C], ALU.mult)\
                            .then_inc(b_ready, 1)
                    if s > 0:
                        flush(i, s - 1, first)
                    elif not first:
                        flush(i - 1, UNROLL - 1, first)

            def flush(i, s, static):
                g = i * UNROLL + s
                dve.wait_ge(summed, upto(i, UNROLL, s))
                if not (static and s == 0):
                    dve.wait_ge(flushed, i * UNROLL + s) if not static else dve.wait_ge(flushed, s)
                o = dve.value_load(goff[0:1, ds(g, 1)] if not static else goff[0:1, g:g + 1], min_val=0,
                                   max_val=(NB - 1) * MSG)
                dst_ap = acc[0:NT, ds(o, MSG)]
                v.tensor_tensor(dst_ap, dst_ap, PS[0:NT, 2 * (s % 2):2 * (s % 2) + 2, :].rearrange("p b n -> p (b n)"),
                                ALU.add).then_inc(flushed, 1)

            for j in range(COLS):
                dve.wait_ge(scattered[j], 16 * FITER)
            dve.wait_ge(acc_zero, 1)
            messages(0, True)
            with dve.Fori(1, MITER) as i:
                messages(i, False)
            last_g = GROUPS - 1
            dve.wait_ge(summed, GROUPS)
            dve.wait_ge(flushed, GROUPS - 1)
            o = dve.value_load(goff[0:1, last_g:last_g + 1], min_val=0, max_val=(NB - 1) * MSG)
            v.tensor_tensor(acc[0:NT, ds(o, MSG)], acc[0:NT, ds(o, MSG)], PS[0:NT, 2:4, :].rearrange("p b n -> p (b n)"),
                            ALU.add).then_inc(flushed, 1)

            for t in range(NB):
                dve.wait_ge(s_ln, t + 1)
                v.scalar_tensor_tensor(S1[:, 0, 0:NT], PS[:, 2, 0:NT], 0.0, sz[:, 0:NT], ALU.max, ALU.add)\
                    .then_inc(s_ready, 1)
                dve.wait_ge(g_psum, t + 1)
                v.tensor_tensor(X[0:NT, t, 0:C], X[0:NT, t, 0:C], PS[0:NT, 3, 0:C], ALU.add)
                xi = X[0:NT, t, C:D].rearrange("p (c i) -> p c i", i=3)
                step(v.tensor_tensor(xi, xi, PS[0:NT, 3, C:D].rearrange("p (i c) -> p c i", i=3), ALU.add))
                step(v.bn_stats(stats[0:NT, t, :], X[0:NT, t, :]))
                v.bn_aggr(aggr[0:NT, t, :], stats[0:NT, t, :]).then_inc(x1_ready, 1)
            dve.wait_ge(x1_ready, NB)
            v.tensor_scalar(var_eps[0:NT, :], aggr[0:NT, :, 1], EPS, None, ALU.add).then_inc(var2_ready, 1)
            step(v.tensor_copy(mean[0:NT, :], aggr[0:NT, :, 0]))
            dve.wait_ge(std2_ready, 1)
            step(v.reciprocal(rstd[0:NT, :], rstd[0:NT, :]))

            def normal2(t):
                if t >= 2:
                    dve.wait_ge(xfT_psum, t - 1)
                v.tensor_scalar(XF[0:NT, t % 2, :], X[0:NT, t, :], mean[0:NT, t:t + 1], rstd[0:NT, t:t + 1],
                                ALU.subtract, ALU.mult).then_inc(xf_ready, 1)

            normal2(0)
            normal2(1)
            for t in range(NB):
                dve.wait_ge(logit_psum, t + 1)
                if t:
                    dve.wait_ge(combT_psum, t)
                step(v.tensor_tensor(prob[0:NT, :], PS[0:NT, 1, 0:X8], rgam[0:NT, :], ALU.add))
                step(v.reduce_max(st1[0:NT, 0:1], prob[0:NT, :], AX_X))
                v.tensor_scalar(prob[0:NT, :], prob[0:NT, :], st1[0:NT, 0:1], None, ALU.subtract)\
                    .then_inc(shift_ready, 1)
                dve.wait_ge(prob_exp, t + 1)
                step(v.reduce_sum(st1[0:NT, 0:1], prob[0:NT, :], AX_X))
                step(v.reciprocal(st1[0:NT, 0:1], st1[0:NT, 0:1]))
                step(v.tensor_scalar(prob[0:NT, :], prob[0:NT, :], st1[0:NT, 0:1], None, ALU.mult))
                mine = prob[0:NT, :].unsqueeze(2).to_broadcast([NT, X8, X8])
                others = prob[0:NT, :].unsqueeze(1).to_broadcast([NT, X8, X8])
                step(v.tensor_tensor(cmp_a[0:NT], others, mine, ALU.is_gt))
                step(v.tensor_tensor(cmp_b[0:NT], others, mine, ALU.is_equal))
                step(v.tensor_tensor(cmp_b[0:NT], cmp_b[0:NT], tie[0:NT], ALU.mult))
                step(v.tensor_tensor(cmp_a[0:NT], cmp_a[0:NT], cmp_b[0:NT], ALU.add))
                step(v.reduce_sum(rank[0:NT, :], cmp_a[0:NT], AX_X))
                step(v.scalar_tensor_tensor(comb[0:NT, :], rank[0:NT, :], 2.0, prob[0:NT, :], ALU.is_lt, ALU.mult))
                v.tensor_tensor(cg[0:NT, :], comb[0:NT, :], gam8[0:NT, :], ALU.mult).then_inc(comb_ready, 1)
                if t + 2 < NB:
                    normal2(t + 2)
                dve.wait_ge(comb_ready, t + 1)
                for e in range(X8):
                    n = t * X8 + e
                    dve.wait_ge(eo_psum, n + 1)
                    if n:
                        dve.wait_ge(eo_used, n)
                    v.scalar_tensor_tensor(X[0:NT, t, :], PS[0:NT, 4 + n % 4, :], cg[0:NT, e:e + 1], X[0:NT, t, :],
                                           ALU.mult, ALU.add).then_inc(eo_used, 1)
                dve.wait_ge(bias_psum, t + 1)
                dve.wait_ge(eo_used, (t + 1) * X8)
                v.tensor_tensor(X[0:NT, t, :], X[0:NT, t, :], PS[0:NT, 2, :], ALU.add).then_inc(o_ready, 1)

        @block.tensor
        def _(pe):
            te = nc.tensor
            idn = ident[0:NT, 0:NT]
            pe.wait_ge(consts, 1)

            def transpose_x(t):
                pe.wait_ge(xn_ready, t + 1)
                if t >= 2:
                    pe.wait_ge(xT_ready, t - 1)
                for k in range(KD):
                    src_ap = XN[0:NT, t % 2, 0:C] if k == 0 else XN[0:NT, t % 2, C + k - 1:D:3]
                    last = te.transpose(PS[:, t % 2, k * NT:(k + 1) * NT], src_ap, idn)
                last.then_inc(xT_psum, 1)

            transpose_x(0)
            for t in range(NB):
                if t + 1 < NB:
                    transpose_x(t + 1)
                pe.wait_ge(xT_ready, t + 1)
                if t == 0:
                    pe.wait_ge(wsv_in, 32)
                else:
                    pe.wait_ge(tab_ready, t)
                for k in range(KD):
                    last = te.matmul(PS[0:NT, 2, k * C:(k + 1) * C], XT[:, t % 2, k, :], wsv[:, min(k, 1), :],
                                     start=True, stop=True)
                last.then_inc(tab_psum, 1)
                for w, (ready, free) in enumerate(((q_psum, q_shift), (k_psum, k_shift), (v_psum, v_ready))):
                    if t == 0:
                        pe.wait_ge(wqkv_in[w], 32)
                    else:
                        pe.wait_ge(free, t)
                    for k in range(KD):
                        last = te.matmul(PS[0:NT, 3 + w, :], XT[:, t % 2, k, :], wqkv[:, w, k, :],
                                         start=(k == 0), stop=(k == KD - 1))
                    last.then_inc(ready, 1)
                pe.wait_ge(q_norm, t + 1)
                if t:
                    pe.wait_ge(qT_ready, t)
                for k in range(KD):
                    last = te.transpose(PS[:, 6, k * NT:(k + 1) * NT], QW[0:NT, k * P:(k + 1) * P], idn)
                last.then_inc(qT_psum, 1)
            pe.wait_ge(k_norm, NB)
            pe.wait_ge(v_ready, NB)
            for k in range(KD):
                for t in range(NB):
                    last = te.matmul(PS[:, 0, k * P:(k + 1) * P], VN[0:NT, t, k * P:(k + 1) * P],
                                     KN[0:NT, t, k * P:(k + 1) * P], start=(t == 0), stop=(t == NB - 1))
            last.then_inc(ctx_psum, 1)
            pe.wait_ge(counts_ready, NB)
            te.matmul(PS[:, 7, 0:NB], ltri[:, :], cnt, start=True, stop=True)
            te.matmul(PS[:, 7, NB:2 * NB], ones[:, 0:P], cnt, start=True, stop=True).then_inc(counts_psum, 1)
            pe.wait_ge(wo_in, 16)
            pe.wait_ge(ctx_ready, 2)
            for k in range(KD):
                if k >= 2:
                    pe.wait_ge(mo_ready, k - 1)
                elif k == 1:
                    pe.wait_ge(tab_ready, NB)
                te.matmul(PS[:, 1 + k % 2, :], ctxT[:, k, :], wo[:, k, :], start=True, stop=True).then_inc(mo_psum, 1)
            for t in range(NB):
                pe.wait_ge(mo_ready, KD)
                pe.wait_ge(qT_ready, t + 1)
                if t >= 2:
                    pe.wait_ge(mix_added, t - 1)
                for k in range(KD):
                    last = te.matmul(PS[0:NT, 3 + t % 2, :], QT[:, t, k, :], MO[:, k, :], start=(k == 0),
                                     stop=(k == KD - 1))
                last.then_inc(y_psum, 1)
            pe.wait_ge(ffn_small_in, 64)
            for k in range(KD):
                last = te.matmul(PS[:, 5, k:k + 1], ins_sb[:, k * P:(k + 1) * P], ones[0:NI, 0:1], start=True, stop=True)
            last.then_inc(mi_psum, 1)
            for k in range(KD):
                last = te.transpose(PS[:, 0, k * X8:(k + 1) * X8], gam_row[:, k * P:(k + 1) * P],
                                    ident[0:X8, 0:X8])
            last.then_inc(gamT_psum, 1)
            pe.wait_ge(z_ready, 1)
            pe.wait_ge(gamT_ready, 1)
            for lo, m, w in ((0, mi_bc, gamT), (8, mi_bc, rmod)):
                for k in range(KD):
                    te.matmul(PS[:, 6, lo:lo + X8], m[:, k, :], w[:, k, :], start=(k == 0), stop=(k == KD - 1))
            for k in range(KD):
                last = te.matmul(PS[0:X8, 6, 16:17], gamT[:, k, :], mi[:, k:k + 1], start=(k == 0), stop=(k == KD - 1))
            last.then_inc(gam_psum, 1)
            for e in range(X8):
                pe.wait_ge(beta_in[e % 2], 16 * (e // 2 + 1))
                for k in range(KD):
                    last = te.matmul(PS[0:X8, 7, :], z_mi[:, k, e, :], bslot[e % 2][:, k, :],
                                     start=(e == 0 and k == 0), stop=(e == X8 - 1 and k == KD - 1))
                last.then_inc(beta_used, 1)

            pe.wait_ge(b2_placed, 48)
            pe.wait_ge(router_ready, 1)
            pe.wait_ge(act_step, 1)

            def filters(i, first):
                for h in range(2):
                    pe.wait_ge(staged, upto(i, 2, h))
                    if not (first and h == 0):
                        pe.wait_ge(fT_ready, i * 2 + h)
                    for c in range(UNROLL):
                        last = te.transpose(PS[0:R, 0, c * P:(c + 1) * P], Fst[:, h, c, :], ident[:, :])
                    last.then_inc(f_used, 1)
                    pe.wait_ge(fT_ready, upto(i, 2, h))
                    if not first:
                        pe.wait_ge(h_ready, upto(i - 1, 2, h))
                    te.matmul(PS[:, 1 + h, :], wf1[:, :], fT[0:R + 1, h, :], start=True, stop=True).then_inc(z_psum, 1)
                for h in range(2):
                    pe.wait_ge(h_ready, upto(i, 2, h))
                    for j in range(h * UNROLL, (h + 1) * UNROLL):
                        free = w_odd if j % 2 else w_even
                        if j >= 4:
                            pe.wait_ge(free, upto(i, COLS // 2, (j - 4) // 2))
                        elif not first:
                            pe.wait_ge(free, upto(i - 1, COLS // 2, (j + 4) // 2))
                        te.matmul(PS[:, 3 + j % 4, :], ones3[:, :], b2s[:, :, :].rearrange("p k n -> p (k n)"),
                                  start=True, stop=False)
                        te.matmul(PS[:, 3 + j % 4, :], hT[:, h, (j % UNROLL) * P:(j % UNROLL + 1) * P],
                                  wf2[:, :, :].rearrange("p k n -> p (k n)"), start=False, stop=True).then_inc(w_psum, 1)

            filters(0, True)
            with pe.Fori(1, FITER) as i:
                filters(i, False)
            pe.wait_ge(w_even, FITER * COLS // 2)
            pe.wait_ge(w_odd, FITER * COLS // 2)

            def sums(i, first):
                per = UNROLL * TPG
                for s in range(UNROLL):
                    if s >= 2:
                        pe.wait_ge(flushed, upto(i, UNROLL, s - 2))
                    elif not first:
                        pe.wait_ge(flushed, upto(i - 1, UNROLL, s + 2))
                    for t in range(TPG):
                        n = s * TPG + t
                        pe.wait_ge(onehot, upto(i, per, n))
                        pe.wait_ge(c_ready, upto(i, per, n))
                        pe.wait_ge(d_ready, upto(i, per, n))
                        pe.wait_ge(b_ready, upto(i, per, n))
                        for half_ in range(2):
                            last = te.matmul(PS[0:NT, 2 * (s % 2) + half_, :], OH[:, s % 2, t, 0:NT],
                                             MB[:, s % 2, t, 4 * half_:4 * half_ + 4, :].rearrange("p k n -> p (k n)"),
                                             start=(t == 0), stop=(t == TPG - 1))
                    last.then_inc(summed, 1)

            sums(0, True)
            with pe.Fori(1, MITER) as i:
                sums(i, False)

            pe.wait_ge(flushed, GROUPS)
            for t in range(NB):
                if t:
                    pe.wait_ge(aT_ready, t)
                for k in range(8):
                    last = te.transpose(PS[:, k // 4, (k % 4) * NT:(k % 4 + 1) * NT],
                                        acc[0:NT, t * MSG + k * C:t * MSG + (k + 1) * C], idn)
                last.then_inc(aT_psum, 1)
                pe.wait_ge(aT_ready, t + 1)
                if t:
                    pe.wait_ge(s_ready, t)
                    pe.wait_ge(v1_ready, t)
                for k in range(2):
                    te.matmul(PS[:, 2, 0:NT], w1s[:, k, :], AT[:, k, 0:NT], start=(k == 0), stop=(k == 1))
                for k in range(2):
                    last = te.matmul(PS[:, 2, NT:4 * NT].rearrange("p (k n) -> p k n", n=NT), w1v[:, k, :],
                                     AT[:, 2 + 3 * k:5 + 3 * k, 0:NT], start=(k == 0), stop=(k == 1))
                last.then_inc(sv_psum, 1)
                pe.wait_ge(s_ready, t + 1)
                pe.wait_ge(v1_ready, t + 1)
                if t:
                    pe.wait_ge(x1_ready, t)
                for k in range(4):
                    last = te.matmul(PS[0:NT, 3, k * C:(k + 1) * C], S1[:, k, 0:NT], w2v[:, :] if k else w2s[:, :],
                                     start=True, stop=True)
                last.then_inc(g_psum, 1)
            pe.wait_ge(x1_ready, NB)
            for t in range(NB):
                pe.wait_ge(xf_ready, t + 1)
                if t:
                    pe.wait_ge(xfT_ready, t)
                for k in range(KD):
                    last = te.transpose(PS[:, 0, k * NT:(k + 1) * NT], XF[0:NT, t % 2, k * P:(k + 1) * P], idn)
                last.then_inc(xfT_psum, 1)
                pe.wait_ge(xfT_ready, t + 1)
                if t:
                    pe.wait_ge(combT_ready, t)
                for k in range(KD):
                    last = te.matmul(PS[0:NT, 1, 0:X8], XFT[:, t % 2, k, 0:NT], gate[:, k, :], start=(k == 0),
                                     stop=(k == KD - 1))
                last.then_inc(logit_psum, 1)
                if t == 0:
                    pe.wait_ge(we_in, 16)
                for e in range(X8):
                    n = t * X8 + e
                    if n >= 4:
                        pe.wait_ge(eo_used, n - 3)
                    if e == 4:
                        pe.wait_ge(comb_ready, t + 1)
                        te.transpose(PS[0:X8, 1, 16:16 + NT], comb[0:NT, :], idn).then_inc(combT_psum, 1)
                    for k in range(KD):
                        last = te.matmul(PS[0:NT, 4 + n % 4, :], XFT[:, t % 2, k, 0:NT], we[:, e, k, :],
                                         start=(k == 0), stop=(k == KD - 1))
                    last.then_inc(eo_psum, 1)
                pe.wait_ge(combT_ready, t + 1)
                if t:
                    pe.wait_ge(o_ready, t)
                te.matmul(PS[0:NT, 2, :], comb_t[0:X8, 0:NT], bb[0:X8, :], start=True, stop=True).then_inc(bias_psum, 1)


_INS = ["x", "src", "dst", "edge_attr_20", "edge_attr_3", "edge_weight", "L0_gnn_W_in2f_s", "L0_gnn_W_in2f_v",
        "L0_gnn_Wf1", "L0_gnn_bf1", "L0_gnn_Wf2", "L0_gnn_bf2", "L0_gnn_W1_s", "L0_gnn_W1_v", "L0_gnn_W2_s",
        "L0_gnn_W2_v", "L0_mix_Wq", "L0_mix_Wk", "L0_mix_Wv", "L0_mix_Wo", "L0_mix_bo", "L0_ffn_Ins_tk",
        "L0_ffn_gate_w", "L0_ffn_expert_w", "L0_ffn_expert_b", "L0_ffn_gamma_w", "L0_ffn_beta_w", "L0_ffn_rmod_w"]


def kernel(**inputs):
    import concourse.bacc as bacc
    from concourse.bass_utils import run_bass_kernel_spmd

    nc = bacc.Bacc("TRN2", target_bir_lowering=False, num_devices=1)
    arrays, args = {}, []
    for name in _INS:
        a = np.ascontiguousarray(inputs[name])
        arrays[f"in_{name}"] = a
        args.append(nc.dram_tensor(f"in_{name}", a.shape, mybir.dt.from_np(a.dtype), kind="ExternalInput").ap())
    shape = tuple(np.shape(inputs["x"]))
    args.append(nc.dram_tensor("out_0", shape, F32, kind="ExternalOutput").ap())
    gps_layer(nc, *args)
    return run_bass_kernel_spmd(nc, [arrays], core_ids=[0]).results[0]["out_0"]
```

```python
from contextlib import ExitStack

import numpy as np

import concourse.bass as bass
from concourse import mybir

F32 = mybir.dt.float32
F32R = mybir.dt.float32r
BF16 = mybir.dt.bfloat16
I32 = mybir.dt.int32
ALU = mybir.AluOpType
ACT = mybir.ActivationFunctionType
AX_X = mybir.AxisListType.X
ds = bass.ds

P = 128
GROUP = 512
TPG = 2
PPG = GROUP // (TPG * P)
UNROLL = 8
STEP = 4
LAG = 7
EPS = 1e-5


def upto(i, per, j):
    return i * per + (j + 1)


def real(count):
    return not isinstance(count, int) or count >= 1


def gps_layer(nc, x, src, dst, edge_attr_20, edge_attr_3, edge_weight, W_in2f_s, W_in2f_v, Wf1, bf1, Wf2, bf2,
              W1_s, W1_v, W2_s, W2_v, Wq, Wk, Wv, Wo, bo, Ins_tk, gate_w, expert_w, expert_b, gamma_w, beta_w,
              rmod_w, out):
    N, D = x.shape
    E, R = edge_attr_20.shape
    C = W_in2f_s.shape[0]
    KD = D // P
    NB = 10
    NT = N // NB
    HEADS, DH = 8, 64
    X8, OUT = expert_w.shape[0], expert_w.shape[2]
    NI = Ins_tk.shape[1]
    GROUPS = -(-(E + NB * (GROUP - 1)) // GROUP)
    GROUPS = -(-GROUPS // (UNROLL // PPG)) * (UNROLL // PPG)
    PAIRS = GROUPS * PPG
    NCOL = PAIRS * TPG
    FULL = E // P
    REM = E - FULL * P
    RC1 = FULL + 1
    SPARE = NCOL - FULL
    REC = 4 * C + 8
    COLS = 2 * STEP
    FITER = NCOL // COLS
    MITER = PAIRS // UNROLL
    GPB = UNROLL // PPG
    STEPS = 2 * FITER
    MSG = 8 * C
    Y0 = float(1.0 / np.sqrt(4.0 * np.pi))
    assert NB * NT == N and NT <= P and C == P and NCOL % COLS == 0 and REM % 32 == 0 and OUT == D

    rec_dram = nc.dram_tensor("edge_records", [NCOL * P, REC], F32, kind="Internal").ap()
    tab_dram = nc.dram_tensor("node_table", [N, 4 * C], F32, kind="Internal").ap()

    ctx = ExitStack()
    with ctx:
        def sb(name, shape, dt=F32):
            return ctx.enter_context(nc.sbuf_tensor(name, shape, dt))

        def sem(name):
            return ctx.enter_context(nc.semaphore(name))

        def sems(name, n):
            return [sem(f"{name}{k}") for k in range(n)]

        PS = ctx.enter_context(nc.psum_tensor("PS", [P, 8, 512], F32))

        X = sb("X", [P, NB, D])
        ident = sb("ident", [P, P])
        iota_f = sb("iota_f", [P, P])
        ones = sb("ones", [P, 320])
        ltri = sb("ltri", [P, P])
        w1s = sb("w1s", [P, 2, C])
        w1v = sb("w1v", [P, 2, C])
        w2s = sb("w2s", [P, C])
        w2v = sb("w2v", [P, C])
        gate = sb("gate", [P, KD, X8])
        small = sb("small", [P, 640])
        gam8 = small[:, 0:8]
        rgam = small[:, 8:16]
        mean = small[:, 16:26]
        var_eps = small[:, 26:36]
        rstd = small[:, 36:46]
        stats = small[:, 48:108].rearrange("p (t s) -> p t s", s=6)
        aggr = small[:, 108:128].rearrange("p (t s) -> p t s", s=2)
        mxq, mxk = small[:, 128:136], small[:, 136:144]
        smq, smk = small[:, 144:152], small[:, 152:160]
        cnt = small[:, 160:170]
        tot = small[:, 170:180]
        pref = small[:, 180:190]
        ngf = small[:, 190:200]
        endg = small[:, 200:210]
        base = small[:, 210:220]
        off = small[:, 220:230]
        cumt = small[:, 230:240]
        cpad = small[:, 240:250]
        rq, rk = small[:, 250:258], small[:, 258:266]
        mi = small[:, 266:270]
        gcol = small[:, 278:279]
        tie = small[:, 468:532].rearrange("p (a b) -> p a b", b=X8)
        ints = sb("ints", [P, 16], I32)
        goff = sb("goff", [P, GROUPS], I32)
        half = sb("half", [P, 1])
        bb = sb("bb", [P, D])

        we_words = X8 * KD * OUT
        R2 = sb("R2", [P, we_words])
        at = [0]

        def r2(words):
            a = at[0]
            at[0] += words
            assert at[0] <= we_words
            return R2[:, a:a + words]

        Fe = r2(NCOL * R).rearrange("p (c r) -> p c r", r=R)
        meta = r2(NCOL * 8).rearrange("p (c m) -> p c m", m=8)
        rcut = r2(NCOL)
        posi = r2(NCOL).bitcast(I32)
        srci = r2(RC1).bitcast(I32)
        srcf = r2(RC1)
        bkt = r2(RC1)
        rnk = r2(RC1)
        tA, tB = r2(RC1), r2(RC1)
        kd = r2(SPARE)
        pd = r2(SPARE)
        rb_words = UNROLL * TPG * REC
        RB = R2[:, we_words - rb_words:we_words].rearrange("p (s t r) -> p s t r", s=UNROLL, t=TPG)
        we = R2[:, :].rearrange("p (e k n) -> p e k n", e=X8, k=KD)
        sums_words = 2 * 2 * 512
        SG = R2[:, we_words - rb_words - sums_words:we_words - rb_words].rearrange("p (s n) -> p s n", s=2)
        EARLY = (we_words - rb_words - sums_words) // (KD * OUT)

        r1_words = 27400
        r1_base = nc.sbuf_base
        R1 = sb("R1", [P, r1_words])

        def rounded(name, word, shape):
            return nc.alloc_sbuf_tensor_at(name, shape, F32R, offset=r1_base + 4 * word)

        class Carve:

            def __init__(self, start=0):
                self.at = start

            def __call__(self, words):
                a = self.at
                self.at += words
                assert self.at <= r1_words, self.at
                return R1[:, a:a + words]

        c1 = Carve()
        wqkv = c1(3 * KD * D).rearrange("p (w k n) -> p w k n", w=3, k=KD)
        KN = c1(NB * D).rearrange("p (t n) -> p t n", t=NB)
        VN = c1(NB * D).rearrange("p (t n) -> p t n", t=NB)
        QT = c1(KD * NB * NT).rearrange("p (t k n) -> p t k n", t=NB, k=KD)
        wo = c1(KD * D).rearrange("p (k n) -> p k n", k=KD)
        XN = c1(2 * D).rearrange("p (s n) -> p s n", s=2)
        XT = c1(2 * KD * NT).rearrange("p (s k n) -> p s k n", s=2, k=KD)
        TAB = c1(2 * D).rearrange("p (s n) -> p s n", s=2)
        QW = c1(D)
        wsv = c1(2 * C).rearrange("p (w n) -> p w n", w=2)
        MO = wqkv[:, 0, :, :]
        ctxT = wqkv[:, 1, 0, :].rearrange("p (k n) -> p k n", k=KD)
        bo_b = wqkv[:, 2, 0, :]
        bslot = [VN[:, 0:4, :], VN[:, 4:8, :]]
        ins_sb = QW[0:NI, :]
        z_mi = VN[:, 8:9, 0:KD * X8 * X8].rearrange("p o (k e f) -> p (o k) e f", k=KD, e=X8)
        gamT = wsv[:, 0, 0:KD * X8].rearrange("p (k e) -> p k e", k=KD)
        rmod = wsv[:, 0, 32:32 + KD * X8].rearrange("p (k e) -> p k e", k=KD)
        gam_row = XN[0:X8, 0, :]
        mi_bc = KN[:, 0, :].rearrange("p (k n) -> p k n", k=KD)
        be_row = XN[0:X8, 1, :]

        acc_at = r1_words - NB * MSG
        acc = R1[:, acc_at:r1_words]
        c2 = Carve(3 * KD * D)
        ST = c2(COLS * REC).rearrange("p (s r) -> p s r", r=REC)
        fT = c2(2 * 512).rearrange("p (h n) -> p h n", h=2)
        tz = c2(2 * 512).rearrange("p (h n) -> p h n", h=2)
        hT = c2(2 * 512).rearrange("p (h n) -> p h n", h=2)
        Fst = c2(2 * STEP * R).rearrange("p (h c r) -> p h c r", h=2, r=R)
        rcst = c2(2 * STEP).rearrange("p (h c) -> p h c", h=2)
        idxst = c2(COLS).bitcast(I32)
        h_high = rounded("h_high", c2.at, [P, 2, 512])
        h_low = rounded("h_low", c2.at + 1024, [P, 2, 512])
        c2(2048)
        wf2_high = rounded("wf2_high", c2.at, [P, 4, C])
        wf2_low = rounded("wf2_low", c2.at + 4 * C, [P, 4, C])
        c2(8 * C)
        assert c2.at <= acc_at

        c3 = Carve()
        GB = c3(UNROLL * TPG * 4 * C).rearrange("p (s t n) -> p s t n", s=UNROLL, t=TPG)
        MB = c3(2 * TPG * 9 * C).rearrange("p (s t k n) -> p s t k n", s=2, t=TPG, k=9)
        OH = c3(UNROLL * TPG * P).rearrange("p (s t n) -> p s t n", s=UNROLL, t=TPG)
        DT = c3(2 * TPG * 3 * C).rearrange("p (s t k n) -> p s t k n", s=2, t=TPG, k=3)
        assert c3.at <= acc_at

        c4 = Carve()
        AT = c4(2 * 8 * P).rearrange("p (s k n) -> p s k n", s=2, k=8)
        S1 = c4(2 * 4 * P).rearrange("p (s k n) -> p s k n", s=2, k=4)
        sz = c4(2 * P).rearrange("p (s n) -> p s n", s=2)
        XF = c4(2 * D).rearrange("p (s n) -> p s n", s=2)
        prob = c4(NB * X8).rearrange("p (t e) -> p t e", t=NB)
        comb = c4(NB * X8).rearrange("p (t e) -> p t e", t=NB)
        cg = c4(NB * X8).rearrange("p (t e) -> p t e", t=NB)
        rank = c4(NB * X8).rearrange("p (t e) -> p t e", t=NB)
        st1 = c4(16)[:, 0:NB]
        cmp_a = c4(NB * X8 * X8).rearrange("p (t a b) -> p t a b", t=NB, a=X8)
        cmp_b = c4(NB * X8 * X8).rearrange("p (t a b) -> p t a b", t=NB, a=X8)
        comb_t = c4(-(-NB * NT // 8) * 8)[:, 0:NB * NT].rearrange("p (t n) -> p t n", t=NB)
        gate_high = rounded("gate_high", c4.at, [P, KD, X8])
        gate_low = rounded("gate_low", c4.at + KD * X8, [P, KD, X8])
        c4(2 * KD * X8)
        we_high = rounded("expert_w_high", c4.at, [P, 2, KD, OUT])
        we_low = rounded("expert_w_low", c4.at + 2 * KD * OUT, [P, 2, KD, OUT])
        c4(4 * KD * OUT)
        assert c4.at <= acc_at
        xT_high = rounded("xT_high", acc_at, [P, NB, KD, NT])
        xT_low = rounded("xT_low", acc_at + NB * KD * NT, [P, NB, KD, NT])

        wf1 = sb("wf1", [R + 1, P])
        wf2 = sb("wf2", [P, 4, C])
        b2s = sb("b2s", [3, 4, C], BF16)
        ones3 = sb("ones3", [3, P], BF16)
        rraw = KN[:, 0:2, :].rearrange("p t n -> p (t n)")[:, 0:RC1 * 3].rearrange("p (c i) -> p c i", i=3)
        ssq = KN[:, 2, 0:RC1]
        inv = KN[:, 3, 0:RC1]
        rtmp = KN[:, 4:6, :].rearrange("p t n -> p (t n)")[:, 0:RC1 * 3].rearrange("p (c i) -> p c i", i=3)
        dsti = KN[:, 6, 0:RC1].bitcast(I32)
        wf2raw = KN[:, 7, :]
        b2raw = KN[0:3, 8, :]
        b2rem = KN[0:3, 9, :]
        b2p = [VN[0:3, k, 0:256].bitcast(BF16) for k in range(3)]

        consts = sem("constants_ready")
        pool_step = sem("pool_step")
        dve_step = sem("dve_step")
        act_step = sem("act_step")
        x_in = sems("x_in", 2)
        wsv_in, wqkv_in, wo_in = sem("wsv_in"), sems("wqkv_in", 3), sem("wo_in")
        bo_in, ffn_small_in, w12_in = sem("bo_in"), sem("ffn_small_in"), sem("w12_in")
        edge_in, f_in, rcut_in, wf_in, b2_in = sem("edge_in"), sem("f_in"), sem("rcut_in"), sem("wf_in"), sem("b2_in")
        edge_zero = sem("edge_buffers_filled")
        b2_parts = sem("b2_parts_made")
        b2_placed = sem("b2_placed")
        var_ready, std_ready, nrm_sq, nrm_root = sem("var_ready"), sem("std_ready"), sem("norm_sq"), sem("norm_root")
        xn_ready = sem("xn_ready")
        xT_psum, xT_ready = sem("xT_psum"), sem("xT_ready")
        tab_psum, tab_ready, tab_out = sem("table_psum"), sem("table_ready"), sems("table_out", 2)
        q_psum, k_psum, v_psum = sem("q_psum"), sem("k_psum"), sem("v_psum")
        q_shift, k_shift, q_exp, k_exp = sem("q_shifted"), sem("k_shifted"), sem("q_exp"), sem("k_exp")
        q_norm, k_norm, v_ready = sem("q_normal"), sem("k_normal"), sem("v_ready")
        qT_psum, qT_ready = sem("qT_psum"), sem("qT_ready")
        counts_ready, counts_psum = sem("counts_ready"), sem("counts_psum")
        pos_ready = sem("positions_ready")
        ctx_psum, ctx_zero, ctx_ready = sem("context_psum"), sem("context_zeroed"), sem("context_ready")
        mo_psum, mo_ready = sem("context_wo_psum"), sem("context_wo_ready")
        y_psum, mix_added = sem("mix_psum"), sem("mix_added")
        mi_psum, mi_ready, z_ready = sem("ins_mean_psum"), sem("ins_mean_ready"), sem("ins_mean_spread")
        gamT_psum, gamT_ready = sem("gammaT_psum"), sem("gammaT_ready")
        gam_psum = sem("gamma_psum")
        beta_in, beta_used = sems("beta_in", 2), sem("beta_used")
        router_ready = sem("router_ready")
        staged, f_staged = sem("edge_columns_staged"), sem("f_staged")
        f_used = sem("f_transposed")
        fT_ready, z_psum, z_abs, l_ready, h_ready = (sem("fT_ready"), sem("z_psum"), sem("z_abs"), sem("log_ready"),
                                                     sem("h_ready"))
        hh_ready, hl_ready = sem("h_high_ready"), sem("h_low_ready")
        wf2_h, wf2_l = sem("wf2_high_ready"), sem("wf2_low_ready")
        w_psum, w_even, w_odd = sem("filter_psum"), sem("filter_even_ready"), sem("filter_odd_ready")
        e_ready = sem("exp_ready")
        scattered = sems("scattered", COLS)
        indirect_turn = sem("indirect_turn")
        rec_in = sems("record_in", UNROLL)
        gathered = sems("pair_gathered", UNROLL)
        acc_zero = sem("sums_zeroed")
        distance = sem("node_distance")
        dot1, dot2, dot3 = sem("dot_x"), sem("dot_xy"), sem("dot_xyz")
        onehot_even, onehot_odd = sem("onehot_even_ready"), sem("onehot_odd_ready")
        ac_ready, b_ready, d_ready, c_ready = (sem("message_ac"), sem("message_b"), sem("message_d"),
                                               sem("message_c"))
        summed, sums_out, flushed = sem("tile_summed"), sem("group_out_of_psum"), sem("group_added")
        we_early_in = sem("early_expert_w_in")
        we_in = sems("expert_w_in", X8 - EARLY)
        we_split_h, we_split_l = sem("expert_w_high_ready"), sem("expert_w_low_ready")
        gate_h, gate_l = sem("gate_high_ready"), sem("gate_low_ready")
        aT_psum, aT_ready = sem("sumsT_psum"), sem("sumsT_ready")
        sv_psum, s_abs, s_ln, s_ready, v1_ready = (sem("mixed_psum"), sem("s_abs"), sem("s_log"), sem("s_ready"),
                                                   sem("v_mixed_ready"))
        g_psum, x1_ready = sem("gnn_psum"), sem("x1_ready")
        var2_ready, std2_ready = sem("var2_ready"), sem("std2_ready")
        xf_ready, xfT_psum = sem("xf_ready"), sem("xfT_psum")
        xT_h, xT_l = sem("xT_high_ready"), sem("xT_low_ready")
        logit_psum, shift_ready, prob_exp = sem("logit_psum"), sem("logits_shifted"), sem("logits_exp")
        comb_ready, combT_psum, combT_ready, bias_psum = (sem("combine_ready"), sem("combineT_psum"),
                                                          sem("combineT_ready"), sem("expert_bias_psum"))
        eo_psum, eo_used = sem("expert_psum"), sem("expert_used")
        bias_added = sem("expert_bias_added")
        o_out = sem("output_stored")

        block = ctx.enter_context(nc.Block())

        def exists(i, c):
            return not isinstance(i, int) or 2 * i + c < STEPS

        def columns_of(i, c):
            first = (i * 2 + c) * STEP
            return slice(first, first + STEP) if isinstance(i, int) else ds(first, STEP)


        @block.sync
        def _(sp):
            xv = x.rearrange("(t p) d -> p t d", p=NT)
            sp.dma_start(X[0:NT, 0:2, :], xv[:, 0:2, :]).then_inc(x_in[0], 16)
            sp.dma_start(wsv[:, 0, :], W_in2f_s).then_inc(wsv_in, 16)
            sp.dma_start(wsv[:, 1, :], W_in2f_v).then_inc(wsv_in, 16)
            sp.dma_start(X[0:NT, 2:NB, :], xv[:, 2:NB, :]).then_inc(x_in[1], 16)
            for w, (wt, s) in enumerate(zip((Wq, Wk, Wv), wqkv_in)):
                sp.dma_start(wqkv[:, w, 0, :], wt[0:C, :]).then_inc(s, 16)
                sp.dma_start(wqkv[:, w, 1:KD, :], wt[C:D, :].rearrange("(c i) n -> c i n", i=3)).then_inc(s, 16)
            sp.dma_start(wo, Wo.rearrange("(k p) n -> p k n", p=P)).then_inc(wo_in, 16)
            sp.dma_start(w1s[:, :, :], W1_s.rearrange("(f a) c -> f a c", a=2)).then_inc(w12_in, 16)
            sp.dma_start(w1v[:, :, :], W1_v.rearrange("(f a) c -> f a c", a=2)).then_inc(w12_in, 16)
            sp.dma_start(w2s[:, :], W2_s).then_inc(w12_in, 16)
            sp.dma_start(w2v[:, :], W2_v).then_inc(w12_in, 16)
            sp.dma_start(gate[:, :, :], gate_w.rearrange("(k p) e -> p k e", p=P)).then_inc(w12_in, 16)
            for t in range(NB):
                sp.wait_ge(tab_ready, t + 1)
                sp.dma_start(tab_dram[t * NT:(t + 1) * NT, :], TAB[0:NT, t % 2, :]).then_inc(tab_out[t % 2], 16)
            sp.wait_ge(ctx_psum, 1)
            sp.wait_ge(tab_psum, NB)
            sp.wait_ge(qT_psum, NB)
            sp.wait_ge(xT_psum, NB)
            sp.dma_start(bo_b[0:NT, :], bo.rearrange("(o n) -> o n", o=1).to_broadcast([NT, D])).then_inc(bo_in, 16)
            sp.dma_start(ins_sb, Ins_tk[0]).then_inc(ffn_small_in, 16)
            sp.dma_start(gam_row, gamma_w).then_inc(ffn_small_in, 16)
            sp.dma_start(be_row, expert_b).then_inc(ffn_small_in, 16)
            sp.dma_start(rmod, rmod_w.rearrange("(k p) e -> p k e", p=P)).then_inc(ffn_small_in, 16)
            for e in range(X8):
                if e >= 2:
                    sp.wait_ge(beta_used, e - 1)
                sp.dma_start(bslot[e % 2], beta_w[e].rearrange("(k p) n -> p k n", p=P)).then_inc(beta_in[e % 2], 16)

            for j in range(COLS):
                sp.wait_ge(scattered[j], 16 * FITER)
            sp.wait_ge(router_ready, 1)
            sp.wait_ge(mix_added, NB)
            rv = rec_dram.rearrange("(g p t) r -> g p (t r)", p=P, t=TPG)

            def load(i, first):
                for s in range(UNROLL):
                    if not first:
                        sp.wait_ge(onehot_even, upto(i - 1, UNROLL * TPG, s * TPG + 1))
                        sp.wait_ge(onehot_odd, upto(i - 1, UNROLL * TPG, s * TPG + 1))
                        sp.wait_ge(b_ready, upto(i - 1, UNROLL * TPG, s * TPG + 1))
                        sp.wait_ge(d_ready, upto(i - 1, UNROLL * TPG, s * TPG + 1))
                        sp.wait_ge(c_ready, upto(i - 1, UNROLL * TPG, s * TPG + 1))
                        sp.wait_ge(dot1, upto(i - 1, UNROLL * TPG, s * TPG + 1))
                    elif s >= 2:
                        sp.wait_ge(gathered[s - 2], 16 * TPG)
                    g = i * UNROLL + s
                    r = rv[g] if first else rv[ds(g, 1)].rearrange("o p r -> p (o r)")
                    sp.dma_start(RB[:, s, :, :].rearrange("p t r -> p (t r)"), r).then_inc(rec_in[s], 16)

            wv = expert_w.rearrange("e (k p) n -> (e k) p n", p=P)
            wd = we.rearrange("p e k n -> p (e k) n")
            pieces = EARLY * KD
            load(0, True)
            with sp.Fori(1, pieces + 1) as i:
                load(i, False)
                sp.dma_start(wd[:, ds(i - 1, 1), :].rearrange("p o n -> p (o n)"),
                             wv[ds(i - 1, 1)].rearrange("o p n -> p (o n)")).then_inc(we_early_in, 16)
            with sp.Fori(pieces + 1, MITER) as i:
                load(i, False)
            for done in (b_ready, d_ready, c_ready, dot1, onehot_even, onehot_odd):
                sp.wait_ge(done, NCOL)
            sp.wait_ge(flushed, GROUPS)
            for e in range(EARLY, X8):
                sp.dma_start(we[:, e], expert_w[e].rearrange("(k p) n -> p k n", p=P)).then_inc(we_in[e - EARLY], 16)
            for t in range(NB):
                sp.wait_ge(eo_used, (X8 - 1) * NB + t + 1)
                sp.dma_start(out[t * NT:(t + 1) * NT, :], X[0:NT, t, :]).then_inc(o_out, 16)
            sp.wait_ge(o_out, 16 * NB)
            for s in range(2):
                sp.wait_ge(tab_out[s], 16 * (NB // 2))

        @block.gpsimd
        def _(pool):
            steps = [0]

            def step(ins):
                steps[0] += 1
                ins.then_inc(pool_step, 1)
                pool.wait_ge(pool_step, steps[0])

            g = nc.gpsimd
            step(g.memset(ones[:, :], 1.0))
            step(g.memset(ident[:, :], 0.0))
            step(g.affine_select(out=ident[:, :], in_=ident[:, :], compare_op=ALU.not_equal, fill=1.0, base=0,
                                 pattern=[[-1, P]], channel_multiplier=1))
            step(g.affine_select(out=ltri[:, :], in_=ones[:, 0:P], compare_op=ALU.is_gt, fill=0.0, base=0,
                                 pattern=[[1, P]], channel_multiplier=-1))
            g.iota(iota_f[:, :], pattern=[[1, P]], base=0, channel_multiplier=0,
                   allow_small_or_imprecise_dtypes=True).then_inc(consts, 1)
            g.memset(meta[:, :, :], 0.0)
            g.memset(srci[:, :], 0)
            g.memset(dsti[:, :], 0)
            g.memset(rraw[:, :, :], 1.0)
            g.memset(rcut[:, :], 0.0)
            g.memset(Fe[:, FULL:NCOL, :], 0.0).then_inc(edge_zero, 1)
            g.memset(ones3[:, :], 1.0)
            g.affine_select(out=tie, in_=ones[:, 0:X8 * X8].rearrange("p (a b) -> p a b", b=X8), compare_op=ALU.is_gt,
                            fill=0.0, base=0, pattern=[[1, X8], [-1, X8]], channel_multiplier=0)
            g.iota(kd[:, :], pattern=[[P, SPARE]], base=-REM, channel_multiplier=1,
                   allow_small_or_imprecise_dtypes=True)
            g.iota(goff[:, :], pattern=[[1, GROUPS]], base=0, channel_multiplier=0).then_inc(consts, 1)
            pool.wait_ge(edge_zero, 1)
            for dest, values in ((srci, src), (dsti, dst)):
                v = values.rearrange("(n o) -> n o", o=1)
                g.dma_start(dest[:, 0:FULL], values[0:P * FULL].rearrange("(p c) -> p c", p=P)).then_inc(edge_in, 16)
                g.dma_start(dest[0:REM, FULL:RC1], v[P * FULL:E, :]).then_inc(edge_in, 16)
            g.dma_start(rraw[:, 0:FULL, :], edge_attr_3[0:P * FULL, :].rearrange("(p c) i -> p c i", p=P))\
                .then_inc(edge_in, 16)
            g.dma_start(rraw[0:REM, FULL, :], edge_attr_3[P * FULL:E, :]).then_inc(edge_in, 16)
            g.dma_start(rcut[:, 0:FULL], edge_weight[0:P * FULL].rearrange("(p c) -> p c", p=P)).then_inc(rcut_in, 16)
            g.dma_start(rcut[0:REM, FULL:RC1], edge_weight.rearrange("(n o) -> n o", o=1)[P * FULL:E, :])\
                .then_inc(rcut_in, 16)
            g.dma_start(wf2raw, Wf2[:, 0:4 * C]).then_inc(wf_in, 16)
            g.dma_start(b2raw, bf2.rearrange("(o n) -> o n", o=1)[:, 0:4 * C].to_broadcast([3, 4 * C]))\
                .then_inc(b2_in, 16)
            g.dma_start(wf1[0:R, :], Wf1).then_inc(wf_in, 16)
            g.dma_start(wf1[R:R + 1, :], bf1.rearrange("(o n) -> o n", o=1)).then_inc(wf_in, 16)
            g.dma_start(Fe[:, 0:FULL, :], edge_attr_20[0:P * FULL, :].rearrange("(p c) r -> p c r", p=P))\
                .then_inc(f_in, 16)
            g.dma_start(Fe[0:REM, FULL, :], edge_attr_20[P * FULL:E, :]).then_inc(f_in, 16)
            pool.wait_ge(b2_parts, 1)
            for k in range(3):
                g.dma_start(b2s[k:k + 1, :, :].rearrange("p k n -> p (k n)"), b2p[k][k:k + 1, :])\
                    .then_inc(b2_placed, 16)

            pool.wait_ge(mix_added, NB)
            pool.wait_ge(router_ready, 1)
            for s in range(2):
                pool.wait_ge(tab_out[s], 16 * (NB // 2))
            g.memset(acc[:, :], 0.0).then_inc(acc_zero, 1)

            def scatter(i):
                for j in range(COLS):
                    pool.wait_ge(w_odd if j % 2 else w_even, upto(i, COLS // 2, j // 2))
                    pool.wait_ge(staged, upto(i, 2, j // STEP))
                    pool.sem_inc(indirect_turn, 1)
                    g.indirect_dma_start(out=rec_dram, out_offset=bass.IndirectOffsetOnAxis(ap=idxst[:, j:j + 1], axis=0),
                                         in_=ST[:, j, :], in_offset=None).then_inc(scattered[j], 16)

            scatter(0)
            with pool.Fori(1, FITER) as i:
                scatter(i)
            def flush(i, q, static):
                n = i * GPB + q
                word = pool.value_load(goff[0:1, n:n + 1] if static else goff[0:1, ds(n, 1)], min_val=0,
                                       max_val=(NB - 1) * MSG)
                pool.wait_ge(sums_out, upto(i, GPB, q))
                if not static or n:
                    pool.wait_ge(flushed, n)
                dst_ap = acc[0:NT, ds(word, MSG)]
                g.tensor_tensor(dst_ap, dst_ap, SG[0:NT, q % 2, :], ALU.add).then_inc(flushed, 1)

            def gather(i, first):
                for s in range(UNROLL):
                    if s % PPG == 0:
                        if s >= LAG:
                            flush(i, (s - LAG) // PPG, first)
                        elif not first:
                            flush(i - 1, (s + UNROLL - LAG) // PPG, False)
                    pool.wait_ge(rec_in[s], 16 * (i + 1) if first else i * 16 + 16)
                    if not first:
                        pool.wait_ge(b_ready, upto(i - 1, UNROLL * TPG, s * TPG + 1))
                        pool.wait_ge(d_ready, upto(i - 1, UNROLL * TPG, s * TPG + 1))
                    pool.sem_inc(indirect_turn, 1)
                    for t in range(TPG):
                        idx = RB[:, s, t, 4 * C + 4:4 * C + 5].bitcast(I32)
                        g.indirect_dma_start(out=GB[:, s, t, :], out_offset=None, in_=tab_dram,
                                             in_offset=bass.IndirectOffsetOnAxis(ap=idx, axis=0))\
                            .then_inc(gathered[s], 16)

            pool.wait_ge(acc_zero, 1)
            gather(0, True)
            with pool.Fori(1, MITER) as i:
                gather(i, False)
            for q in range((UNROLL - LAG) // PPG, GPB):
                flush(MITER - 1, q, True)

        @block.scalar
        def _(act):
            a = nc.scalar
            act.wait_ge(var_ready, 1)
            a.activation(rstd[0:NT, :], var_eps[0:NT, :], ACT.Sqrt).then_inc(std_ready, 1)
            act.wait_ge(nrm_sq, 1)
            a.activation(inv, ssq, ACT.Sqrt).then_inc(nrm_root, 1)
            a.preload_act_table_set("natural_log_exp_and_others")

            def evac_xT(t):
                act.wait_ge(xT_psum, t + 1)
                if t >= 2:
                    act.wait_ge(v_psum, t - 1)
                a.activation(XT[:, t % 2, :, :].rearrange("p k n -> p (k n)"), PS[:, t % 2, 0:KD * NT], ACT.Copy)\
                    .then_inc(xT_ready, 1)

            evac_xT(0)
            for t in range(NB):
                if t + 1 < NB:
                    evac_xT(t + 1)
                act.wait_ge(tab_psum, t + 1)
                if t >= 2:
                    act.wait_ge(tab_out[t % 2], 16 * (t // 2))
                a.activation(TAB[0:NT, t % 2, :], PS[0:NT, 2, :], ACT.Copy, scale=Y0 / float(np.sqrt(C)))\
                    .then_inc(tab_ready, 1)
                act.wait_ge(q_shift, t + 1)
                a.activation(QW[0:NT, :], QW[0:NT, :], ACT.Exp).then_inc(q_exp, 1)
                act.wait_ge(k_shift, t + 1)
                a.activation(KN[0:NT, t, :], KN[0:NT, t, :], ACT.Exp).then_inc(k_exp, 1)
                act.wait_ge(v_psum, t + 1)
                a.activation(VN[0:NT, t, :], PS[0:NT, 5, :], ACT.Copy).then_inc(v_ready, 1)
                act.wait_ge(qT_psum, t + 1)
                a.activation(QT[:, t, :, :].rearrange("p k n -> p (k n)"), PS[:, 6, 0:KD * NT], ACT.Copy)\
                    .then_inc(qT_ready, 1)
            act.wait_ge(ctx_psum, 1)
            act.wait_ge(ctx_zero, 1)
            for hh in range(2):
                r = slice(hh * DH, (hh + 1) * DH)
                a.activation(ctxT[r, :, hh * DH:(hh + 1) * DH],
                             PS[r, 0, :].rearrange("p (k n) -> p k n", k=KD)[:, :, hh * DH:(hh + 1) * DH], ACT.Copy)\
                    .then_inc(ctx_ready, 1)
            for k in range(KD):
                act.wait_ge(mo_psum, k + 1)
                a.activation(MO[:, k, :], PS[:, 1 + k % 2, :], ACT.Copy).then_inc(mo_ready, 1)

            act.wait_ge(mix_added, NB)
            act.wait_ge(router_ready, 1)
            a.activation(fT[0:32, :, :].rearrange("p h n -> p (h n)"),
                         ones[0:32, 0:1].to_broadcast([32, 2 * 512]), ACT.Copy).then_inc(act_step, 1)
            act.wait_ge(act_step, 1)

            a.activation(wf2_high[:, :, :], wf2[:, :, :], ACT.Copy).then_inc(wf2_h, 1)

            def radial(i, c):
                m = i * 2 + c
                act.wait_ge(f_used, m + 1)
                if real(m - 1):
                    act.wait_ge(z_psum, m - 1)
                a.activation(fT[0:R, c % 2, :], PS[0:R, 0, :], ACT.Copy).then_inc(fT_ready, 1)

            def log_part(i, c):
                m = i * 2 + c
                h = c % 2
                act.wait_ge(z_psum, m + 1)
                if real(m - 1):
                    act.wait_ge(h_ready, m - 1)
                a.activation(tz[:, h, :], PS[:, 1 + h, :], ACT.Abs).then_inc(z_abs, 1)
                act.wait_ge(z_abs, m + 1)
                a.activation(tz[:, h, :], tz[:, h, :], ACT.Exp, scale=-1.0).then_inc(e_ready, 1)
                act.wait_ge(e_ready, m + 1)
                a.activation(tz[:, h, :], tz[:, h, :], ACT.Ln, bias=half[:, 0:1], scale=0.5).then_inc(l_ready, 1)

            def high(i, c):
                m = i * 2 + c
                act.wait_ge(h_ready, m + 1)
                if real((m - 1) * STEP):
                    act.wait_ge(w_psum, (m - 1) * STEP)
                a.activation(h_high[:, c % 2, :], hT[:, c % 2, :], ACT.Copy).then_inc(hh_ready, 1)

            def even(i, c, j):
                m = i * 2 + c
                act.wait_ge(w_psum, m * STEP + j + 1)
                act.wait_ge(staged, m + 1)
                a.activation(ST[:, c % 2 * STEP + j, 0:4 * C], PS[:, 3 + j, :], ACT.Copy,
                             scale=rcst[:, c % 2, j:j + 1]).then_inc(w_even, 1)

            def filters(i):
                for h in range(2):
                    if exists(i, h + 1):
                        high(i, h + 1)
                    even(i, h, 0)
                    if exists(i, h + 2):
                        log_part(i, h + 2)
                    if exists(i, h + 3):
                        radial(i, h + 3)
                    even(i, h, 2)

            radial(0, 0)
            radial(0, 1)
            log_part(0, 0)
            radial(0, 2)
            log_part(0, 1)
            high(0, 0)
            filters(0)
            with act.Fori(1, FITER - 2) as i:
                filters(i)
            filters(FITER - 2)
            filters(FITER - 1)

            per = UNROLL * TPG

            def x_terms(i, s, first):
                for t in range(TPG):
                    act.wait_ge(gathered[s], i * (16 * TPG) + 16 * TPG)
                    if s >= 2:
                        act.wait_ge(b_ready, upto(i, per, (s - 2) * TPG + t))
                    elif not first:
                        act.wait_ge(b_ready, upto(i - 1, per, (s + UNROLL - 2) * TPG + t))
                    a.activation(DT[:, s % 2, t, 0, :], GB[:, s, t, C:2 * C], ACT.Copy,
                                 scale=RB[:, s, t, 4 * C:4 * C + 1]).then_inc(dot1, 1)

            def onehot(i, s, first):
                if not first:
                    act.wait_ge(summed, upto(i - 1, per, s * TPG))
                a.activation(OH[:, s, 0, 0:NT], iota_f[:, 0:NT], ACT.Abs,
                             bias=RB[:, s, 0, 4 * C + 3:4 * C + 4]).then_inc(distance, 1)
                act.wait_ge(distance, upto(i, UNROLL, s))
                a.activation(OH[:, s, 0, 0:NT], OH[:, s, 0, 0:NT], ACT.Relu, bias=ones[:, 0:1], scale=-1.0)\
                    .then_inc(onehot_even, TPG)

            def c_messages(i, s):
                for t in range(TPG):
                    act.wait_ge(ac_ready, upto(i, per, s * TPG + t))
                    for k in range(3):
                        last = a.activation(MB[:, s % 2, t, 2 + k, :], MB[:, s % 2, t, 8, :], ACT.Copy,
                                            scale=RB[:, s, t, 4 * C + k:4 * C + k + 1])
                    last.then_inc(c_ready, 1)

            def sums_from_psum(i, q, first):
                act.wait_ge(summed, upto(i, per, (q + 1) * PPG * TPG - 1))
                if q >= 2 or not first:
                    act.wait_ge(flushed, i * GPB + q - 1)
                a.activation(SG[0:NT, q % 2, :], PS[0:NT, 2 * q:2 * q + 2, :].rearrange("p b n -> p (b n)"),
                             ACT.Copy).then_inc(sums_out, 1)

            def scalar_messages(i, first, last):
                for s in range(UNROLL):
                    if s + 1 < UNROLL:
                        x_terms(i, s + 1, first)
                    elif not last:
                        x_terms(i + 1, 0, False)
                    if s % PPG:
                        if s > 1:
                            sums_from_psum(i, s // PPG - 1, first)
                        elif not first:
                            sums_from_psum(i - 1, GPB - 1, False)
                    onehot(i, s, first)
                    c_messages(i, s)

            x_terms(0, 0, True)
            scalar_messages(0, True, False)
            with act.Fori(1, MITER - 1) as i:
                scalar_messages(i, False, False)
            scalar_messages(MITER - 1, False, True)
            sums_from_psum(MITER - 1, GPB - 1, False)

            def evac_sums(t):
                act.wait_ge(aT_psum, t + 1)
                if t >= 2:
                    act.wait_ge(sv_psum, t - 1)
                for b in range(2):
                    last = a.activation(AT[:, t % 2, 4 * b:4 * b + 4, 0:NT],
                                        PS[:, 4 * (t % 2) + b, 0:4 * NT].rearrange("p (k n) -> p k n", n=NT), ACT.Copy)
                last.then_inc(aT_ready, 1)

            def ssp_part(t):
                h = t % 2
                act.wait_ge(sv_psum, t + 1)
                if t >= 2:
                    act.wait_ge(g_psum, t - 1)
                a.activation(sz[:, h, 0:NT], PS[:, 4 * h + 2, 0:NT], ACT.Abs).then_inc(s_abs, 1)
                a.activation(S1[:, h, 1:4, 0:NT], PS[:, 4 * h + 2, NT:4 * NT].rearrange("p (k n) -> p k n", n=NT),
                             ACT.Copy).then_inc(v1_ready, 1)
                act.wait_ge(s_abs, 2 * t + 1)
                a.activation(sz[:, h, 0:NT], sz[:, h, 0:NT], ACT.Exp, scale=-1.0).then_inc(s_abs, 1)
                act.wait_ge(s_abs, 2 * t + 2)
                a.activation(sz[:, h, 0:NT], sz[:, h, 0:NT], ACT.Ln, bias=half[:, 0:1], scale=0.5).then_inc(s_ln, 1)

            act.wait_ge(summed, NCOL)
            evac_sums(0)
            for t in range(NB):
                if t + 1 < NB:
                    evac_sums(t + 1)
                ssp_part(t)
            act.wait_ge(var2_ready, 1)
            a.activation(rstd[0:NT, :], var_eps[0:NT, :], ACT.Sqrt).then_inc(std2_ready, 1)
            a.activation(gate_high[:, :, :], gate[:, :, :], ACT.Copy).then_inc(gate_h, 1)
            for t in range(NB):
                act.wait_ge(xfT_psum, t + 1)
                a.activation(xT_high[:, t, :, :], PS[:, t % 2, 0:KD * NT].rearrange("p (k n) -> p k n", k=KD),
                             ACT.Copy).then_inc(xT_h, 1)

            def split_high(e):
                if e < EARLY:
                    act.wait_ge(we_early_in, 16 * EARLY * KD)
                else:
                    act.wait_ge(we_in[e - EARLY], 16)
                if e >= 2:
                    act.wait_ge(eo_psum, (e - 1) * NB)
                a.activation(we_high[:, e % 2, :, :], we[:, e, :, :], ACT.Copy).then_inc(we_split_h, 1)

            split_high(0)
            act.wait_ge(shift_ready, 1)
            a.activation(prob[0:NT], prob[0:NT], ACT.Exp).then_inc(prob_exp, 1)
            split_high(1)
            for g in range(3):
                act.wait_ge(combT_psum, g + 1)
                n = min(4, NB - 4 * g)
                a.activation(comb_t[0:X8, 4 * g:4 * g + n, :],
                             PS[0:X8, (0, 1, 3)[g], 0:n * NT].rearrange("p (t n) -> p t n", t=n),
                             ACT.Copy).then_inc(combT_ready, 1)
            for e in range(2, X8):
                split_high(e)

        @block.vector
        def _(dve):
            v = nc.vector
            steps = [0]

            def step(ins):
                steps[0] += 1
                ins.then_inc(dve_step, 1)
                dve.wait_ge(dve_step, steps[0])

            dve.wait_ge(x_in[0], 16)
            for t in range(NB):
                if t == 2:
                    dve.wait_ge(x_in[1], 16)
                last = v.bn_stats(stats[0:NT, t, :], X[0:NT, t, :])
            step(last)
            for t in range(NB):
                last = v.bn_aggr(aggr[0:NT, t, :], stats[0:NT, t, :])
            step(last)
            v.tensor_scalar(var_eps[0:NT, :], aggr[0:NT, :, 1], EPS, None, ALU.add).then_inc(var_ready, 1)
            step(v.memset(half[:, :], 0.5))
            step(v.tensor_copy(mean[0:NT, :], aggr[0:NT, :, 0]))
            dve.wait_ge(std_ready, 1)
            step(v.reciprocal(rstd[0:NT, :], rstd[0:NT, :]))

            def normal(t):
                if t >= 2:
                    dve.wait_ge(xT_psum, t - 1)
                v.tensor_scalar(XN[0:NT, t % 2, :], X[0:NT, t, :], mean[0:NT, t:t + 1], rstd[0:NT, t:t + 1],
                                ALU.subtract, ALU.mult).then_inc(xn_ready, 1)

            normal(0)
            normal(1)
            dve.wait_ge(consts, 2)
            dve.wait_ge(edge_in, 16 * 6)
            step(v.tensor_tensor(rtmp, rraw, rraw, ALU.mult))
            step(v.tensor_tensor(ssq, rtmp[:, :, 0], rtmp[:, :, 1], ALU.add))
            v.tensor_tensor(ssq, ssq, rtmp[:, :, 2], ALU.add).then_inc(nrm_sq, 1)
            step(v.tensor_copy(meta[:, 0:RC1, 4].bitcast(I32), dsti))
            dve.wait_ge(b2_in, 16)
            dve.wait_ge(wf_in, 48)
            w4 = wf2raw.rearrange("p (g f a) -> p g a f", g=2, a=2)
            r4 = b2raw.rearrange("p (g f a) -> p g a f", g=2, a=2)
            step(v.tensor_copy(wf2[:, :, :].rearrange("p (g a) f -> p g a f", g=2), w4))
            step(v.tensor_copy(b2rem.rearrange("p (g a f) -> p g a f", g=2, a=2), r4))
            step(v.tensor_scalar(wf2[:, 2, :], wf2[:, 2, :], float(np.sqrt(3.0)), None, ALU.mult))
            step(v.tensor_scalar(b2rem[:, 2 * C:3 * C], b2rem[:, 2 * C:3 * C], float(np.sqrt(3.0)), None, ALU.mult))
            for k in range(3):
                last = v.tensor_copy(b2p[k], b2rem)
                if k < 2:
                    step(last)
                    step(v.tensor_tensor(b2rem, b2rem, b2p[k], ALU.subtract))
            last.then_inc(b2_parts, 1)
            dve.wait_ge(nrm_root, 1)
            step(v.reciprocal(inv, inv))
            step(v.tensor_tensor(meta[:, 0:RC1, 0:3], rraw, inv.unsqueeze(2).to_broadcast([P, RC1, 3]), ALU.mult))
            step(v.tensor_copy(srcf, srci))
            step(v.memset(srcf[REM:P, FULL:RC1], 1e6))
            step(v.tensor_scalar(bkt, srcf, float(NT), None, ALU.is_ge))
            for b in range(2, NB + 1):
                step(v.scalar_tensor_tensor(bkt, srcf, float(b * NT), bkt, ALU.is_ge, ALU.add))
            v.scalar_tensor_tensor(meta[:, 0:RC1, 3], bkt, float(NT), srcf, ALU.mult, ALU.subtract)
            step(v.memset(rnk, 0.0))

            def shift(bank, dst, mx, psum_ready, t, signal):
                dve.wait_ge(psum_ready, t + 1)
                src3 = PS[0:NT, bank, :].rearrange("p (h d) -> p h d", h=HEADS)
                step(v.reduce_max(mx[0:NT, :], src3, AX_X))
                v.tensor_tensor(dst.rearrange("p (h d) -> p h d", h=HEADS), src3,
                                mx[0:NT, :].unsqueeze(2).to_broadcast([NT, HEADS, DH]), ALU.subtract)\
                    .then_inc(signal, 1)

            def normalise(dst, sm, exp_ready, t, signal):
                dve.wait_ge(exp_ready, t + 1)
                d3 = dst.rearrange("p (h d) -> p h d", h=HEADS)
                step(v.reduce_sum(sm[0:NT, :], d3, AX_X))
                step(v.reciprocal(sm[0:NT, :], sm[0:NT, :]))
                v.tensor_tensor(d3, d3, sm[0:NT, :].unsqueeze(2).to_broadcast([NT, HEADS, DH]), ALU.mult)\
                    .then_inc(signal, 1)

            for t in range(NB):
                if t + 2 < NB:
                    normal(t + 2)
                if t == 0:
                    dve.wait_ge(b2_placed, 48)
                else:
                    dve.wait_ge(qT_psum, t)
                shift(3, QW[0:NT, :], mxq, q_psum, t, q_shift)
                shift(4, KN[0:NT, t, :], mxk, k_psum, t, k_shift)
                normalise(QW[0:NT, :], smq, q_exp, t, q_norm)
                normalise(KN[0:NT, t, :], smk, k_exp, t, k_norm)
                step(v.tensor_scalar(tA, bkt, float(t), None, ALU.is_equal))
                step(v.tensor_tensor_scan(tB, ones[:, 0:RC1], tA, 0.0, ALU.mult, ALU.add))
                v.tensor_copy(cnt[:, t:t + 1], tB[:, RC1 - 1:RC1]).then_inc(counts_ready, 1)
                step(v.tensor_tensor(tA, tA, tB, ALU.mult))
                step(v.tensor_tensor(rnk, rnk, tA, ALU.add))
            dve.wait_ge(k_psum, NB)
            v.memset(ctxT[:, :, :].rearrange("p k n -> p (k n)"), 0.0).then_inc(ctx_zero, 1)
            dve.wait_ge(counts_psum, 1)
            step(v.tensor_copy(pref, PS[:, 7, 0:NB]))
            step(v.tensor_copy(tot, PS[:, 7, NB:2 * NB]))
            step(v.tensor_scalar(ints[:, 0:NB], tot, float(GROUP - 1), None, ALU.add))
            step(v.tensor_scalar(ints[:, 0:NB], ints[:, 0:NB], GROUP.bit_length() - 1, None, ALU.arith_shift_right))
            step(v.tensor_copy(ngf, ints[:, 0:NB]))
            step(v.tensor_tensor_scan(endg, ones[:, 0:NB], ngf, 0.0, ALU.mult, ALU.add))
            step(v.tensor_tensor_scan(cumt, ones[:, 0:NB], tot, 0.0, ALU.mult, ALU.add))
            step(v.tensor_tensor(base, endg, ngf, ALU.subtract))
            step(v.tensor_scalar(base, base, float(GROUP), None, ALU.mult))
            step(v.scalar_tensor_tensor(off, pref, -1.0, base, ALU.add, ALU.add))
            step(v.tensor_tensor(cpad, base, cumt, ALU.subtract))
            step(v.tensor_tensor(cpad, cpad, tot, ALU.add))
            step(v.tensor_copy(pd, kd))
            for b in range(NB):
                step(v.tensor_scalar(tA, bkt, float(b), off[:, b:b + 1], ALU.is_equal, ALU.mult))
                step(v.tensor_tensor(rnk, rnk, tA, ALU.add))
                step(v.tensor_scalar(tB[:, 0:SPARE], kd, cpad[:, b:b + 1], tot[:, b:b + 1], ALU.is_ge, ALU.mult))
                step(v.tensor_tensor(pd, pd, tB[:, 0:SPARE], ALU.add))
            step(v.tensor_copy(posi[:, 0:RC1], rnk))
            step(v.tensor_copy(posi[:, RC1:NCOL], pd[:, 1:SPARE]))
            step(v.tensor_copy(posi[REM:P, FULL:RC1], pd[REM:P, 0:1]))
            step(v.tensor_copy(tA[:, 0:GROUPS], goff[:, :]))
            step(v.tensor_scalar(tB[:, 0:GROUPS], tA[:, 0:GROUPS], endg[:, 0:1], None, ALU.is_ge))
            for b in range(1, NB - 1):
                step(v.scalar_tensor_tensor(tB[:, 0:GROUPS], tA[:, 0:GROUPS], endg[:, b:b + 1], tB[:, 0:GROUPS],
                                            ALU.is_ge, ALU.add))
            step(v.tensor_scalar(goff[:, :], tB[:, 0:GROUPS], float(MSG), None, ALU.mult))
            dve.wait_ge(w12_in, 16 * 5)
            v.tensor_scalar(w1s[:, :, :], w1s[:, :, :], float(1 / np.sqrt(2 * C)), None, ALU.mult)
            v.tensor_scalar(w1v[:, :, :], w1v[:, :, :], float(1 / np.sqrt(2 * C)), None, ALU.mult)
            v.tensor_scalar(w2s[:, :], w2s[:, :], float(1 / np.sqrt(C)), None, ALU.mult)
            v.tensor_scalar(w2v[:, :], w2v[:, :], float(1 / np.sqrt(C)), None, ALU.mult)
            dve.wait_ge(bo_in, 16)
            step(v.tensor_tensor(X[0:NT, :, :], X[0:NT, :, :],
                                 bo_b[0:NT, :].unsqueeze(1).to_broadcast([NT, NB, D]), ALU.add))
            for t in range(NB):
                dve.wait_ge(y_psum, t + 1)
                v.tensor_tensor(X[0:NT, t, :], X[0:NT, t, :], PS[0:NT, 3 + t % 2, :], ALU.add).then_inc(mix_added, 1)
            dve.wait_ge(mi_psum, 1)
            step(v.tensor_scalar(mi, PS[:, 5, 0:KD], 1.0 / NI, None, ALU.mult))
            step(v.memset(z_mi, 0.0))
            for e in range(X8):
                v.tensor_copy(z_mi[:, :, e, e], mi)
            v.tensor_copy(mi_bc, mi.unsqueeze(2).to_broadcast([P, KD, P])).then_inc(z_ready, 1)
            dve.wait_ge(gamT_psum, 1)
            v.tensor_copy(gamT, PS[:, 0, 0:KD * X8].rearrange("p (k e) -> p k e", k=KD)).then_inc(gamT_ready, 1)
            dve.wait_ge(gam_psum, 1)
            v.tensor_copy(gam8, PS[:, 6, 0:X8])
            v.tensor_copy(rgam, PS[:, 6, 8:8 + X8])
            step(v.tensor_copy(gcol[0:X8, :], PS[0:X8, 6, 16:17]))
            dve.wait_ge(beta_used, X8)
            v.scalar_tensor_tensor(bb[0:X8, :], be_row, gcol[0:X8, :], PS[0:X8, 7, :], ALU.mult, ALU.add)\
                .then_inc(router_ready, 1)
            dve.wait_ge(router_ready, 1)
            dve.wait_ge(f_in, 32)
            dve.wait_ge(rcut_in, 32)

            dve.wait_ge(wf2_h, 1)
            v.tensor_tensor(wf2_low[:, :, :], wf2[:, :, :], wf2_high[:, :, :].bitcast(F32), ALU.subtract)\
                .then_inc(wf2_l, 1)

            def stage_f(i, c):
                m = i * 2 + c
                if real(m - 1):
                    dve.wait_ge(f_used, m - 1)
                v.tensor_copy(Fst[:, c % 2, :, :], Fe[:, columns_of(i, c), :]).then_inc(f_staged, 1)

            def stage(i, h):
                cols = columns_of(i, h)
                if real(i):
                    for j in range(h * STEP, (h + 1) * STEP):
                        dve.wait_ge(scattered[j], i * 16)
                v.tensor_copy(rcst[:, h, :], rcut[:, cols])
                v.tensor_copy(ST[:, h * STEP:(h + 1) * STEP, 4 * C:REC], meta[:, cols, :])
                v.tensor_copy(idxst[:, h * STEP:(h + 1) * STEP], posi[:, cols]).then_inc(staged, 1)

            def hidden(i, c):
                m = i * 2 + c
                h = c % 2
                dve.wait_ge(l_ready, m + 1)
                if real(m - 1):
                    dve.wait_ge(hh_ready, m - 1)
                    dve.wait_ge(hl_ready, m - 1)
                v.scalar_tensor_tensor(hT[:, h, :], PS[:, 1 + h, :], 0.0, tz[:, h, :], ALU.max, ALU.add)\
                    .then_inc(h_ready, 1)

            def low(i, c):
                m = i * 2 + c
                h = c % 2
                dve.wait_ge(hh_ready, m + 1)
                if real((m - 1) * STEP):
                    dve.wait_ge(w_psum, (m - 1) * STEP)
                v.tensor_tensor(h_low[:, h, :], hT[:, h, :], h_high[:, h, :].bitcast(F32), ALU.subtract)\
                    .then_inc(hl_ready, 1)

            def odd(i, c, j):
                m = i * 2 + c
                dve.wait_ge(w_psum, m * STEP + j + 1)
                dve.wait_ge(staged, m + 1)
                v.tensor_scalar(ST[:, c % 2 * STEP + j, 0:4 * C], PS[:, 3 + j, :],
                                rcst[:, c % 2, j:j + 1], None, ALU.mult).then_inc(w_odd, 1)

            def filters(i):
                for h in range(2):
                    stage(i, h)
                    if exists(i, h + 1):
                        low(i, h + 1)
                    odd(i, h, 1)
                    if exists(i, h + 2):
                        hidden(i, h + 2)
                    if exists(i, h + 4):
                        stage_f(i, h + 4)
                    odd(i, h, 3)

            for m in range(4):
                stage_f(0, m)
            hidden(0, 0)
            hidden(0, 1)
            low(0, 0)
            filters(0)
            with dve.Fori(1, FITER - 2) as i:
                filters(i)
            filters(FITER - 2)
            filters(FITER - 1)

            def messages(i, first):
                per = UNROLL * TPG
                for s in range(UNROLL):
                    dve.wait_ge(rec_in[s], i * 16 + 16)
                    w4 = [RB[:, s, t, 0:4 * C].rearrange("p (k n) -> p k n", k=4) for t in range(TPG)]
                    for t in range(TPG):
                        if s >= 2:
                            dve.wait_ge(summed, upto(i, per, (s - 2) * TPG + t))
                        elif not first:
                            dve.wait_ge(summed, upto(i - 1, per, (s + UNROLL - 2) * TPG + t))
                        dve.wait_ge(gathered[s], i * (16 * TPG) + 16 * TPG)
                        v.tensor_tensor(MB[:, s % 2, t, 0:9:8, :], w4[t][:, 0:3:2, :],
                                        GB[:, s, t, 0:C].unsqueeze(1).to_broadcast([P, 2, C]), ALU.mult)\
                            .then_inc(ac_ready, 1)
                    for k, (have, done) in enumerate(((dot1, dot2), (dot2, dot3))):
                        for t in range(TPG):
                            dve.wait_ge(have, upto(i, per, s * TPG + t))
                            v.scalar_tensor_tensor(DT[:, s % 2, t, k + 1, :], GB[:, s, t, (k + 2) * C:(k + 3) * C],
                                                   RB[:, s, t, 4 * C + k + 1:4 * C + k + 2], DT[:, s % 2, t, k, :],
                                                   ALU.mult, ALU.add).then_inc(done, 1)
                    for t in range(TPG):
                        v.tensor_tensor(MB[:, s % 2, t, 5:8, :],
                                        GB[:, s, t, C:4 * C].rearrange("p (k n) -> p k n", k=3),
                                        w4[t][:, 3:4, :].to_broadcast([P, 3, C]), ALU.mult).then_inc(d_ready, 1)
                    if not first:
                        dve.wait_ge(summed, upto(i - 1, per, s * TPG + 1))
                    v.tensor_scalar(OH[:, s, 1, 0:NT], iota_f[:, 0:NT], RB[:, s, 1, 4 * C + 3:4 * C + 4], 0.0,
                                    ALU.add, ALU.is_equal).then_inc(onehot_odd, TPG)
                    for t in range(TPG):
                        dve.wait_ge(dot3, upto(i, per, s * TPG + t))
                        v.tensor_tensor(MB[:, s % 2, t, 1, :], DT[:, s % 2, t, 2, :], RB[:, s, t, C:2 * C], ALU.mult)\
                            .then_inc(b_ready, 1)
            for j in range(COLS):
                dve.wait_ge(scattered[j], 16 * FITER)
            messages(0, True)
            with dve.Fori(1, MITER) as i:
                messages(i, False)

            def activate(t):
                dve.wait_ge(s_ln, t + 1)
                dve.wait_ge(v1_ready, t + 1)
                v.scalar_tensor_tensor(S1[:, t % 2, 0, 0:NT], PS[:, 4 * (t % 2) + 2, 0:NT], 0.0, sz[:, t % 2, 0:NT],
                                       ALU.max, ALU.add).then_inc(s_ready, 1)

            activate(0)
            for t in range(NB):
                if t + 1 < NB:
                    activate(t + 1)
                gnn = PS[0:NT, 4 * (t % 2) + 3, :]
                dve.wait_ge(g_psum, t + 1)
                v.tensor_tensor(X[0:NT, t, 0:C], X[0:NT, t, 0:C], gnn[:, 0:C], ALU.add)
                xi = X[0:NT, t, C:D].rearrange("p (c i) -> p c i", i=3)
                step(v.tensor_tensor(xi, xi, gnn[:, C:D].rearrange("p (i c) -> p c i", i=3), ALU.add))
                step(v.bn_stats(stats[0:NT, t, :], X[0:NT, t, :]))
                v.bn_aggr(aggr[0:NT, t, :], stats[0:NT, t, :]).then_inc(x1_ready, 1)
            dve.wait_ge(x1_ready, NB)
            v.tensor_scalar(var_eps[0:NT, :], aggr[0:NT, :, 1], EPS, None, ALU.add).then_inc(var2_ready, 1)
            step(v.tensor_copy(mean[0:NT, :], aggr[0:NT, :, 0]))
            dve.wait_ge(std2_ready, 1)
            step(v.reciprocal(rstd[0:NT, :], rstd[0:NT, :]))

            def normal2(t):
                if t >= 2:
                    dve.wait_ge(xfT_psum, t - 1)
                v.tensor_scalar(XF[0:NT, t % 2, :], X[0:NT, t, :], mean[0:NT, t:t + 1], rstd[0:NT, t:t + 1],
                                ALU.subtract, ALU.mult).then_inc(xf_ready, 1)

            def split_low(e):
                dve.wait_ge(we_split_h, e + 1)
                if e >= 2:
                    dve.wait_ge(eo_psum, (e - 1) * NB)
                v.tensor_tensor(we_low[:, e % 2, :, :], we[:, e, :, :], we_high[:, e % 2, :, :].bitcast(F32),
                                ALU.subtract).then_inc(we_split_l, 1)

            normal2(0)
            normal2(1)
            dve.wait_ge(gate_h, 1)
            v.tensor_tensor(gate_low[:, :, :], gate[:, :, :], gate_high[:, :, :].bitcast(F32), ALU.subtract)\
                .then_inc(gate_l, 1)
            for t in range(NB):
                dve.wait_ge(xT_h, t + 1)
                v.tensor_tensor(xT_low[:, t, :, :], PS[:, t % 2, 0:KD * NT].rearrange("p (k n) -> p k n", k=KD),
                                xT_high[:, t, :, :].bitcast(F32), ALU.subtract).then_inc(xT_l, 1)
                if t + 2 < NB:
                    normal2(t + 2)
            split_low(0)
            dve.wait_ge(logit_psum, NB)
            logits = PS[0:NT, 2, 0:NB * X8].rearrange("p (t e) -> p t e", t=NB)
            over_e = st1[0:NT, :].unsqueeze(2).to_broadcast([NT, NB, X8])
            step(v.tensor_tensor(prob[0:NT], logits, rgam[0:NT, :].unsqueeze(1).to_broadcast([NT, NB, X8]), ALU.add))
            step(v.reduce_max(st1[0:NT, :], prob[0:NT], AX_X))
            v.tensor_tensor(prob[0:NT], prob[0:NT], over_e, ALU.subtract).then_inc(shift_ready, 1)
            dve.wait_ge(prob_exp, 1)
            step(v.reduce_sum(st1[0:NT, :], prob[0:NT], AX_X))
            step(v.reciprocal(st1[0:NT, :], st1[0:NT, :]))
            step(v.tensor_tensor(prob[0:NT], prob[0:NT], over_e, ALU.mult))
            mine = prob[0:NT].unsqueeze(3).to_broadcast([NT, NB, X8, X8])
            others = prob[0:NT].unsqueeze(2).to_broadcast([NT, NB, X8, X8])
            step(v.tensor_tensor(cmp_a[0:NT], others, mine, ALU.is_gt))
            step(v.tensor_tensor(cmp_b[0:NT], others, mine, ALU.is_equal))
            step(v.tensor_tensor(cmp_b[0:NT], cmp_b[0:NT],
                                 tie[0:NT].unsqueeze(1).to_broadcast([NT, NB, X8, X8]), ALU.mult))
            step(v.tensor_tensor(cmp_a[0:NT], cmp_a[0:NT], cmp_b[0:NT], ALU.add))
            step(v.reduce_sum(rank[0:NT], cmp_a[0:NT], AX_X))
            v.scalar_tensor_tensor(comb[0:NT], rank[0:NT], 2.0, prob[0:NT], ALU.is_lt, ALU.mult)\
                .then_inc(comb_ready, 1)
            dve.wait_ge(comb_ready, 1)
            step(v.tensor_tensor(cg[0:NT], comb[0:NT], gam8[0:NT, :].unsqueeze(1).to_broadcast([NT, NB, X8]),
                                 ALU.mult))
            split_low(1)
            for e in range(X8):
                for t in range(NB):
                    n = e * NB + t
                    dve.wait_ge(eo_psum, n + 1)
                    if e == 2:
                        dve.wait_ge(bias_added, t + 1)
                    elif e:
                        dve.wait_ge(eo_used, n - NB + 1)
                    last = v.scalar_tensor_tensor(X[0:NT, t, :], PS[0:NT, 4 + n % 4, :], cg[0:NT, t, e:e + 1],
                                                  X[0:NT, t, :], ALU.mult, ALU.add)
                    last.then_inc(eo_used, 1)
                    if e == 1:
                        dve.wait_ge(bias_psum, t + 1)
                        dve.wait_ge(eo_used, n + 1)
                        v.tensor_tensor(X[0:NT, t, :], X[0:NT, t, :], PS[0:NT, t % 2, :], ALU.add)\
                            .then_inc(bias_added, 1)
                    if t == 2 and 1 <= e < X8 - 1:
                        split_low(e + 1)

        @block.tensor
        def _(pe):
            te = nc.tensor
            idn = ident[0:NT, 0:NT]
            pe.wait_ge(consts, 1)

            def transpose_x(t):
                pe.wait_ge(xn_ready, t + 1)
                if t >= 2:
                    pe.wait_ge(xT_ready, t - 1)
                for k in range(KD):
                    src_ap = XN[0:NT, t % 2, 0:C] if k == 0 else XN[0:NT, t % 2, C + k - 1:D:3]
                    last = te.transpose(PS[:, t % 2, k * NT:(k + 1) * NT], src_ap, idn)
                last.then_inc(xT_psum, 1)

            transpose_x(0)
            for t in range(NB):
                if t + 1 < NB:
                    transpose_x(t + 1)
                pe.wait_ge(xT_ready, t + 1)
                if t == 0:
                    pe.wait_ge(wsv_in, 32)
                else:
                    pe.wait_ge(tab_ready, t)
                for k in range(KD):
                    last = te.matmul(PS[0:NT, 2, k * C:(k + 1) * C], XT[:, t % 2, k, :], wsv[:, min(k, 1), :],
                                     start=True, stop=True)
                last.then_inc(tab_psum, 1)
                for w, (ready, free) in enumerate(((q_psum, q_shift), (k_psum, k_shift), (v_psum, v_ready))):
                    if t == 0:
                        pe.wait_ge(wqkv_in[w], 32)
                    else:
                        pe.wait_ge(free, t)
                    for k in range(KD):
                        last = te.matmul(PS[0:NT, 3 + w, :], XT[:, t % 2, k, :], wqkv[:, w, k, :],
                                         start=(k == 0), stop=(k == KD - 1))
                    last.then_inc(ready, 1)
                pe.wait_ge(q_norm, t + 1)
                if t:
                    pe.wait_ge(qT_ready, t)
                for k in range(KD):
                    last = te.transpose(PS[:, 6, k * NT:(k + 1) * NT], QW[0:NT, k * P:(k + 1) * P], idn)
                last.then_inc(qT_psum, 1)
            pe.wait_ge(k_norm, NB)
            pe.wait_ge(v_ready, NB)
            for k in range(KD):
                for t in range(NB):
                    last = te.matmul(PS[:, 0, k * P:(k + 1) * P], VN[0:NT, t, k * P:(k + 1) * P],
                                     KN[0:NT, t, k * P:(k + 1) * P], start=(t == 0), stop=(t == NB - 1))
            last.then_inc(ctx_psum, 1)
            pe.wait_ge(counts_ready, NB)
            te.matmul(PS[:, 7, 0:NB], ltri[:, :], cnt, start=True, stop=True)
            te.matmul(PS[:, 7, NB:2 * NB], ones[:, 0:P], cnt, start=True, stop=True).then_inc(counts_psum, 1)
            pe.wait_ge(wo_in, 16)
            pe.wait_ge(ctx_ready, 2)
            for k in range(KD):
                if k >= 2:
                    pe.wait_ge(mo_ready, k - 1)
                elif k == 1:
                    pe.wait_ge(tab_ready, NB)
                te.matmul(PS[:, 1 + k % 2, :], ctxT[:, k, :], wo[:, k, :], start=True, stop=True).then_inc(mo_psum, 1)
            for t in range(NB):
                pe.wait_ge(mo_ready, KD)
                pe.wait_ge(qT_ready, t + 1)
                if t >= 2:
                    pe.wait_ge(mix_added, t - 1)
                for k in range(KD):
                    last = te.matmul(PS[0:NT, 3 + t % 2, :], QT[:, t, k, :], MO[:, k, :], start=(k == 0),
                                     stop=(k == KD - 1))
                last.then_inc(y_psum, 1)
            pe.wait_ge(ffn_small_in, 64)
            for k in range(KD):
                last = te.matmul(PS[:, 5, k:k + 1], ins_sb[:, k * P:(k + 1) * P], ones[0:NI, 0:1], start=True, stop=True)
            last.then_inc(mi_psum, 1)
            for k in range(KD):
                last = te.transpose(PS[:, 0, k * X8:(k + 1) * X8], gam_row[:, k * P:(k + 1) * P],
                                    ident[0:X8, 0:X8])
            last.then_inc(gamT_psum, 1)
            pe.wait_ge(z_ready, 1)
            pe.wait_ge(gamT_ready, 1)
            for lo, m, w in ((0, mi_bc, gamT), (8, mi_bc, rmod)):
                for k in range(KD):
                    te.matmul(PS[:, 6, lo:lo + X8], m[:, k, :], w[:, k, :], start=(k == 0), stop=(k == KD - 1))
            for k in range(KD):
                last = te.matmul(PS[0:X8, 6, 16:17], gamT[:, k, :], mi[:, k:k + 1], start=(k == 0), stop=(k == KD - 1))
            last.then_inc(gam_psum, 1)
            for e in range(X8):
                pe.wait_ge(beta_in[e % 2], 16 * (e // 2 + 1))
                for k in range(KD):
                    last = te.matmul(PS[0:X8, 7, :], z_mi[:, k, e, :], bslot[e % 2][:, k, :],
                                     start=(e == 0 and k == 0), stop=(e == X8 - 1 and k == KD - 1))
                last.then_inc(beta_used, 1)

            pe.wait_ge(b2_placed, 48)
            pe.wait_ge(router_ready, 1)
            pe.wait_ge(act_step, 1)

            pe.wait_ge(wf2_l, 1)

            def transposes(i, c):
                m = i * 2 + c
                pe.wait_ge(f_staged, m + 1)
                if real(m):
                    pe.wait_ge(fT_ready, m)
                for j in range(STEP):
                    last = te.transpose(PS[0:R, 0, j * P:(j + 1) * P], Fst[:, c % 2, j, :], ident[:, :])
                last.then_inc(f_used, 1)

            def layer1(i, c):
                m = i * 2 + c
                pe.wait_ge(fT_ready, m + 1)
                if real(m - 1):
                    pe.wait_ge(h_ready, m - 1)
                te.matmul(PS[:, 1 + c % 2, :], wf1[:, :], fT[0:R + 1, c % 2, :], start=True, stop=True)\
                    .then_inc(z_psum, 1)

            def layer2(i, c, j):
                m = i * 2 + c
                if j == 0:
                    pe.wait_ge(hl_ready, m + 1)
                if real(m):
                    pe.wait_ge(w_odd if j % 2 else w_even, (m - 1) * (STEP // 2) + j // 2 + 1)
                edges = slice(j * P, (j + 1) * P)
                te.matmul(PS[:, 3 + j, :], ones3[:, :], b2s[:, :, :].rearrange("p k n -> p (k n)"),
                          start=True, stop=False)
                for part, weights in ((h_high, wf2_high), (h_high, wf2_low), (h_low, wf2_high)):
                    last = te.matmul(PS[:, 3 + j, :], part[:, c % 2, edges],
                                     weights[:, :, :].rearrange("p k n -> p (k n)"), start=False,
                                     stop=part is h_low)
                last.then_inc(w_psum, 1)

            def filters(i):
                for h in range(2):
                    layer2(i, h, 0)
                    if exists(i, h + 2):
                        layer1(i, h + 2)
                    layer2(i, h, 1)
                    if exists(i, h + 3):
                        transposes(i, h + 3)
                    layer2(i, h, 2)
                    layer2(i, h, 3)

            transposes(0, 0)
            transposes(0, 1)
            layer1(0, 0)
            transposes(0, 2)
            layer1(0, 1)
            filters(0)
            with pe.Fori(1, FITER - 2) as i:
                filters(i)
            filters(FITER - 2)
            filters(FITER - 1)
            pe.wait_ge(h_ready, STEPS)
            pe.wait_ge(fT_ready, STEPS)
            pe.wait_ge(w_even, FITER * COLS // 2)
            pe.wait_ge(w_odd, FITER * COLS // 2)

            def sums(i, first):
                per = UNROLL * TPG
                for s in range(UNROLL):
                    bank = 2 * (s // PPG)
                    if s % PPG == 0 and not first:
                        pe.wait_ge(sums_out, upto(i - 1, GPB, s // PPG))
                    for t in range(TPG):
                        n = s * TPG + t
                        pe.wait_ge(onehot_odd if t else onehot_even, upto(i, per, s * TPG + 1))
                        pe.wait_ge(c_ready, upto(i, per, n))
                        pe.wait_ge(d_ready, upto(i, per, n))
                        pe.wait_ge(b_ready, upto(i, per, n))
                        for half_ in range(2):
                            last = te.matmul(PS[0:NT, bank + half_, :], OH[:, s, t, 0:NT],
                                             MB[:, s % 2, t, 4 * half_:4 * half_ + 4, :].rearrange("p k n -> p (k n)"),
                                             start=(s % PPG == 0 and t == 0),
                                             stop=(s % PPG == PPG - 1 and t == TPG - 1))
                        last.then_inc(summed, 1)

            sums(0, True)
            with pe.Fori(1, MITER) as i:
                sums(i, False)

            def transpose_sums(t):
                if t >= 2:
                    pe.wait_ge(aT_ready, t - 1)
                for k in range(8):
                    last = te.transpose(PS[:, 4 * (t % 2) + k // 4, (k % 4) * NT:(k % 4 + 1) * NT],
                                        acc[0:NT, t * MSG + k * C:t * MSG + (k + 1) * C], idn)
                last.then_inc(aT_psum, 1)

            def first_mixing(t):
                h, bank = t % 2, 4 * (t % 2) + 2
                pe.wait_ge(aT_ready, t + 1)
                if t >= 2:
                    pe.wait_ge(s_ready, t - 1)
                    pe.wait_ge(v1_ready, t - 1)
                for k in range(2):
                    te.matmul(PS[:, bank, 0:NT], w1s[:, k, :], AT[:, h, k, 0:NT], start=(k == 0), stop=(k == 1))
                for k in range(2):
                    last = te.matmul(PS[:, bank, NT:4 * NT].rearrange("p (k n) -> p k n", n=NT), w1v[:, k, :],
                                     AT[:, h, 2 + 3 * k:5 + 3 * k, 0:NT], start=(k == 0), stop=(k == 1))
                last.then_inc(sv_psum, 1)

            def second_mixing(t):
                h = t % 2
                pe.wait_ge(s_ready, t + 1)
                pe.wait_ge(v1_ready, t + 1)
                if t >= 2:
                    pe.wait_ge(x1_ready, t - 1)
                for k in range(4):
                    last = te.matmul(PS[0:NT, 4 * h + 3, k * C:(k + 1) * C], S1[:, h, k, 0:NT],
                                     w2v[:, :] if k else w2s[:, :], start=True, stop=True)
                last.then_inc(g_psum, 1)

            pe.wait_ge(flushed, GROUPS)
            transpose_sums(0)
            transpose_sums(1)
            first_mixing(0)
            for t in range(NB):
                if t + 2 < NB:
                    transpose_sums(t + 2)
                if t + 1 < NB:
                    first_mixing(t + 1)
                second_mixing(t)
            def split_product(psum, xs, ws):
                (xh, xl), (wh, wl) = xs, ws
                terms = [(m, w, k) for k in range(KD) for m, w in ((xh, wh), (xh, wl), (xl, wh))]
                for n, (m, w, k) in enumerate(terms):
                    last = te.matmul(psum, m[:, k, :], w[:, k, :], start=(n == 0), stop=(n == len(terms) - 1))
                return last

            def transpose_xf(t):
                pe.wait_ge(xf_ready, t + 1)
                if t >= 2:
                    pe.wait_ge(xT_l, t - 1)
                for k in range(KD):
                    last = te.transpose(PS[:, t % 2, k * NT:(k + 1) * NT], XF[0:NT, t % 2, k * P:(k + 1) * P], idn)
                last.then_inc(xfT_psum, 1)

            pe.wait_ge(x1_ready, NB)
            transpose_xf(0)
            transpose_xf(1)
            pe.wait_ge(gate_l, 1)
            for t in range(NB):
                pe.wait_ge(xT_l, t + 1)
                split_product(PS[0:NT, 2, t * X8:(t + 1) * X8], (xT_high[:, t], xT_low[:, t]),
                              (gate_high, gate_low)).then_inc(logit_psum, 1)
                if t + 2 < NB:
                    transpose_xf(t + 2)
            for e in range(X8):
                pe.wait_ge(we_split_l, e + 1)
                for t in range(NB):
                    n = e * NB + t
                    if n == 4:
                        pe.wait_ge(comb_ready, 1)
                        for u in range(NB):
                            last = te.transpose(PS[0:X8, (0, 1, 3)[u // 4], (u % 4) * NT:(u % 4 + 1) * NT],
                                                comb[0:NT, u, :], idn)
                            if u % 4 == 3 or u == NB - 1:
                                last.then_inc(combT_psum, 1)
                    if n >= 4:
                        pe.wait_ge(eo_used, n - 3)
                    split_product(PS[0:NT, 4 + n % 4, :], (xT_high[:, t], xT_low[:, t]),
                                  (we_high[:, e % 2], we_low[:, e % 2])).then_inc(eo_psum, 1)
                    if e == 1:
                        if t == 0:
                            pe.wait_ge(combT_ready, 3)
                        elif t >= 2:
                            pe.wait_ge(bias_added, t - 1)
                        te.matmul(PS[0:NT, t % 2, :], comb_t[0:X8, t, :], bb[0:X8, :], start=True, stop=True)\
                            .then_inc(bias_psum, 1)


_INS = ["x", "src", "dst", "edge_attr_20", "edge_attr_3", "edge_weight", "L0_gnn_W_in2f_s", "L0_gnn_W_in2f_v",
        "L0_gnn_Wf1", "L0_gnn_bf1", "L0_gnn_Wf2", "L0_gnn_bf2", "L0_gnn_W1_s", "L0_gnn_W1_v", "L0_gnn_W2_s",
        "L0_gnn_W2_v", "L0_mix_Wq", "L0_mix_Wk", "L0_mix_Wv", "L0_mix_Wo", "L0_mix_bo", "L0_ffn_Ins_tk",
        "L0_ffn_gate_w", "L0_ffn_expert_w", "L0_ffn_expert_b", "L0_ffn_gamma_w", "L0_ffn_beta_w", "L0_ffn_rmod_w"]


def kernel(**inputs):
    import concourse.bacc as bacc
    from concourse.bass_utils import run_bass_kernel_spmd

    nc = bacc.Bacc("TRN2", target_bir_lowering=False, num_devices=1)
    arrays, args = {}, []
    for name in _INS:
        a = np.ascontiguousarray(inputs[name])
        arrays[f"in_{name}"] = a
        args.append(nc.dram_tensor(f"in_{name}", a.shape, mybir.dt.from_np(a.dtype), kind="ExternalInput").ap())
    shape = tuple(np.shape(inputs["x"]))
    args.append(nc.dram_tensor("out_0", shape, F32, kind="ExternalOutput").ap())
    gps_layer(nc, *args)
    return run_bass_kernel_spmd(nc, [arrays], core_ids=[0]).results[0]["out_0"]
```

```python
from contextlib import ExitStack

import numpy as np

import concourse.bass as bass
from concourse import mybir

F32 = mybir.dt.float32
F32R = mybir.dt.float32r
BF16 = mybir.dt.bfloat16
I32 = mybir.dt.int32
ALU = mybir.AluOpType
ACT = mybir.ActivationFunctionType
AX_X = mybir.AxisListType.X
ds = bass.ds

P = 128
GROUP = 512
TPG = 2
PPG = GROUP // (TPG * P)
UNROLL = 8
STEP = 4
RING = 4
LAG = 7
EPS = 1e-5


def upto(i, per, j):
    return i * per + (j + 1)


def real(count):
    return not isinstance(count, int) or count >= 1


def gps_layer(nc, x, src, dst, edge_attr_20, edge_attr_3, edge_weight, W_in2f_s, W_in2f_v, Wf1, bf1, Wf2, bf2,
              W1_s, W1_v, W2_s, W2_v, Wq, Wk, Wv, Wo, bo, Ins_tk, gate_w, expert_w, expert_b, gamma_w, beta_w,
              rmod_w, out):
    N, D = x.shape
    E, R = edge_attr_20.shape
    C = W_in2f_s.shape[0]
    KD = D // P
    NB = 10
    NT = N // NB
    HEADS, DH = 8, 64
    X8, OUT = expert_w.shape[0], expert_w.shape[2]
    NI = Ins_tk.shape[1]
    GROUPS = (E + NB * (GROUP - 1)) // GROUP
    GROUPS = -(-GROUPS // (UNROLL // PPG)) * (UNROLL // PPG)
    PAIRS = GROUPS * PPG
    NCOL = PAIRS * TPG
    FULL = E // P
    REM = E - FULL * P
    RC1 = FULL + 1
    SPARE = NCOL - FULL
    REC = 4 * C + 8
    COLS = RING * STEP
    FITER = -(-RC1 // COLS)
    LOOPED = FITER * COLS
    MITER = PAIRS // UNROLL
    GPB = UNROLL // PPG
    STEPS = RING * FITER
    MSG = 8 * C
    Y0 = float(1.0 / np.sqrt(4.0 * np.pi))
    assert NB * NT == N and NT <= P and C == P and RC1 <= LOOPED <= NCOL and REM % 32 == 0 and OUT == D

    rec_dram = nc.dram_tensor("edge_records", [NCOL * P, REC], F32, kind="Internal").ap()
    tab_dram = nc.dram_tensor("node_table", [N, 4 * C], F32, kind="Internal").ap()

    ctx = ExitStack()
    with ctx:
        def sb(name, shape, dt=F32):
            return ctx.enter_context(nc.sbuf_tensor(name, shape, dt))

        def sem(name):
            return ctx.enter_context(nc.semaphore(name))

        def sems(name, n):
            return [sem(f"{name}{k}") for k in range(n)]

        PS = ctx.enter_context(nc.psum_tensor("PS", [P, 8, 512], F32))

        X = sb("X", [P, NB, D])
        ident = sb("ident", [P, P])
        iota_f = sb("iota_f", [P, P])
        ones = sb("ones", [P, 320])
        ltri = sb("ltri", [P, P])
        w1s = sb("w1s", [P, 2, C])
        w1v = sb("w1v", [P, 2, C])
        w2s = sb("w2s", [P, C])
        w2v = sb("w2v", [P, C])
        gate = sb("gate", [P, KD, X8])
        small = sb("small", [P, 640])
        gam8 = small[:, 0:8]
        rgam = small[:, 8:16]
        mean = small[:, 16:26]
        var_eps = small[:, 26:36]
        rstd = small[:, 36:46]
        stats = small[:, 48:108].rearrange("p (t s) -> p t s", s=6)
        aggr = small[:, 108:128].rearrange("p (t s) -> p t s", s=2)
        mxq, mxk = small[:, 128:136], small[:, 136:144]
        smq, smk = small[:, 144:152], small[:, 152:160]
        cnt = small[:, 160:170]
        tot = small[:, 170:180]
        pref = small[:, 180:190]
        ngf = small[:, 190:200]
        endg = small[:, 200:210]
        base = small[:, 210:220]
        off = small[:, 220:230]
        cumt = small[:, 230:240]
        cpad = small[:, 240:250]
        mi = small[:, 266:270]
        newton = small[:, 284:294]
        gcol = small[:, 278:279]
        tie = small[:, 468:532].rearrange("p (a b) -> p a b", b=X8)
        ints = sb("ints", [P, 16], I32)
        goff = sb("goff", [P, GROUPS], I32)
        half = sb("half", [P, 1])
        bb = sb("bb", [P, D])

        WE_SLOTS = 3
        r2_words = 16384
        r2_base = nc.sbuf_base
        R2 = sb("R2", [P, r2_words])
        at = [0]

        def r2(words):
            a = at[0]
            at[0] += words
            assert at[0] <= r2_words
            return R2[:, a:a + words]

        Fe = r2(LOOPED * R).rearrange("p (c r) -> p c r", r=R)
        meta = r2(LOOPED * 8).rearrange("p (c m) -> p c m", m=8)
        rcut = r2(LOOPED)
        posi = r2(NCOL).bitcast(I32)
        empty = R2[:, at[0]:at[0] + REC]
        srci = r2(RC1).bitcast(I32)
        srcf = r2(RC1)
        assert REC <= 2 * RC1
        bkt = r2(RC1)
        rnk = r2(RC1)
        tA, tB = r2(RC1), r2(RC1)
        kd = r2(SPARE)
        pd = r2(SPARE)
        fT = r2(2 * 512).rearrange("p (h n) -> p h n", h=2)
        tz = r2(2 * 512).rearrange("p (h n) -> p h n", h=2)
        hT = r2(2 * 512).rearrange("p (h n) -> p h n", h=2)
        Fst = r2(2 * STEP * R).rearrange("p (h c r) -> p h c r", h=2, r=R)
        b2_rows = r2(4 * C)
        rb_words = UNROLL * TPG * REC
        RB = R2[:, r2_words - rb_words:r2_words].rearrange("p (s t r) -> p s t r", s=UNROLL, t=TPG)
        we = R2[:, 0:WE_SLOTS * KD * OUT].rearrange("p (e k n) -> p e k n", e=WE_SLOTS, k=KD)
        sums_words = 2 * 2 * 512
        SG = R2[:, r2_words - rb_words - sums_words:r2_words - rb_words].rearrange("p (s n) -> p s n", s=2)
        EARLY = (r2_words - rb_words - sums_words) // (KD * OUT)

        r1_words = 27400
        r1_base = nc.sbuf_base
        R1 = sb("R1", [P, r1_words])

        def rounded(name, word, shape, base=r1_base):
            return nc.alloc_sbuf_tensor_at(name, shape, F32R, offset=base + 4 * word)

        class Carve:

            def __init__(self, start=0):
                self.at = start

            def __call__(self, words):
                a = self.at
                self.at += words
                assert self.at <= r1_words, self.at
                return R1[:, a:a + words]

        c1 = Carve()
        wqkv = c1(3 * KD * D).rearrange("p (w k n) -> p w k n", w=3, k=KD)
        KN = c1(NB * D).rearrange("p (t n) -> p t n", t=NB)
        VN = c1(NB * D).rearrange("p (t n) -> p t n", t=NB)
        QT = c1(KD * NB * NT).rearrange("p (t k n) -> p t k n", t=NB, k=KD)
        wo = c1(KD * D).rearrange("p (k n) -> p k n", k=KD)
        c1_late = c1.at
        XN = c1(2 * D).rearrange("p (s n) -> p s n", s=2)
        XT = c1(2 * KD * NT).rearrange("p (s k n) -> p s k n", s=2, k=KD)
        TAB = c1(2 * D).rearrange("p (s n) -> p s n", s=2)
        QW = c1(D)
        wsv = c1(2 * C).rearrange("p (w n) -> p w n", w=2)
        MO = wqkv[:, 0, :, :]
        ctxT = wqkv[:, 1, 0, :].rearrange("p (k n) -> p k n", k=KD)
        bo_b = wqkv[:, 2, 0, :]
        bslot = [VN[:, 0:4, :], VN[:, 4:8, :], KN[:, 1:5, :], KN[:, 5:9, :]]
        ins_sb = QW[0:NI, :]
        z_mi = VN[:, 8:9, 0:KD * X8 * X8].rearrange("p o (k e f) -> p (o k) e f", k=KD, e=X8)
        gamT = wsv[:, 0, 0:KD * X8].rearrange("p (k e) -> p k e", k=KD)
        rmod = wsv[:, 0, 32:32 + KD * X8].rearrange("p (k e) -> p k e", k=KD)
        gam_row = XN[0:X8, 0, :]
        mi_bc = KN[:, 0, :].rearrange("p (k n) -> p k n", k=KD)
        be_row = XN[0:X8, 1, :]

        acc_at = r1_words - NB * MSG
        acc = R1[:, acc_at:r1_words]
        wf2_high = rounded("wf2_high", (2 * KD + 1) * D, [P, 4, C])
        wf2_low = rounded("wf2_low", (2 * KD + 2) * D, [P, 4, C])
        c2 = Carve((2 * KD + 3) * D)
        ST = c2(COLS * REC).rearrange("p (s r) -> p s r", r=REC)
        idxst = c2(COLS).bitcast(I32)
        h_high = rounded("h_high", c2.at, [P, 2, 512])
        h_low = rounded("h_low", c2.at + 1024, [P, 2, 512])
        c2(2048)
        assert c2.at <= acc_at

        c3 = Carve()
        GB = c3(UNROLL * TPG * 4 * C).rearrange("p (s t n) -> p s t n", s=UNROLL, t=TPG)
        MB = c3(2 * TPG * 9 * C).rearrange("p (s t k n) -> p s t k n", s=2, t=TPG, k=9)
        OH = c3(UNROLL * TPG * P).rearrange("p (s t n) -> p s t n", s=UNROLL, t=TPG)
        DT = c3(2 * TPG * 3 * C).rearrange("p (s t k n) -> p s t k n", s=2, t=TPG, k=3)
        assert c3.at <= acc_at

        c4 = Carve()
        AT = c4(2 * 8 * P).rearrange("p (s k n) -> p s k n", s=2, k=8)
        S1 = c4(2 * 4 * P).rearrange("p (s k n) -> p s k n", s=2, k=4)
        sz = c4(2 * P).rearrange("p (s n) -> p s n", s=2)
        XF = c4(2 * D).rearrange("p (s n) -> p s n", s=2)
        prob = c4(NB * X8).rearrange("p (t e) -> p t e", t=NB)
        comb = c4(NB * X8).rearrange("p (t e) -> p t e", t=NB)
        cg = c4(NB * X8).rearrange("p (t e) -> p t e", t=NB)
        rank = c4(NB * X8).rearrange("p (t e) -> p t e", t=NB)
        st1 = c4(16)[:, 0:NB]
        cmp_a = c4(NB * X8 * X8).rearrange("p (t a b) -> p t a b", t=NB, a=X8)
        cmp_b = c4(NB * X8 * X8).rearrange("p (t a b) -> p t a b", t=NB, a=X8)
        comb_t = c4(-(-NB * NT // 8) * 8)[:, 0:NB * NT].rearrange("p (t n) -> p t n", t=NB)
        gate_high = rounded("gate_high", c4.at, [P, KD, X8])
        gate_low = rounded("gate_low", c4.at + KD * X8, [P, KD, X8])
        c4(2 * KD * X8)
        we_high = rounded("expert_w_high", c4.at, [P, 2, KD, OUT])
        we_low = rounded("expert_w_low", c4.at + 2 * KD * OUT, [P, 2, KD, OUT])
        c4(4 * KD * OUT)
        assert c4.at <= acc_at
        xT_at = WE_SLOTS * KD * OUT
        assert xT_at + 2 * KD * N <= r2_words
        xT_high = rounded("xT_high", xT_at, [P, KD, N], r2_base)
        xT_low = rounded("xT_low", xT_at + KD * N, [P, KD, N], r2_base)

        wf1 = sb("wf1", [R + 1, P])
        wf2 = sb("wf2", [P, 4, C])
        b2s = sb("b2s", [3, 4, C], BF16)
        ones3 = sb("ones3", [3, P], BF16)
        rraw = KN[:, 0:2, :].rearrange("p t n -> p (t n)")[:, 0:RC1 * 3].rearrange("p (c i) -> p c i", i=3)
        ssq = KN[:, 2, 0:RC1]
        inv = KN[:, 3, 0:RC1]
        rtmp = KN[:, 4:6, :].rearrange("p t n -> p (t n)")[:, 0:RC1 * 3].rearrange("p (c i) -> p c i", i=3)
        dsti = KN[:, 6, 0:RC1].bitcast(I32)
        wf2raw = KN[:, 7, :]
        b2raw = KN[0:3, 8, :]
        b2rem = KN[0:3, 9, :]
        b2p = [VN[0:3, 7 + k, 0:256].bitcast(BF16) for k in range(3)]

        consts = sem("constants_ready")
        pool_step = sem("pool_step")
        dve_step = sem("dve_step")
        act_step = sem("act_step")
        x_in = sems("x_in", 2)
        wsv_in, wqkv_in, wo_in = sem("wsv_in"), sems("wqkv_in", 3), sem("wo_in")
        bo_added = sem("bo_added")
        bo_in, ffn_small_in, w12_in = sem("bo_in"), sem("ffn_small_in"), sem("w12_in")
        edge_in, f_in, rcut_in, wf_in, b2_in = sem("edge_in"), sem("f_in"), sem("rcut_in"), sem("wf_in"), sem("b2_in")
        edge_zero = sem("edge_buffers_filled")
        b2_parts = sem("b2_parts_made")
        b2_placed = sem("b2_placed")
        var_ready, std_ready, nrm_sq, nrm_root = sem("var_ready"), sem("std_ready"), sem("norm_sq"), sem("norm_root")
        xn_ready = sem("xn_ready")
        xT_psum, xT_ready = sem("xT_psum"), sem("xT_ready")
        tab_psum, tab_ready, tab_out = sem("table_psum"), sem("table_ready"), sems("table_out", 2)
        q_psum, k_psum, v_psum = sem("q_psum"), sem("k_psum"), sem("v_psum")
        q_shift, k_shift, q_exp, k_exp = sem("q_shifted"), sem("k_shifted"), sem("q_exp"), sem("k_exp")
        q_norm, k_norm, v_ready = sem("q_normal"), sem("k_normal"), sem("v_ready")
        qT_psum, qT_ready = sem("qT_psum"), sem("qT_ready")
        counts_ready, counts_psum = sem("counts_ready"), sem("counts_psum")
        counts_read, places_ready = sem("counts_read"), sem("places_ready")
        empty_ready, empty_scattered = sem("empty_record_ready"), sem("empty_scattered")
        ctx_psum, ctx_zero, ctx_ready = sem("context_psum"), sem("context_zeroed"), sem("context_ready")
        mo_psum, mo_ready = sem("context_wo_psum"), sem("context_wo_ready")
        y_psum, mix_added = sem("mix_psum"), sem("mix_added")
        mi_psum, z_ready = sem("ins_mean_psum"), sem("ins_mean_spread")
        gamT_ready = sem("gammaT_ready")
        gam_psum = sem("gamma_psum")
        beta_in, beta_used = sems("beta_in", 4), sem("beta_used")
        router_ready = sem("router_ready")
        staged, f_staged = sem("edge_columns_staged"), sem("f_staged")
        f_used = sem("f_transposed")
        fT_ready, z_psum, h_ready = sem("fT_ready"), sem("z_psum"), sem("h_ready")
        log_stage = sem("log_stage")
        hh_ready, hl_ready = sem("h_high_ready"), sem("h_low_ready")
        wf2_h, wf2_l = sem("wf2_high_ready"), sem("wf2_low_ready")
        w_psum, w_act, w_dve = sem("filter_psum"), sem("filter_by_act"), sem("filter_by_dve")
        b2_psum, b2_ready = sem("b2_psum"), sem("b2_rows_ready")
        scattered = sems("step_scattered", RING)
        indirect_turn = sem("indirect_turn")
        rec_in = sems("record_in", UNROLL)
        gathered = sems("pair_gathered", UNROLL)
        acc_zero = sem("sums_zeroed")
        dot1, dot_sum = sem("dot_x"), sem("dot_sum")
        onehot = sem("onehot_ready")
        ac_ready, b_ready, d_ready, c_ready = (sem("message_ac"), sem("message_b"), sem("message_d"),
                                               sem("message_c"))
        summed, sums_out, flushed = sem("tile_summed"), sem("group_out_of_psum"), sem("group_added")
        we_early_in = sem("early_expert_w_in")
        we_in = sems("expert_w_in", WE_SLOTS)
        we_split_h, we_split_l = sem("expert_w_high_ready"), sem("expert_w_low_ready")
        gate_h, gate_l = sem("gate_high_ready"), sem("gate_low_ready")
        aT_psum, aT_ready = sem("sumsT_psum"), sem("sumsT_ready")
        sv_psum, s_abs, s_ln, s_ready, v1_ready = (sem("mixed_psum"), sem("s_abs"), sem("s_log"), sem("s_ready"),
                                                   sem("v_mixed_ready"))
        g_psum, x1_ready = sem("gnn_psum"), sem("x1_ready")
        var2_ready, std2_step, std2_ready = sem("var2_ready"), sem("log_var2_ready"), sem("std2_ready")
        rstd2_ready = sem("rstd2_ready")
        xf_even, xf_odd, xfT_psum = sem("xf_even_ready"), sem("xf_odd_ready"), sem("xfT_psum")
        xT_h, xT_l = sem("xT_high_ready"), sem("xT_low_ready")
        logitT_psum, logitT_ready = sem("logitT_psum"), sem("logitT_ready")
        logit_psum, shift_ready, prob_exp = sem("logit_psum"), sem("logits_shifted"), sem("logits_exp")
        comb_ready, combT_psum, combT_ready, bias_psum = (sem("combine_ready"), sem("combineT_psum"),
                                                          sem("combineT_ready"), sem("expert_bias_psum"))
        eo_psum, eo_used = sem("expert_psum"), sem("expert_used")
        bias_added = sem("expert_bias_added")
        o_out = sem("output_stored")

        block = ctx.enter_context(nc.Block())

        quads = [(t, min(4, NB - t)) for t in range(0, NB, 4)]
        XF_SPREAD = NB - 3

        def xf_bank(t):
            return 7 if t < XF_SPREAD else (0, 1, 7)[t - XF_SPREAD]

        y_banks = (3, 4, 5, 6, 0, 1, 2)

        def exists(i, c):
            return not isinstance(i, int) or RING * i + c < STEPS

        def columns_of(i, c):
            first = (i * RING + c) * STEP
            return slice(first, first + STEP) if isinstance(i, int) else ds(first, STEP)


        @block.sync
        def _(sp):
            xv = x.rearrange("(t p) d -> p t d", p=NT)
            sp.dma_start(X[0:NT, 0:2, :], xv[:, 0:2, :]).then_inc(x_in[0], 16)
            sp.dma_start(wsv[:, 0, :], W_in2f_s).then_inc(wsv_in, 16)
            sp.dma_start(wsv[:, 1, :], W_in2f_v).then_inc(wsv_in, 16)
            sp.dma_start(X[0:NT, 2:NB, :], xv[:, 2:NB, :]).then_inc(x_in[1], 16)
            for w, (wt, s) in enumerate(zip((Wq, Wk, Wv), wqkv_in)):
                if w == 1:
                    sp.wait_ge(edge_in, 16 * 6)
                sp.dma_start(wqkv[:, w, 0, :], wt[0:C, :]).then_inc(s, 16)
                sp.dma_start(wqkv[:, w, 1:KD, :], wt[C:D, :].rearrange("(c i) n -> c i n", i=3)).then_inc(s, 16)
            sp.dma_start(wo, Wo.rearrange("(k p) n -> p k n", p=P)).then_inc(wo_in, 16)
            sp.dma_start(w1s[:, :, :], W1_s.rearrange("(f a) c -> f a c", a=2)).then_inc(w12_in, 16)
            sp.dma_start(w1v[:, :, :], W1_v.rearrange("(f a) c -> f a c", a=2)).then_inc(w12_in, 16)
            sp.dma_start(w2s[:, :], W2_s).then_inc(w12_in, 16)
            sp.dma_start(w2v[:, :], W2_v).then_inc(w12_in, 16)
            sp.dma_start(gate[:, :, :], gate_w.rearrange("(k p) e -> p k e", p=P)).then_inc(w12_in, 16)
            for t in range(NB):
                sp.wait_ge(tab_ready, t + 1)
                sp.dma_start(tab_dram[t * NT:(t + 1) * NT, :], TAB[0:NT, t % 2, :]).then_inc(tab_out[t % 2], 16)
            sp.wait_ge(ctx_psum, 1)
            sp.wait_ge(tab_psum, NB)
            sp.wait_ge(qT_psum, NB)
            sp.wait_ge(xT_psum, NB)
            sp.dma_start(bo_b[0:NT, :], bo.rearrange("(o n) -> o n", o=1).to_broadcast([NT, D])).then_inc(bo_in, 16)
            sp.dma_start(ins_sb, Ins_tk[0]).then_inc(ffn_small_in, 16)
            sp.dma_start(gam_row, gamma_w).then_inc(ffn_small_in, 16)
            sp.dma_start(be_row, expert_b).then_inc(ffn_small_in, 16)
            sp.dma_start(rmod, rmod_w.rearrange("(k p) e -> p k e", p=P)).then_inc(ffn_small_in, 16)
            for e in range(X8):
                if e >= 4:
                    sp.wait_ge(beta_used, e - 3)
                sp.dma_start(bslot[e % 4], beta_w[e].rearrange("(k p) n -> p k n", p=P)).then_inc(beta_in[e % 4], 16)

            for c in range(RING):
                sp.wait_ge(scattered[c], 16 * STEP * FITER)
            sp.wait_ge(empty_scattered, 16 * (NCOL - LOOPED))
            sp.wait_ge(router_ready, 1)
            sp.wait_ge(mix_added, NB)
            rv = rec_dram.rearrange("(g p t) r -> g p (t r)", p=P, t=TPG)

            def load(i, first):
                for s in range(UNROLL):
                    if not first:
                        sp.wait_ge(onehot, upto(i - 1, UNROLL * TPG, s * TPG + 1))
                        sp.wait_ge(b_ready, upto(i - 1, UNROLL * TPG, s * TPG + 1))
                        sp.wait_ge(d_ready, upto(i - 1, UNROLL * TPG, s * TPG + 1))
                        sp.wait_ge(c_ready, upto(i - 1, UNROLL * TPG, s * TPG + 1))
                        sp.wait_ge(dot1, upto(i - 1, UNROLL * TPG, s * TPG + 1))
                    elif s >= 3:
                        sp.wait_ge(gathered[s - 3], 16 * TPG)
                    g = i * UNROLL + s
                    r = rv[g] if first else rv[ds(g, 1)].rearrange("o p r -> p (o r)")
                    sp.dma_start(RB[:, s, :, :].rearrange("p t r -> p (t r)"), r).then_inc(rec_in[s], 16)

            wv = expert_w.rearrange("e (k p) n -> (e k) p n", p=P)
            wd = we.rearrange("p e k n -> p (e k) n")
            pieces = EARLY * KD
            load(0, True)
            with sp.Fori(1, pieces + 1) as i:
                load(i, False)
                sp.dma_start(wd[:, ds(i - 1, 1), :].rearrange("p o n -> p (o n)"),
                             wv[ds(i - 1, 1)].rearrange("o p n -> p (o n)")).then_inc(we_early_in, 16)
            with sp.Fori(pieces + 1, MITER) as i:
                load(i, False)
            for done in (b_ready, d_ready, c_ready, dot1, onehot):
                sp.wait_ge(done, NCOL)
            sp.wait_ge(flushed, GROUPS)
            for e in range(EARLY, X8):
                if e >= WE_SLOTS:
                    sp.wait_ge(we_split_l, e - WE_SLOTS + 1)
                sp.dma_start(we[:, e % WE_SLOTS], expert_w[e].rearrange("(k p) n -> p k n", p=P))\
                    .then_inc(we_in[(e - EARLY) % WE_SLOTS], 16)
            for t in range(NB):
                sp.wait_ge(eo_used, (X8 - 1) * NB + t + 1)
                sp.dma_start(out[t * NT:(t + 1) * NT, :], X[0:NT, t, :]).then_inc(o_out, 16)
            sp.wait_ge(o_out, 16 * NB)
            for s in range(2):
                sp.wait_ge(tab_out[s], 16 * (NB // 2))

        @block.gpsimd
        def _(pool):
            steps = [0]

            def step(ins):
                steps[0] += 1
                ins.then_inc(pool_step, 1)
                pool.wait_ge(pool_step, steps[0])

            g = nc.gpsimd
            g.memset(srci[:, :], 0)
            g.memset(dsti[:, :], 0)
            g.memset(rraw[:, :, :], 1.0).then_inc(edge_zero, 1)
            pool.wait_ge(edge_zero, 1)
            g.dma_start(rraw[:, 0:FULL, :], edge_attr_3[0:P * FULL, :].rearrange("(p c) i -> p c i", p=P))\
                .then_inc(edge_in, 16)
            g.dma_start(rraw[0:REM, FULL, :], edge_attr_3[P * FULL:E, :]).then_inc(edge_in, 16)
            for dest, values in ((srci, src), (dsti, dst)):
                v = values.rearrange("(n o) -> n o", o=1)
                g.dma_start(dest[:, 0:FULL], values[0:P * FULL].rearrange("(p c) -> p c", p=P)).then_inc(edge_in, 16)
                g.dma_start(dest[0:REM, FULL:RC1], v[P * FULL:E, :]).then_inc(edge_in, 16)
            step(g.memset(ones[:, :], 1.0))
            step(g.memset(ident[:, :], 0.0))
            step(g.affine_select(out=ident[:, :], in_=ident[:, :], compare_op=ALU.not_equal, fill=1.0, base=0,
                                 pattern=[[-1, P]], channel_multiplier=1))
            step(g.affine_select(out=ltri[:, :], in_=ones[:, 0:P], compare_op=ALU.is_gt, fill=0.0, base=0,
                                 pattern=[[1, P]], channel_multiplier=-1))
            g.iota(iota_f[:, :], pattern=[[1, P]], base=0, channel_multiplier=0,
                   allow_small_or_imprecise_dtypes=True).then_inc(consts, 1)
            g.memset(meta[:, :, :], 0.0)
            g.memset(rcut[:, :], 0.0)
            g.memset(Fe[:, FULL:LOOPED, :], 0.0).then_inc(edge_zero, 1)
            g.memset(ones3[:, :], 1.0)
            g.affine_select(out=tie, in_=ones[:, 0:X8 * X8].rearrange("p (a b) -> p a b", b=X8), compare_op=ALU.is_gt,
                            fill=0.0, base=0, pattern=[[1, X8], [-1, X8]], channel_multiplier=0)
            g.iota(kd[:, :], pattern=[[P, SPARE]], base=-REM, channel_multiplier=1,
                   allow_small_or_imprecise_dtypes=True)
            g.iota(goff[:, :], pattern=[[1, GROUPS]], base=0, channel_multiplier=0).then_inc(consts, 1)
            pool.wait_ge(edge_zero, 2)
            g.dma_start(rcut[:, 0:FULL], edge_weight[0:P * FULL].rearrange("(p c) -> p c", p=P)).then_inc(rcut_in, 16)
            g.dma_start(rcut[0:REM, FULL:RC1], edge_weight.rearrange("(n o) -> n o", o=1)[P * FULL:E, :])\
                .then_inc(rcut_in, 16)
            g.dma_start(wf2raw, Wf2[:, 0:4 * C]).then_inc(wf_in, 16)
            g.dma_start(b2raw, bf2.rearrange("(o n) -> o n", o=1)[:, 0:4 * C].to_broadcast([3, 4 * C]))\
                .then_inc(b2_in, 16)
            g.dma_start(wf1[0:R, :], Wf1).then_inc(wf_in, 16)
            g.dma_start(wf1[R:R + 1, :], bf1.rearrange("(o n) -> o n", o=1)).then_inc(wf_in, 16)
            pool.wait_ge(b2_parts, 1)
            for k in range(3):
                g.dma_start(b2s[k:k + 1, :, :].rearrange("p k n -> p (k n)"), b2p[k][k:k + 1, :])\
                    .then_inc(b2_placed, 16)

            pool.wait_ge(v_psum, 1)
            g.dma_start(Fe[:, 0:FULL, :], edge_attr_20[0:P * FULL, :].rearrange("(p c) r -> p c r", p=P))\
                .then_inc(f_in, 16)
            g.dma_start(Fe[0:REM, FULL, :], edge_attr_20[P * FULL:E, :]).then_inc(f_in, 16)
            pool.wait_ge(xn_ready, NB)
            pool.wait_ge(bo_in, 16)
            g.tensor_tensor(X[0:NT, :, :], X[0:NT, :, :], bo_b[0:NT, :].unsqueeze(1).to_broadcast([NT, NB, D]),
                            ALU.add).then_inc(bo_added, 1)
            pool.wait_ge(places_ready, 1)
            g.memset(empty, 0.0).then_inc(empty_ready, 1)
            pool.wait_ge(empty_ready, 1)
            for c in range(LOOPED, NCOL):
                g.indirect_dma_start(out=rec_dram, out_offset=bass.IndirectOffsetOnAxis(ap=posi[:, c:c + 1], axis=0),
                                     in_=empty, in_offset=None).then_inc(empty_scattered, 16)
            late = c1_late - acc_at
            pool.wait_ge(mix_added, NB)
            g.memset(acc[:, 0:late], 0.0)
            pool.wait_ge(router_ready, 1)
            for s in range(2):
                pool.wait_ge(tab_out[s], 16 * (NB // 2))
            g.memset(acc[:, late:], 0.0).then_inc(acc_zero, 1)

            def scatter(i):
                for j in range(COLS):
                    if j % STEP == 0:
                        pool.wait_ge(w_act, upto(i, RING, j // STEP))
                    else:
                        pool.wait_ge(w_dve, upto(i, RING * (STEP - 1), j // STEP * (STEP - 1) + j % STEP - 1))
                    pool.wait_ge(staged, upto(i, RING, j // STEP))
                    pool.sem_inc(indirect_turn, 1)
                    place = bass.IndirectOffsetOnAxis(ap=idxst[:, j:j + 1], axis=0)
                    g.indirect_dma_start(out=rec_dram, out_offset=place,
                                         in_=ST[:, j, :], in_offset=None).then_inc(scattered[j // STEP], 16)

            scatter(0)
            with pool.Fori(1, FITER) as i:
                scatter(i)
            def flush(i, q, static):
                n = i * GPB + q
                word = pool.value_load(goff[0:1, n:n + 1] if static else goff[0:1, ds(n, 1)], min_val=0,
                                       max_val=(NB - 1) * MSG)
                pool.wait_ge(sums_out, upto(i, GPB, q))
                if not static or n:
                    pool.wait_ge(flushed, n)
                dst_ap = acc[0:NT, ds(word, MSG)]
                g.tensor_tensor(dst_ap, dst_ap, SG[0:NT, q % 2, :], ALU.add).then_inc(flushed, 1)

            def gather(i, first):
                for s in range(UNROLL):
                    if s % PPG == 0:
                        if s >= LAG:
                            flush(i, (s - LAG) // PPG, first)
                        elif not first:
                            flush(i - 1, (s + UNROLL - LAG) // PPG, False)
                    pool.wait_ge(rec_in[s], 16 * (i + 1) if first else i * 16 + 16)
                    if not first:
                        pool.wait_ge(b_ready, upto(i - 1, UNROLL * TPG, s * TPG + 1))
                        pool.wait_ge(d_ready, upto(i - 1, UNROLL * TPG, s * TPG + 1))
                    pool.sem_inc(indirect_turn, 1)
                    for t in range(TPG):
                        idx = RB[:, s, t, 4 * C + 4:4 * C + 5].bitcast(I32)
                        g.indirect_dma_start(out=GB[:, s, t, :], out_offset=None, in_=tab_dram,
                                             in_offset=bass.IndirectOffsetOnAxis(ap=idx, axis=0))\
                            .then_inc(gathered[s], 16)

            pool.wait_ge(acc_zero, 1)
            gather(0, True)
            with pool.Fori(1, MITER) as i:
                gather(i, False)
            for q in range((UNROLL - LAG) // PPG, GPB):
                flush(MITER - 1, q, True)

            for t in range(NB):
                r, w = rstd[0:NT, t:t + 1], newton[0:NT, t:t + 1]
                pool.wait_ge(std2_ready, t + 1)
                step(g.tensor_tensor(w, r, r, ALU.mult))
                step(g.tensor_tensor(w, w, var_eps[0:NT, t:t + 1], ALU.mult))
                step(g.tensor_scalar(w, w, -0.5, 1.5, ALU.mult, ALU.add))
                g.tensor_tensor(r, r, w, ALU.mult).then_inc(rstd2_ready, 1)
                if t % 2 == 0:
                    pool.wait_ge(rstd2_ready, t + 1)
                    if t >= 2:
                        pool.wait_ge(xfT_psum, t - 1)
                    g.tensor_scalar(XF[0:NT, 0, :], X[0:NT, t, :], aggr[0:NT, t, 0:1], r, ALU.subtract, ALU.mult)\
                        .then_inc(xf_even, 1)

        @block.scalar
        def _(act):
            a = nc.scalar
            act.wait_ge(var_ready, 1)
            a.activation(rstd[0:NT, :], var_eps[0:NT, :], ACT.Sqrt).then_inc(std_ready, 1)
            act.wait_ge(nrm_sq, 1)
            a.activation(inv, ssq, ACT.Sqrt).then_inc(nrm_root, 1)
            a.preload_act_table_set("natural_log_exp_and_others")

            def evac_xT(t):
                act.wait_ge(xT_psum, t + 1)
                if t >= 2:
                    act.wait_ge(v_psum, t - 1)
                a.activation(XT[:, t % 2, :, :].rearrange("p k n -> p (k n)"), PS[:, t % 2, 0:KD * NT], ACT.Copy)\
                    .then_inc(xT_ready, 1)

            evac_xT(0)
            for t in range(NB):
                if t + 1 < NB:
                    evac_xT(t + 1)
                act.wait_ge(tab_psum, t + 1)
                if t >= 2:
                    act.wait_ge(tab_out[t % 2], 16 * (t // 2))
                a.activation(TAB[0:NT, t % 2, :], PS[0:NT, 2, :], ACT.Copy, scale=Y0 / float(np.sqrt(C)))\
                    .then_inc(tab_ready, 1)
                act.wait_ge(q_shift, t + 1)
                a.activation(QW[0:NT, :], QW[0:NT, :], ACT.Exp).then_inc(q_exp, 1)
                act.wait_ge(k_shift, t + 1)
                a.activation(KN[0:NT, t, :], KN[0:NT, t, :], ACT.Exp).then_inc(k_exp, 1)
                act.wait_ge(v_psum, t + 1)
                a.activation(VN[0:NT, t, :], PS[0:NT, 5, :], ACT.Copy).then_inc(v_ready, 1)
                act.wait_ge(qT_psum, t + 1)
                a.activation(QT[:, t, :, :].rearrange("p k n -> p (k n)"), PS[:, 6, 0:KD * NT], ACT.Copy)\
                    .then_inc(qT_ready, 1)
            act.wait_ge(ctx_psum, 1)
            act.wait_ge(ctx_zero, 1)
            for hh in range(2):
                r = slice(hh * DH, (hh + 1) * DH)
                a.activation(ctxT[r, :, hh * DH:(hh + 1) * DH],
                             PS[r, 0, :].rearrange("p (k n) -> p k n", k=KD)[:, :, hh * DH:(hh + 1) * DH], ACT.Copy)\
                    .then_inc(ctx_ready, 1)
            for k in range(KD):
                act.wait_ge(mo_psum, k + 1)
                a.activation(MO[:, k, :], PS[:, 1 + k % 2, :], ACT.Copy).then_inc(mo_ready, 1)

            a.activation(fT[0:32, :, :].rearrange("p h n -> p (h n)"),
                         ones[0:32, 0:1].to_broadcast([32, 2 * 512]), ACT.Copy).then_inc(act_step, 1)
            act.wait_ge(act_step, 1)
            a.activation(wf2_high[:, :, :], wf2[:, :, :], ACT.Copy).then_inc(wf2_h, 1)
            act.wait_ge(b2_psum, 1)
            a.activation(b2_rows, PS[:, 3, :], ACT.Copy).then_inc(b2_ready, 1)

            def radial(i, c):
                m = i * RING + c
                act.wait_ge(f_used, m + 1)
                if real(m - 1):
                    act.wait_ge(z_psum, m - 1)
                a.activation(fT[0:R, c % 2, :], PS[0:R, 0, :], ACT.Copy).then_inc(fT_ready, 1)

            def log_part(i, c):
                m = i * RING + c
                h = c % 2
                act.wait_ge(z_psum, m + 1)
                if real(m - 1):
                    act.wait_ge(h_ready, m - 1)
                a.activation(tz[:, h, :], PS[:, 1 + h, :], ACT.Abs).then_inc(log_stage, 1)
                act.wait_ge(log_stage, m * 3 + 1)
                a.activation(tz[:, h, :], tz[:, h, :], ACT.Exp, scale=-1.0).then_inc(log_stage, 1)
                act.wait_ge(log_stage, m * 3 + 2)
                a.activation(tz[:, h, :], tz[:, h, :], ACT.Ln, bias=half[:, 0:1], scale=0.5).then_inc(log_stage, 1)

            def high(i, c):
                m = i * RING + c
                act.wait_ge(h_ready, m + 1)
                if real((m - 1) * STEP):
                    act.wait_ge(w_psum, (m - 1) * STEP)
                a.activation(h_high[:, c % 2, :], hT[:, c % 2, :], ACT.Copy).then_inc(hh_ready, 1)

            def first_column(i, c):
                m = i * RING + c
                act.wait_ge(w_psum, m * STEP + 1)
                act.wait_ge(staged, m + 1)
                a.activation(ST[:, c * STEP, 0:4 * C], PS[:, 3, :], ACT.Copy).then_inc(w_act, 1)

            def filters(i):
                for c in range(RING):
                    if exists(i, c + 1):
                        high(i, c + 1)
                    first_column(i, c)
                    if exists(i, c + 3):
                        log_part(i, c + 3)
                    if exists(i, c + 4):
                        radial(i, c + 4)

            radial(0, 0)
            radial(0, 1)
            log_part(0, 0)
            radial(0, 2)
            log_part(0, 1)
            radial(0, 3)
            log_part(0, 2)
            act.wait_ge(mix_added, NB)
            act.wait_ge(router_ready, 1)
            high(0, 0)
            filters(0)
            with act.Fori(1, FITER - 1) as i:
                filters(i)
            filters(FITER - 1)

            per = UNROLL * TPG

            def x_terms(i, s, first):
                for t in range(TPG):
                    act.wait_ge(gathered[s], i * (16 * TPG) + 16 * TPG)
                    if s >= 2:
                        act.wait_ge(b_ready, upto(i, per, (s - 2) * TPG + t))
                    elif not first:
                        act.wait_ge(b_ready, upto(i - 1, per, (s + UNROLL - 2) * TPG + t))
                    a.activation(DT[:, s % 2, t, 0, :], GB[:, s, t, C:2 * C], ACT.Copy,
                                 scale=RB[:, s, t, 4 * C:4 * C + 1]).then_inc(dot1, 1)

            def c_messages(i, s):
                for t in range(TPG):
                    act.wait_ge(ac_ready, upto(i, per, s * TPG + t))
                    for k in range(3):
                        last = a.activation(MB[:, s % 2, t, 2 + k, :], MB[:, s % 2, t, 8, :], ACT.Copy,
                                            scale=RB[:, s, t, 4 * C + k:4 * C + k + 1])
                    last.then_inc(c_ready, 1)

            def sums_from_psum(i, q, first):
                act.wait_ge(summed, upto(i, per, (q + 1) * PPG * TPG - 1))
                if q >= 2 or not first:
                    act.wait_ge(flushed, i * GPB + q - 1)
                a.activation(SG[0:NT, q % 2, :], PS[0:NT, 2 * q:2 * q + 2, :].rearrange("p b n -> p (b n)"),
                             ACT.Copy).then_inc(sums_out, 1)

            def scalar_messages(i, first, last):
                for s in range(UNROLL):
                    if s + 1 < UNROLL:
                        x_terms(i, s + 1, first)
                    elif not last:
                        x_terms(i + 1, 0, False)
                    if s % PPG:
                        if s > 1:
                            sums_from_psum(i, s // PPG - 1, first)
                        elif not first:
                            sums_from_psum(i - 1, GPB - 1, False)
                    c_messages(i, s)

            x_terms(0, 0, True)
            scalar_messages(0, True, False)
            with act.Fori(1, MITER - 1) as i:
                scalar_messages(i, False, False)
            scalar_messages(MITER - 1, False, True)
            sums_from_psum(MITER - 1, GPB - 1, False)

            def evac_sums(t):
                act.wait_ge(aT_psum, t + 1)
                if t >= 2:
                    act.wait_ge(sv_psum, t - 1)
                for b in range(2):
                    last = a.activation(AT[:, t % 2, 4 * b:4 * b + 4, 0:NT],
                                        PS[:, 4 * (t % 2) + b, 0:4 * NT].rearrange("p (k n) -> p k n", n=NT), ACT.Copy)
                last.then_inc(aT_ready, 1)

            def ssp_part(t):
                h = t % 2
                act.wait_ge(sv_psum, t + 1)
                if t >= 2:
                    act.wait_ge(g_psum, t - 1)
                a.activation(sz[:, h, 0:NT], PS[:, 4 * h + 2, 0:NT], ACT.Abs).then_inc(s_abs, 1)
                a.activation(S1[:, h, 1:4, 0:NT], PS[:, 4 * h + 2, NT:4 * NT].rearrange("p (k n) -> p k n", n=NT),
                             ACT.Copy).then_inc(v1_ready, 1)
                act.wait_ge(s_abs, 2 * t + 1)
                a.activation(sz[:, h, 0:NT], sz[:, h, 0:NT], ACT.Exp, scale=-1.0).then_inc(s_abs, 1)
                act.wait_ge(s_abs, 2 * t + 2)
                a.activation(sz[:, h, 0:NT], sz[:, h, 0:NT], ACT.Ln, bias=half[:, 0:1], scale=0.5).then_inc(s_ln, 1)

            def split_high(e):
                if e < EARLY:
                    act.wait_ge(we_early_in, 16 * EARLY * KD)
                else:
                    act.wait_ge(we_in[(e - EARLY) % WE_SLOTS], 16 * ((e - EARLY) // WE_SLOTS + 1))
                if e >= 2:
                    act.wait_ge(eo_psum, (e - 1) * NB)
                a.activation(we_high[:, e % 2, :, :], we[:, e % WE_SLOTS, :, :], ACT.Copy).then_inc(we_split_h, 1)

            def inverse_std(t):
                act.wait_ge(var2_ready, t + 1)
                a.activation(rstd[0:NT, t:t + 1], var_eps[0:NT, t:t + 1], ACT.Ln).then_inc(std2_step, 1)
                act.wait_ge(std2_step, t + 1)
                a.activation(rstd[0:NT, t:t + 1], rstd[0:NT, t:t + 1], ACT.Exp, scale=-0.5).then_inc(std2_ready, 1)

            def xT_high_part(t):
                act.wait_ge(xfT_psum, t + 1)
                a.activation(xT_high[:, :, t * NT:(t + 1) * NT],
                             PS[:, xf_bank(t), 0:KD * NT].rearrange("p (k n) -> p k n", k=KD),
                             ACT.Copy).then_inc(xT_h, 1)

            act.wait_ge(summed, NCOL)
            a.activation(gate_high[:, :, :], gate[:, :, :], ACT.Copy).then_inc(gate_h, 1)
            evac_sums(0)
            for t in range(NB + 4):
                if t + 1 < NB:
                    evac_sums(t + 1)
                if t < NB:
                    ssp_part(t)
                if 2 <= t < NB + 2:
                    inverse_std(t - 2)
                if t == 4:
                    split_high(0)
                if t >= 4:
                    xT_high_part(t - 4)
            for q, (t0, n) in enumerate(quads):
                act.wait_ge(logitT_psum, q + 1)
                a.activation(comb_t[0:X8, t0:t0 + n, :], PS[0:X8, 3 + q, 0:n * NT].rearrange("p (t n) -> p t n", t=n),
                             ACT.Copy).then_inc(logitT_ready, 1)
            act.wait_ge(shift_ready, 1)
            a.activation(prob[0:NT], prob[0:NT], ACT.Exp).then_inc(prob_exp, 1)
            split_high(1)
            for q, (t0, n) in enumerate(quads):
                act.wait_ge(combT_psum, q + 1)
                a.activation(comb_t[0:X8, t0:t0 + n, :],
                             PS[0:X8, (0, 1, 3)[q], 0:n * NT].rearrange("p (t n) -> p t n", t=n),
                             ACT.Copy).then_inc(combT_ready, 1)
            for e in range(2, X8):
                split_high(e)

        @block.vector
        def _(dve):
            v = nc.vector
            steps = [0]

            def step(ins):
                steps[0] += 1
                ins.then_inc(dve_step, 1)
                dve.wait_ge(dve_step, steps[0])

            dve.wait_ge(x_in[0], 16)
            for t in range(NB):
                if t == 2:
                    dve.wait_ge(x_in[1], 16)
                last = v.bn_stats(stats[0:NT, t, :], X[0:NT, t, :])
            step(last)
            for t in range(NB):
                last = v.bn_aggr(aggr[0:NT, t, :], stats[0:NT, t, :])
            step(last)
            v.tensor_scalar(var_eps[0:NT, :], aggr[0:NT, :, 1], EPS, None, ALU.add).then_inc(var_ready, 1)
            step(v.memset(half[:, :], 0.5))
            step(v.tensor_copy(mean[0:NT, :], aggr[0:NT, :, 0]))
            dve.wait_ge(std_ready, 1)
            step(v.reciprocal(rstd[0:NT, :], rstd[0:NT, :]))

            def normal(t):
                if t >= 2:
                    dve.wait_ge(xT_psum, t - 1)
                v.tensor_scalar(XN[0:NT, t % 2, :], X[0:NT, t, :], mean[0:NT, t:t + 1], rstd[0:NT, t:t + 1],
                                ALU.subtract, ALU.mult).then_inc(xn_ready, 1)

            normal(0)
            normal(1)
            dve.wait_ge(consts, 2)
            dve.wait_ge(edge_in, 16 * 6)
            step(v.tensor_tensor(rtmp, rraw, rraw, ALU.mult))
            step(v.tensor_tensor(ssq, rtmp[:, :, 0], rtmp[:, :, 1], ALU.add))
            v.tensor_tensor(ssq, ssq, rtmp[:, :, 2], ALU.add).then_inc(nrm_sq, 1)
            step(v.tensor_copy(meta[:, 0:RC1, 4].bitcast(I32), dsti))
            dve.wait_ge(nrm_root, 1)
            step(v.reciprocal(inv, inv))
            step(v.tensor_tensor(meta[:, 0:RC1, 0:3], rraw, inv.unsqueeze(2).to_broadcast([P, RC1, 3]), ALU.mult))
            def filter_weights():
                dve.wait_ge(b2_in, 16)
                dve.wait_ge(wf_in, 48)
                w4 = wf2raw.rearrange("p (g f a) -> p g a f", g=2, a=2)
                r4 = b2raw.rearrange("p (g f a) -> p g a f", g=2, a=2)
                step(v.tensor_copy(wf2[:, :, :].rearrange("p (g a) f -> p g a f", g=2), w4))
                step(v.tensor_copy(b2rem.rearrange("p (g a f) -> p g a f", g=2, a=2), r4))
                step(v.tensor_scalar(wf2[:, 2, :], wf2[:, 2, :], float(np.sqrt(3.0)), None, ALU.mult))
                step(v.tensor_scalar(b2rem[:, 2 * C:3 * C], b2rem[:, 2 * C:3 * C], float(np.sqrt(3.0)), None, ALU.mult))
                for k in range(3):
                    last = v.tensor_copy(b2p[k], b2rem)
                    if k < 2:
                        step(last)
                        step(v.tensor_tensor(b2rem, b2rem, b2p[k], ALU.subtract))
                last.then_inc(b2_parts, 1)

            def receiving_blocks():
                step(v.tensor_copy(srcf, srci))
                step(v.memset(srcf[REM:P, FULL:RC1], 1e6))
                step(v.tensor_scalar(bkt, srcf, float(NT), None, ALU.is_ge))
                for b in range(2, NB + 1):
                    step(v.scalar_tensor_tensor(bkt, srcf, float(b * NT), bkt, ALU.is_ge, ALU.add))
                v.scalar_tensor_tensor(meta[:, 0:RC1, 3], bkt, -float(NT), srcf, ALU.mult, ALU.add)
                step(v.memset(rnk, 0.0))

            def count_block(t):
                step(v.tensor_scalar(tA, bkt, float(t), None, ALU.is_equal))
                step(v.tensor_tensor_scan(tB, ones[:, 0:RC1], tA, 0.0, ALU.mult, ALU.add))
                v.tensor_copy(cnt[:, t:t + 1], tB[:, RC1 - 1:RC1]).then_inc(counts_ready, 1)
                step(v.tensor_tensor(tA, tA, tB, ALU.mult))
                step(v.tensor_tensor(rnk, rnk, tA, ALU.add))

            def shift(bank, dst, mx, psum_ready, t, signal):
                dve.wait_ge(psum_ready, t + 1)
                src3 = PS[0:NT, bank, :].rearrange("p (h d) -> p h d", h=HEADS)
                step(v.reduce_max(mx[0:NT, :], src3, AX_X))
                v.tensor_tensor(dst.rearrange("p (h d) -> p h d", h=HEADS), src3,
                                mx[0:NT, :].unsqueeze(2).to_broadcast([NT, HEADS, DH]), ALU.subtract)\
                    .then_inc(signal, 1)

            def normalise(dst, sm, exp_ready, t, signal):
                dve.wait_ge(exp_ready, t + 1)
                d3 = dst.rearrange("p (h d) -> p h d", h=HEADS)
                step(v.reduce_sum(sm[0:NT, :], d3, AX_X))
                step(v.reciprocal(sm[0:NT, :], sm[0:NT, :]))
                v.tensor_tensor(d3, d3, sm[0:NT, :].unsqueeze(2).to_broadcast([NT, HEADS, DH]), ALU.mult)\
                    .then_inc(signal, 1)

            for t in range(NB):
                if t + 2 < NB:
                    normal(t + 2)
                if t == 3:
                    dve.wait_ge(b2_placed, 48)
                if t:
                    dve.wait_ge(qT_psum, t)
                shift(3, QW[0:NT, :], mxq, q_psum, t, q_shift)
                shift(4, KN[0:NT, t, :], mxk, k_psum, t, k_shift)
                normalise(QW[0:NT, :], smq, q_exp, t, q_norm)
                normalise(KN[0:NT, t, :], smk, k_exp, t, k_norm)
                if t == 0:
                    filter_weights()
                elif t == 1:
                    receiving_blocks()
                    count_block(0)
                    count_block(1)
                else:
                    count_block(t)
            dve.wait_ge(k_psum, NB)
            v.memset(ctxT[:, :, :].rearrange("p k n -> p (k n)"), 0.0).then_inc(ctx_zero, 1)
            dve.wait_ge(counts_psum, 1)
            step(v.tensor_copy(pref, PS[:, 7, 0:NB]))
            v.tensor_copy(tot, PS[:, 7, NB:2 * NB]).then_inc(counts_read, 1)
            dve.wait_ge(counts_read, 1)
            step(v.tensor_scalar(ints[:, 0:NB], tot, float(GROUP - 1), None, ALU.add))
            step(v.tensor_scalar(ints[:, 0:NB], ints[:, 0:NB], GROUP.bit_length() - 1, None, ALU.arith_shift_right))
            step(v.tensor_copy(ngf, ints[:, 0:NB]))
            step(v.tensor_tensor_scan(endg, ones[:, 0:NB], ngf, 0.0, ALU.mult, ALU.add))
            step(v.tensor_tensor_scan(cumt, ones[:, 0:NB], tot, 0.0, ALU.mult, ALU.add))
            step(v.tensor_tensor(base, endg, ngf, ALU.subtract))
            step(v.tensor_scalar(base, base, float(GROUP), None, ALU.mult))
            step(v.scalar_tensor_tensor(off, pref, -1.0, base, ALU.add, ALU.add))
            step(v.tensor_tensor(cpad, base, cumt, ALU.subtract))
            step(v.tensor_tensor(cpad, cpad, tot, ALU.add))
            step(v.tensor_copy(pd, kd))
            for b in range(NB):
                step(v.tensor_scalar(tA, bkt, float(b), off[:, b:b + 1], ALU.is_equal, ALU.mult))
                step(v.tensor_tensor(rnk, rnk, tA, ALU.add))
                step(v.tensor_scalar(tB[:, 0:SPARE], kd, cpad[:, b:b + 1], tot[:, b:b + 1], ALU.is_ge, ALU.mult))
                step(v.tensor_tensor(pd, pd, tB[:, 0:SPARE], ALU.add))
            step(v.tensor_copy(posi[:, 0:RC1], rnk))
            step(v.tensor_copy(posi[:, RC1:NCOL], pd[:, 1:SPARE]))
            v.tensor_copy(posi[REM:P, FULL:RC1], pd[REM:P, 0:1]).then_inc(places_ready, 1)
            dve.wait_ge(mi_psum, 1)
            step(v.tensor_scalar(mi, PS[:, 7, 0:KD], 1.0 / NI, None, ALU.mult))
            step(v.memset(z_mi, 0.0))
            for e in range(X8):
                v.tensor_copy(z_mi[:, :, e, e], mi)
            v.tensor_copy(mi_bc, mi.unsqueeze(2).to_broadcast([P, KD, P])).then_inc(z_ready, 1)
            v.tensor_copy(gamT, PS[:, 7, X8:(KD + 1) * X8].rearrange("p (k e) -> p k e", k=KD)).then_inc(gamT_ready, 1)
            def stage_f(i, c):
                m = i * RING + c
                if real(m - 1):
                    dve.wait_ge(f_used, m - 1)
                v.tensor_copy(Fst[:, c % 2, :, :], Fe[:, columns_of(i, c), :]).then_inc(f_staged, 1)

            def stage(i, c):
                cols = columns_of(i, c)
                if real(i):
                    dve.wait_ge(scattered[c], i * (16 * STEP))
                v.tensor_copy(ST[:, c * STEP:(c + 1) * STEP, 4 * C:REC], meta[:, cols, :])
                v.tensor_copy(idxst[:, c * STEP:(c + 1) * STEP], posi[:, cols]).then_inc(staged, 1)

            def hidden(i, c):
                m = i * RING + c
                h = c % 2
                dve.wait_ge(log_stage, m * 3 + 3)
                if real(m - 1):
                    dve.wait_ge(hh_ready, m - 1)
                    dve.wait_ge(hl_ready, m - 1)
                v.scalar_tensor_tensor(hT[:, h, :], PS[:, 1 + h, :], 0.0, tz[:, h, :], ALU.max, ALU.add)\
                    .then_inc(h_ready, 1)

            def low(i, c):
                m = i * RING + c
                h = c % 2
                dve.wait_ge(hh_ready, m + 1)
                if real((m - 1) * STEP):
                    dve.wait_ge(w_psum, (m - 1) * STEP)
                v.tensor_tensor(h_low[:, h, :], hT[:, h, :], h_high[:, h, :].bitcast(F32), ALU.subtract)\
                    .then_inc(hl_ready, 1)

            def column(i, c, j):
                m = i * RING + c
                dve.wait_ge(w_psum, m * STEP + j + 1)
                v.tensor_tensor(ST[:, c * STEP + j, 0:4 * C], PS[:, 3 + j, :], b2_rows, ALU.add)\
                    .then_inc(w_dve, 1)

            def filters(i):
                for c in range(RING):
                    stage(i, c)
                    if exists(i, c + 2):
                        hidden(i, c + 2)
                    if exists(i, c + 1):
                        low(i, c + 1)
                    column(i, c, 1)
                    column(i, c, 2)
                    if exists(i, c + 5):
                        stage_f(i, c + 5)
                    column(i, c, 3)

            dve.wait_ge(f_in, 32)
            stage_f(0, 0)
            stage_f(0, 1)
            dve.wait_ge(bo_added, 1)
            for t in range(NB):
                dve.wait_ge(y_psum, t + 1)
                v.tensor_tensor(X[0:NT, t, :], X[0:NT, t, :], PS[0:NT, y_banks[t % len(y_banks)], :], ALU.add)\
                    .then_inc(mix_added, 1)
            dve.wait_ge(gam_psum, 1)
            v.tensor_copy(gam8, PS[:, 6, 0:X8])
            v.tensor_copy(rgam, PS[:, 6, 8:8 + X8])
            step(v.tensor_copy(gcol[0:X8, :], PS[0:X8, 6, 16:17]))
            stage_f(0, 2)
            stage_f(0, 3)
            step(v.tensor_copy(tA[:, 0:GROUPS], goff[:, :]))
            step(v.tensor_scalar(tB[:, 0:GROUPS], tA[:, 0:GROUPS], endg[:, 0:1], None, ALU.is_ge))
            for b in range(1, NB - 1):
                step(v.scalar_tensor_tensor(tB[:, 0:GROUPS], tA[:, 0:GROUPS], endg[:, b:b + 1], tB[:, 0:GROUPS],
                                            ALU.is_ge, ALU.add))
            step(v.tensor_scalar(goff[:, :], tB[:, 0:GROUPS], float(MSG), None, ALU.mult))
            dve.wait_ge(w12_in, 16 * 5)
            v.tensor_scalar(w1s[:, :, :], w1s[:, :, :], float(1 / np.sqrt(2 * C)), None, ALU.mult)
            v.tensor_scalar(w1v[:, :, :], w1v[:, :, :], float(1 / np.sqrt(2 * C)), None, ALU.mult)
            v.tensor_scalar(w2s[:, :], w2s[:, :], float(1 / np.sqrt(C)), None, ALU.mult)
            v.tensor_scalar(w2v[:, :], w2v[:, :], float(1 / np.sqrt(C)), None, ALU.mult)
            dve.wait_ge(rcut_in, 32)
            step(v.tensor_copy(meta[:, :, 5], rcut))
            dve.wait_ge(wf2_h, 1)
            v.tensor_tensor(wf2_low[:, :, :], wf2[:, :, :], wf2_high[:, :, :].bitcast(F32), ALU.subtract)\
                .then_inc(wf2_l, 1)
            hidden(0, 0)
            hidden(0, 1)
            stage_f(0, 4)
            dve.wait_ge(beta_used, X8)
            v.scalar_tensor_tensor(bb[0:X8, :], be_row, gcol[0:X8, :], PS[0:X8, 7, :], ALU.mult, ALU.add)\
                .then_inc(router_ready, 1)
            dve.wait_ge(router_ready, 1)

            dve.wait_ge(b2_ready, 1)
            low(0, 0)
            filters(0)
            with dve.Fori(1, FITER - 2) as i:
                filters(i)
            filters(FITER - 2)
            filters(FITER - 1)

            def messages(i, first):
                per = UNROLL * TPG
                for s in range(UNROLL):
                    dve.wait_ge(rec_in[s], i * 16 + 16)
                    w4 = RB[:, s, :, 0:4 * C].rearrange("p t (k n) -> p t k n", k=4)
                    dve.wait_ge(gathered[s], i * (16 * TPG) + 16 * TPG)
                    for t in range(TPG):
                        if s >= 2:
                            dve.wait_ge(summed, upto(i, per, (s - 2) * TPG + t))
                        elif not first:
                            dve.wait_ge(summed, upto(i - 1, per, (s + UNROLL - 2) * TPG + t))
                        v.tensor_tensor(MB[:, s % 2, t, 0:9:8, :], w4[:, t, 0:3:2, :],
                                        GB[:, s, t, 0:C].unsqueeze(1).to_broadcast([P, 2, C]), ALU.mult)\
                            .then_inc(ac_ready, 1)
                    for k in range(2):
                        for t in range(TPG):
                            if k == 0:
                                dve.wait_ge(dot1, upto(i, per, s * TPG + t))
                            else:
                                dve.wait_ge(dot_sum, upto(i, 2 * per, s * 2 * TPG + t))
                            v.scalar_tensor_tensor(DT[:, s % 2, t, k + 1, :], GB[:, s, t, (k + 2) * C:(k + 3) * C],
                                                   RB[:, s, t, 4 * C + k + 1:4 * C + k + 2], DT[:, s % 2, t, k, :],
                                                   ALU.mult, ALU.add).then_inc(dot_sum, 1)
                    v.tensor_tensor(MB[:, s % 2, :, 5:8, :],
                                    GB[:, s, :, C:4 * C].rearrange("p t (k n) -> p t k n", k=3),
                                    w4[:, :, 3:4, :].to_broadcast([P, TPG, 3, C]), ALU.mult).then_inc(d_ready, TPG)
                    for t in range(TPG):
                        if not first:
                            dve.wait_ge(summed, upto(i - 1, per, s * TPG + t))
                        v.tensor_scalar(OH[:, s, t, 0:NT], iota_f[:, 0:NT], RB[:, s, t, 4 * C + 3:4 * C + 4],
                                        RB[:, s, t, 4 * C + 5:4 * C + 6], ALU.is_equal, ALU.mult).then_inc(onehot, 1)
                    dve.wait_ge(dot_sum, upto(i, 2 * per, s * 2 * TPG + 2 * TPG - 1))
                    v.tensor_tensor(MB[:, s % 2, :, 1, :], DT[:, s % 2, :, 2, :], w4[:, :, 1, :], ALU.mult)\
                        .then_inc(b_ready, TPG)

            for c in range(RING):
                dve.wait_ge(scattered[c], 16 * STEP * FITER)
            messages(0, True)
            with dve.Fori(1, MITER) as i:
                messages(i, False)

            def activate(t):
                dve.wait_ge(s_ln, t + 1)
                dve.wait_ge(v1_ready, t + 1)
                v.scalar_tensor_tensor(S1[:, t % 2, 0, 0:NT], PS[:, 4 * (t % 2) + 2, 0:NT], 0.0, sz[:, t % 2, 0:NT],
                                       ALU.max, ALU.add).then_inc(s_ready, 1)

            def add_gnn(t):
                gnn = PS[0:NT, 3, :]
                dve.wait_ge(g_psum, t + 1)
                v.tensor_tensor(X[0:NT, t, 0:C], X[0:NT, t, 0:C], gnn[:, 0:C], ALU.add)
                xi = X[0:NT, t, C:D].rearrange("p (c i) -> p c i", i=3)
                v.tensor_tensor(xi, xi, gnn[:, C:D].rearrange("p (i c) -> p c i", i=3), ALU.add).then_inc(x1_ready, 1)
                dve.wait_ge(x1_ready, t + 1)
                step(v.bn_stats(stats[0:NT, t, :], X[0:NT, t, :]))
                step(v.bn_aggr(aggr[0:NT, t, :], stats[0:NT, t, :]))
                v.tensor_scalar(var_eps[0:NT, t:t + 1], aggr[0:NT, t, 1:2], EPS, None, ALU.add).then_inc(var2_ready, 1)

            def normal2_odd(t):
                dve.wait_ge(rstd2_ready, t + 1)
                if t >= 2:
                    dve.wait_ge(xfT_psum, t - 1)
                v.tensor_scalar(XF[0:NT, 1, :], X[0:NT, t, :], aggr[0:NT, t, 0:1], rstd[0:NT, t:t + 1], ALU.subtract,
                                ALU.mult).then_inc(xf_odd, 1)

            def xT_low_part(t):
                dve.wait_ge(xT_h, t + 1)
                v.tensor_tensor(xT_low[:, :, t * NT:(t + 1) * NT],
                                PS[:, xf_bank(t), 0:KD * NT].rearrange("p (k n) -> p k n", k=KD),
                                xT_high[:, :, t * NT:(t + 1) * NT].bitcast(F32), ALU.subtract).then_inc(xT_l, 1)

            def split_low(e):
                dve.wait_ge(we_split_h, e + 1)
                if e >= 2:
                    dve.wait_ge(eo_psum, (e - 1) * NB)
                v.tensor_tensor(we_low[:, e % 2, :, :], we[:, e % WE_SLOTS, :, :], we_high[:, e % 2, :, :].bitcast(F32),
                                ALU.subtract).then_inc(we_split_l, 1)

            dve.wait_ge(gate_h, 1)
            v.tensor_tensor(gate_low[:, :, :], gate[:, :, :], gate_high[:, :, :].bitcast(F32), ALU.subtract)\
                .then_inc(gate_l, 1)
            activate(0)
            for t in range(NB + 4):
                if t >= 4:
                    xT_low_part(t - 4)
                if t + 1 < NB:
                    activate(t + 1)
                if t < NB:
                    add_gnn(t)
                if 2 <= t < NB + 2 and t % 2:
                    normal2_odd(t - 2)
                if t == 5:
                    split_low(0)
            dve.wait_ge(logit_psum, 1)
            logits = PS[0:NT, 2, 0:NB * X8].rearrange("p (t e) -> p t e", t=NB)
            over_e = st1[0:NT, :].unsqueeze(2).to_broadcast([NT, NB, X8])
            step(v.tensor_tensor(prob[0:NT], logits, rgam[0:NT, :].unsqueeze(1).to_broadcast([NT, NB, X8]), ALU.add))
            step(v.reduce_max(st1[0:NT, :], prob[0:NT], AX_X))
            v.tensor_tensor(prob[0:NT], prob[0:NT], over_e, ALU.subtract).then_inc(shift_ready, 1)
            dve.wait_ge(prob_exp, 1)
            step(v.reduce_sum(st1[0:NT, :], prob[0:NT], AX_X))
            step(v.reciprocal(st1[0:NT, :], st1[0:NT, :]))
            step(v.tensor_tensor(prob[0:NT], prob[0:NT], over_e, ALU.mult))
            mine = prob[0:NT].unsqueeze(3).to_broadcast([NT, NB, X8, X8])
            others = prob[0:NT].unsqueeze(2).to_broadcast([NT, NB, X8, X8])
            step(v.tensor_tensor(cmp_a[0:NT], others, mine, ALU.is_gt))
            step(v.tensor_tensor(cmp_b[0:NT], others, mine, ALU.is_equal))
            step(v.tensor_tensor(cmp_b[0:NT], cmp_b[0:NT],
                                 tie[0:NT].unsqueeze(1).to_broadcast([NT, NB, X8, X8]), ALU.mult))
            step(v.tensor_tensor(cmp_a[0:NT], cmp_a[0:NT], cmp_b[0:NT], ALU.add))
            step(v.reduce_sum(rank[0:NT], cmp_a[0:NT], AX_X))
            v.scalar_tensor_tensor(comb[0:NT], rank[0:NT], 2.0, prob[0:NT], ALU.is_lt, ALU.mult)\
                .then_inc(comb_ready, 1)
            dve.wait_ge(comb_ready, 1)
            step(v.tensor_tensor(cg[0:NT], comb[0:NT], gam8[0:NT, :].unsqueeze(1).to_broadcast([NT, NB, X8]),
                                 ALU.mult))
            split_low(1)
            for e in range(X8):
                for t in range(NB):
                    n = e * NB + t
                    dve.wait_ge(eo_psum, n + 1)
                    if e == 2:
                        dve.wait_ge(bias_added, t + 1)
                    elif e:
                        dve.wait_ge(eo_used, n - NB + 1)
                    last = v.scalar_tensor_tensor(X[0:NT, t, :], PS[0:NT, 4 + n % 4, :], cg[0:NT, t, e:e + 1],
                                                  X[0:NT, t, :], ALU.mult, ALU.add)
                    last.then_inc(eo_used, 1)
                    if e == 1:
                        dve.wait_ge(bias_psum, t + 1)
                        dve.wait_ge(eo_used, n + 1)
                        v.tensor_tensor(X[0:NT, t, :], X[0:NT, t, :], PS[0:NT, t % 2, :], ALU.add)\
                            .then_inc(bias_added, 1)
                    if t == 2 and 1 <= e < X8 - 1:
                        split_low(e + 1)

        @block.tensor
        def _(pe):
            te = nc.tensor
            idn = ident[0:NT, 0:NT]
            pe.wait_ge(consts, 1)

            def transpose_x(t):
                pe.wait_ge(xn_ready, t + 1)
                if t >= 2:
                    pe.wait_ge(xT_ready, t - 1)
                for k in range(KD):
                    src_ap = XN[0:NT, t % 2, 0:C] if k == 0 else XN[0:NT, t % 2, C + k - 1:D:3]
                    last = te.transpose(PS[:, t % 2, k * NT:(k + 1) * NT], src_ap, idn)
                last.then_inc(xT_psum, 1)

            transpose_x(0)
            for t in range(NB):
                if t + 1 < NB:
                    transpose_x(t + 1)
                pe.wait_ge(xT_ready, t + 1)
                if t == 0:
                    pe.wait_ge(wsv_in, 32)
                else:
                    pe.wait_ge(tab_ready, t)
                for k in range(KD):
                    last = te.matmul(PS[0:NT, 2, k * C:(k + 1) * C], XT[:, t % 2, k, :], wsv[:, min(k, 1), :],
                                     start=True, stop=True)
                last.then_inc(tab_psum, 1)
                for w, (ready, free) in enumerate(((q_psum, q_shift), (k_psum, k_shift), (v_psum, v_ready))):
                    if t == 0:
                        pe.wait_ge(wqkv_in[w], 32)
                    else:
                        pe.wait_ge(free, t)
                    for k in range(KD):
                        last = te.matmul(PS[0:NT, 3 + w, :], XT[:, t % 2, k, :], wqkv[:, w, k, :],
                                         start=(k == 0), stop=(k == KD - 1))
                    last.then_inc(ready, 1)
                pe.wait_ge(q_norm, t + 1)
                if t:
                    pe.wait_ge(qT_ready, t)
                for k in range(KD):
                    last = te.transpose(PS[:, 6, k * NT:(k + 1) * NT], QW[0:NT, k * P:(k + 1) * P], idn)
                last.then_inc(qT_psum, 1)
            pe.wait_ge(k_norm, NB)
            pe.wait_ge(v_ready, NB)
            for k in range(KD):
                for t in range(NB):
                    last = te.matmul(PS[:, 0, k * P:(k + 1) * P], VN[0:NT, t, k * P:(k + 1) * P],
                                     KN[0:NT, t, k * P:(k + 1) * P], start=(t == 0), stop=(t == NB - 1))
            last.then_inc(ctx_psum, 1)
            pe.wait_ge(counts_ready, NB)
            te.matmul(PS[:, 7, 0:NB], ltri[:, :], cnt, start=True, stop=True)
            te.matmul(PS[:, 7, NB:2 * NB], ones[:, 0:P], cnt, start=True, stop=True).then_inc(counts_psum, 1)
            pe.wait_ge(wo_in, 16)
            pe.wait_ge(ctx_ready, 2)
            for k in range(KD):
                if k >= 2:
                    pe.wait_ge(mo_ready, k - 1)
                elif k == 1:
                    pe.wait_ge(tab_ready, NB)
                te.matmul(PS[:, 1 + k % 2, :], ctxT[:, k, :], wo[:, k, :], start=True, stop=True).then_inc(mo_psum, 1)
            for t in range(NB):
                pe.wait_ge(mo_ready, KD)
                pe.wait_ge(qT_ready, t + 1)
                if t >= len(y_banks):
                    pe.wait_ge(mix_added, t - len(y_banks) + 1)
                for k in range(KD):
                    last = te.matmul(PS[0:NT, y_banks[t % len(y_banks)], :], QT[:, t, k, :], MO[:, k, :],
                                     start=(k == 0), stop=(k == KD - 1))
                last.then_inc(y_psum, 1)
                if t == 2:
                    pe.wait_ge(ffn_small_in, 64)
                    pe.wait_ge(counts_read, 1)
                    for k in range(KD):
                        te.matmul(PS[:, 7, k:k + 1], ins_sb[:, k * P:(k + 1) * P], ones[0:NI, 0:1], start=True,
                                  stop=True)
                    for k in range(KD):
                        last = te.transpose(PS[:, 7, (k + 1) * X8:(k + 2) * X8], gam_row[:, k * P:(k + 1) * P],
                                            ident[0:X8, 0:X8])
                    last.then_inc(mi_psum, 1)
            pe.wait_ge(mix_added, NB)
            pe.wait_ge(z_ready, 1)
            pe.wait_ge(gamT_ready, 1)
            for lo, m, w in ((0, mi_bc, gamT), (8, mi_bc, rmod)):
                for k in range(KD):
                    te.matmul(PS[:, 6, lo:lo + X8], m[:, k, :], w[:, k, :], start=(k == 0), stop=(k == KD - 1))
            for k in range(KD):
                last = te.matmul(PS[0:X8, 6, 16:17], gamT[:, k, :], mi[:, k:k + 1], start=(k == 0), stop=(k == KD - 1))
            last.then_inc(gam_psum, 1)
            def transposes(i, c):
                m = i * RING + c
                pe.wait_ge(f_staged, m + 1)
                if real(m):
                    pe.wait_ge(fT_ready, m)
                for j in range(STEP):
                    last = te.transpose(PS[0:R, 0, j * P:(j + 1) * P], Fst[:, c % 2, j, :], ident[:, :])
                last.then_inc(f_used, 1)

            def layer1(i, c):
                m = i * RING + c
                pe.wait_ge(fT_ready, m + 1)
                if real(m - 1):
                    pe.wait_ge(h_ready, m - 1)
                te.matmul(PS[:, 1 + c % 2, :], wf1[:, :], fT[0:R + 1, c % 2, :], start=True, stop=True)\
                    .then_inc(z_psum, 1)

            pe.wait_ge(b2_placed, 48)
            b2_parts3 = b2s[:, :, :].rearrange("p k n -> p (k n)")
            te.matmul(PS[:, 3, :], ones3[:, :], b2_parts3, start=True, stop=True).then_inc(b2_psum, 1)
            pe.wait_ge(act_step, 1)
            transposes(0, 0)
            transposes(0, 1)
            for e in range(X8):
                if e == 1:
                    layer1(0, 0)
                    transposes(0, 2)
                elif e == 2:
                    layer1(0, 1)
                    transposes(0, 3)
                elif e == 4:
                    layer1(0, 2)
                pe.wait_ge(beta_in[e % 4], 16 * (e // 4 + 1))
                for k in range(KD):
                    last = te.matmul(PS[0:X8, 7, :], z_mi[:, k, e, :], bslot[e % 4][:, k, :],
                                     start=(e == 0 and k == 0), stop=(e == X8 - 1 and k == KD - 1))
                last.then_inc(beta_used, 1)

            pe.wait_ge(router_ready, 1)
            pe.wait_ge(b2_ready, 1)
            pe.wait_ge(wf2_l, 1)

            def layer2(i, c, j):
                m = i * RING + c
                if j == 0:
                    pe.wait_ge(hl_ready, m + 1)
                if real(m) and j == 0:
                    pe.wait_ge(w_act, m)
                elif real(m):
                    pe.wait_ge(w_dve, (m - 1) * (STEP - 1) + j)
                edges = slice(j * P, (j + 1) * P)
                if j == 0:
                    te.matmul(PS[:, 3, :], ones3[:, :], b2_parts3, start=True, stop=False)
                for part, weights in ((h_high, wf2_high), (h_high, wf2_low), (h_low, wf2_high)):
                    last = te.matmul(PS[:, 3 + j, :], part[:, c % 2, edges],
                                     weights[:, :, :].rearrange("p k n -> p (k n)"),
                                     start=(j > 0 and weights is wf2_high and part is h_high), stop=part is h_low)
                last.then_inc(w_psum, 1)

            def filters(i):
                for c in range(RING):
                    layer2(i, c, 0)
                    if exists(i, c + 3):
                        layer1(i, c + 3)
                    layer2(i, c, 1)
                    if exists(i, c + 4):
                        transposes(i, c + 4)
                    layer2(i, c, 2)
                    layer2(i, c, 3)

            filters(0)
            with pe.Fori(1, FITER - 1) as i:
                filters(i)
            filters(FITER - 1)
            pe.wait_ge(h_ready, STEPS)
            pe.wait_ge(fT_ready, STEPS)
            pe.wait_ge(w_act, STEPS)
            pe.wait_ge(w_dve, STEPS * (STEP - 1))

            def sums(i, first):
                per = UNROLL * TPG
                for s in range(UNROLL):
                    bank = 2 * (s // PPG)
                    if s % PPG == 0 and not first:
                        pe.wait_ge(sums_out, upto(i - 1, GPB, s // PPG))
                    for t in range(TPG):
                        n = s * TPG + t
                        pe.wait_ge(onehot, upto(i, per, n))
                        pe.wait_ge(c_ready, upto(i, per, n))
                        pe.wait_ge(d_ready, upto(i, per, n))
                        pe.wait_ge(b_ready, upto(i, per, n))
                        for part in range(2):
                            last = te.matmul(PS[0:NT, bank + part, :], OH[:, s, t, 0:NT],
                                             MB[:, s % 2, t, 4 * part:4 * part + 4, :].rearrange("p k n -> p (k n)"),
                                             start=(s % PPG == 0 and t == 0),
                                             stop=(s % PPG == PPG - 1 and t == TPG - 1))
                        last.then_inc(summed, 1)

            sums(0, True)
            with pe.Fori(1, MITER) as i:
                sums(i, False)

            def transpose_sums(t):
                if t >= 2:
                    pe.wait_ge(aT_ready, t - 1)
                for k in range(8):
                    last = te.transpose(PS[:, 4 * (t % 2) + k // 4, (k % 4) * NT:(k % 4 + 1) * NT],
                                        acc[0:NT, t * MSG + k * C:t * MSG + (k + 1) * C], idn)
                last.then_inc(aT_psum, 1)

            def first_mixing(t):
                h, bank = t % 2, 4 * (t % 2) + 2
                pe.wait_ge(aT_ready, t + 1)
                if t >= 2:
                    pe.wait_ge(s_ready, t - 1)
                    pe.wait_ge(v1_ready, t - 1)
                for k in range(2):
                    te.matmul(PS[:, bank, 0:NT], w1s[:, k, :], AT[:, h, k, 0:NT], start=(k == 0), stop=(k == 1))
                for k in range(2):
                    last = te.matmul(PS[:, bank, NT:4 * NT].rearrange("p (k n) -> p k n", n=NT), w1v[:, k, :],
                                     AT[:, h, 2 + 3 * k:5 + 3 * k, 0:NT], start=(k == 0), stop=(k == 1))
                last.then_inc(sv_psum, 1)

            def second_mixing(t):
                h = t % 2
                pe.wait_ge(s_ready, t + 1)
                pe.wait_ge(v1_ready, t + 1)
                if t:
                    pe.wait_ge(x1_ready, t)
                for k in range(4):
                    last = te.matmul(PS[0:NT, 3, k * C:(k + 1) * C], S1[:, h, k, 0:NT],
                                     w2v[:, :] if k else w2s[:, :], start=True, stop=True)
                last.then_inc(g_psum, 1)

            def transpose_xf(t):
                pe.wait_ge(xf_odd if t % 2 else xf_even, t // 2 + 1)
                if t:
                    pe.wait_ge(xT_l, t if t <= XF_SPREAD else XF_SPREAD)
                if t >= XF_SPREAD:
                    pe.wait_ge(aT_ready, NB)
                for k in range(KD):
                    last = te.transpose(PS[:, xf_bank(t), k * NT:(k + 1) * NT], XF[0:NT, t % 2, k * P:(k + 1) * P], idn)
                last.then_inc(xfT_psum, 1)

            pe.wait_ge(flushed, GROUPS)
            transpose_sums(0)
            transpose_sums(1)
            first_mixing(0)
            for t in range(NB + 3):
                if t + 2 < NB:
                    transpose_sums(t + 2)
                if t + 1 < NB:
                    first_mixing(t + 1)
                if t < NB:
                    second_mixing(t)
                if t >= 3:
                    transpose_xf(t - 3)
            def split_product(psum, xs, ws):
                (xh, xl), (wh, wl) = xs, ws
                terms = [(m, w, k) for k in range(KD) for m, w in ((xh, wh), (xh, wl), (xl, wh))]
                for n, (m, w, k) in enumerate(terms):
                    last = te.matmul(psum, m[:, k, :], w[:, k, :], start=(n == 0), stop=(n == len(terms) - 1))
                return last

            pe.wait_ge(gate_l, 1)
            for q in range(len(quads)):
                t0, n = quads[q]
                pe.wait_ge(xT_l, t0 + n)
                terms = [(m, w, k) for k in range(KD)
                         for m, w in ((xT_high, gate_high), (xT_low, gate_high), (xT_high, gate_low))]
                for j, (m, w, k) in enumerate(terms):
                    last = te.matmul(PS[0:X8, 3 + q, 0:n * NT], w[:, k, :], m[:, k, t0 * NT:(t0 + n) * NT],
                                     start=(j == 0), stop=(j == len(terms) - 1))
                last.then_inc(logitT_psum, 1)
            for q, (t0, n) in enumerate(quads):
                pe.wait_ge(logitT_ready, q + 1)
                for t in range(t0, t0 + n):
                    last = te.transpose(PS[0:NT, 2, t * X8:(t + 1) * X8], comb_t[0:X8, t, :], ident[0:X8, 0:X8])
            last.then_inc(logit_psum, 1)
            for e in range(X8):
                pe.wait_ge(we_split_l, e + 1)
                for t in range(NB):
                    n = e * NB + t
                    if n == 4:
                        pe.wait_ge(comb_ready, 1)
                        for u in range(NB):
                            last = te.transpose(PS[0:X8, (0, 1, 3)[u // 4], (u % 4) * NT:(u % 4 + 1) * NT],
                                                comb[0:NT, u, :], idn)
                            if u % 4 == 3 or u == NB - 1:
                                last.then_inc(combT_psum, 1)
                    if n >= 4:
                        pe.wait_ge(eo_used, n - 3)
                    split_product(PS[0:NT, 4 + n % 4, :], [x[:, :, t * NT:(t + 1) * NT] for x in (xT_high, xT_low)],
                                  (we_high[:, e % 2], we_low[:, e % 2])).then_inc(eo_psum, 1)
                    if e == 1:
                        if t == 0:
                            pe.wait_ge(combT_ready, 3)
                        elif t >= 2:
                            pe.wait_ge(bias_added, t - 1)
                        te.matmul(PS[0:NT, t % 2, :], comb_t[0:X8, t, :], bb[0:X8, :], start=True, stop=True)\
                            .then_inc(bias_psum, 1)


_INS = ["x", "src", "dst", "edge_attr_20", "edge_attr_3", "edge_weight", "L0_gnn_W_in2f_s", "L0_gnn_W_in2f_v",
        "L0_gnn_Wf1", "L0_gnn_bf1", "L0_gnn_Wf2", "L0_gnn_bf2", "L0_gnn_W1_s", "L0_gnn_W1_v", "L0_gnn_W2_s",
        "L0_gnn_W2_v", "L0_mix_Wq", "L0_mix_Wk", "L0_mix_Wv", "L0_mix_Wo", "L0_mix_bo", "L0_ffn_Ins_tk",
        "L0_ffn_gate_w", "L0_ffn_expert_w", "L0_ffn_expert_b", "L0_ffn_gamma_w", "L0_ffn_beta_w", "L0_ffn_rmod_w"]


def kernel(**inputs):
    import concourse.bacc as bacc
    from concourse.bass_utils import run_bass_kernel_spmd

    nc = bacc.Bacc("TRN2", target_bir_lowering=False, num_devices=1)
    arrays, args = {}, []
    for name in _INS:
        a = np.ascontiguousarray(inputs[name])
        arrays[f"in_{name}"] = a
        args.append(nc.dram_tensor(f"in_{name}", a.shape, mybir.dt.from_np(a.dtype), kind="ExternalInput").ap())
    shape = tuple(np.shape(inputs["x"]))
    args.append(nc.dram_tensor("out_0", shape, F32, kind="ExternalOutput").ap())
    gps_layer(nc, *args)
    return run_bass_kernel_spmd(nc, [arrays], core_ids=[0]).results[0]["out_0"]
```
